# Optimizing a Trainium2 kernel written in Bass

```python
import numpy as np
import jax
import jax.numpy as jnp

def _softmax(x, axis=-1):
    return jax.nn.softmax(x, axis=axis)

def _gelu(x):
    return jax.nn.gelu(x, approximate=True)

def _silu(x):
    return jax.nn.silu(x)

def _sigmoid(x):
    return jax.nn.sigmoid(x)

def _layernorm(x, axis=-1, eps=1e-05):
    m = jnp.mean(x, axis=axis, keepdims=True)
    v = jnp.var(x, axis=axis, keepdims=True)
    return (x - m) / jnp.sqrt(v + eps)

def _scatter_add(tgt, idx, src, axis=0):
    return tgt.at[idx].add(src)

def _segment_sum(src, seg, n):
    return jax.ops.segment_sum(src, seg, n)
kernel_name = 'mk_early_fusion_embed_d2_tok_img512_r4_c29094'

def setup_inputs(seed: int=0):
    np.random.seed(seed)
    _w = jnp.asarray

    def _rec_inputs():
        import jax
        import jax.numpy as jnp
        _rk = jax.random.key(seed)
        x = 7.57192e-06 + 1.00007 * jax.random.normal(jax.random.fold_in(_rk, 1), (32, 3, 224, 224), jnp.float32)
        x_txt = jax.random.randint(jax.random.fold_in(_rk, 51), (32, 77), 0, 31999, jnp.int32)
        return (x, x_txt)
    x, x_txt = _rec_inputs()

    def _L0_tok_setup():
        import jax, jax.numpy as jnp
        import numpy as np
        DEPTH = 4
        HEADS = 8
        DIM = 128
        HID = 256
        P = 16
        IMG = 224
        GRID = IMG // P
        NPATCH = GRID * GRID
        NTOK = NPATCH + 1
        BATCH = 64
        EPS = 1e-05

        def layernorm(x, w, b):
            mu = jnp.mean(x, axis=-1, keepdims=True)
            var = jnp.mean(jnp.square(x - mu), axis=-1, keepdims=True)
            return (x - mu) * jax.lax.rsqrt(var + EPS) * w + b
        key = jax.random.key(seed)
        ks = jax.random.split(key, 12)
        s = 0.02
        inp = {'x': jax.random.normal(ks[0], (BATCH, 3, IMG, IMG), jnp.float32), 'conv_w': jax.random.normal(ks[1], (3 * P * P, DIM), jnp.float32) * s, 'conv_b': jnp.zeros((DIM,), jnp.float32), 'cls_token': jax.random.normal(ks[2], (1, 1, DIM), jnp.float32) * s, 'pos_embed': jax.random.normal(ks[3], (1, NTOK, DIM), jnp.float32) * s, 'ln1_w': jnp.ones((DEPTH, DIM), jnp.float32), 'ln1_b': jnp.zeros((DEPTH, DIM), jnp.float32), 'qkv_w': jax.random.normal(ks[4], (DEPTH, DIM, 3 * DIM), jnp.float32) * s, 'qkv_b': jnp.zeros((DEPTH, 3 * DIM), jnp.float32), 'proj_w': jax.random.normal(ks[5], (DEPTH, DIM, DIM), jnp.float32) * s, 'proj_b': jnp.zeros((DEPTH, DIM), jnp.float32), 'ln2_w': jnp.ones((DEPTH, DIM), jnp.float32), 'ln2_b': jnp.zeros((DEPTH, DIM), jnp.float32), 'fc1_w': jax.random.normal(ks[6], (DEPTH, DIM, HID), jnp.float32) * s, 'fc1_b': jnp.zeros((DEPTH, HID), jnp.float32), 'fc2_w': jax.random.normal(ks[7], (DEPTH, HID, DIM), jnp.float32) * s, 'fc2_b': jnp.zeros((DEPTH, DIM), jnp.float32), 'norm_w': jnp.ones((DIM,), jnp.float32), 'norm_b': jnp.zeros((DIM,), jnp.float32)}
        return inp
    _L0_tok_all = _L0_tok_setup()
    _L0_tok_in = {k: v for k, v in _L0_tok_all.items() if k in ('conv_w', 'conv_b', 'cls_token', 'pos_embed', 'ln1_w', 'ln1_b', 'qkv_w', 'qkv_b', 'proj_w', 'proj_b', 'ln2_w', 'ln2_b', 'fc1_w', 'fc1_b', 'fc2_w', 'fc2_b', 'norm_w', 'norm_b')}
    del _L0_tok_all

    def _L0_txt_setup():
        import jax, jax.numpy as jnp
        import numpy as np
        import math
        VOCAB = 8000
        SEMEME_SIZE = 512
        D_MODEL = 128
        B, S = (8, 512)
        SPARSITY = 0.005
        key = jax.random.key(seed)
        k1, k2, k3 = jax.random.split(key, 3)
        x = jax.random.randint(k1, (B, S), 0, VOCAB, dtype=jnp.int64)
        word2sememe = (jax.random.uniform(k2, (VOCAB, SEMEME_SIZE)) < SPARSITY).astype(jnp.float32)
        W = jax.random.normal(k3, (SEMEME_SIZE, D_MODEL), dtype=jnp.float32)
        return {'x': x, 'word2sememe': word2sememe, 'W': W}
    _L0_txt_all = _L0_txt_setup()
    _L0_txt_in = {k: v for k, v in _L0_txt_all.items() if k in ('word2sememe', 'W')}
    del _L0_txt_all

    def _L0_attn_setup():
        import jax, jax.numpy as jnp
        import numpy as np
        from math import sqrt
        key = jax.random.key(seed)
        k1, k2, k3, k4 = jax.random.split(key, 4)
        bs, N, D, H = (2, 1024, 128, 8)
        z = jax.random.normal(k1, (bs, N, D), dtype=jnp.float32)
        w_qkv = jax.random.normal(k2, (3 * D, D), dtype=jnp.float32) * (1.0 / sqrt(D))
        w_agg = jax.random.normal(k3, (D, D), dtype=jnp.float32) * (1.0 / sqrt(D))
        b_agg = jax.random.normal(k4, (D,), dtype=jnp.float32) * 0.01
        return {'z': z, 'w_qkv': w_qkv, 'w_agg': w_agg, 'b_agg': b_agg}
    _L0_attn_all = _L0_attn_setup()
    _L0_attn_in = {k: v for k, v in _L0_attn_all.items() if k in ('w_qkv', 'w_agg', 'b_agg')}
    del _L0_attn_all

    def _L0_ffn_setup():
        import jax, jax.numpy as jnp
        import numpy as np
        B, S, D = (4, 256, 128)
        E = 16
        DH = 4 * D
        DS = 2 * D
        TOP_K = 2
        TEMP = 0.7
        SHARED_SCALE = 0.25
        EPS = 1e-05

        def layer_norm(x, g, b):
            mu = jnp.mean(x, axis=-1, keepdims=True)
            var = jnp.mean(jnp.square(x - mu), axis=-1, keepdims=True)
            return (x - mu) * jax.lax.rsqrt(var + EPS) * g + b
        key = jax.random.key(seed)
        ks = jax.random.split(key, 12)
        s = 0.02
        return {'x': jax.random.normal(ks[0], (B, S, D), jnp.float32), 'ln_in_g': jnp.ones((D,), jnp.float32), 'ln_in_b': jnp.zeros((D,), jnp.float32), 'router_w': jax.random.normal(ks[1], (D, E), jnp.float32) * s, 'router_b': jnp.zeros((E,), jnp.float32), 'ew1': jax.random.normal(ks[2], (E, D, DH), jnp.float32) * s, 'eb1': jnp.zeros((E, DH), jnp.float32), 'ew2': jax.random.normal(ks[3], (E, DH, D), jnp.float32) * s, 'eb2': jnp.zeros((E, D), jnp.float32), 'sw1': jax.random.normal(ks[4], (D, DS), jnp.float32) * s, 'sb1': jnp.zeros((DS,), jnp.float32), 'sw2': jax.random.normal(ks[5], (DS, D), jnp.float32) * s, 'sb2': jnp.zeros((D,), jnp.float32), 'ff_ln_g': jnp.ones((D,), jnp.float32), 'ff_ln_b': jnp.zeros((D,), jnp.float32), 'ff_w1': jax.random.normal(ks[6], (D, DH), jnp.float32) * s, 'ff_b1': jnp.zeros((DH,), jnp.float32), 'ff_w2': jax.random.normal(ks[7], (DH, D), jnp.float32) * s, 'ff_b2': jnp.zeros((D,), jnp.float32)}
    _L0_ffn_all = _L0_ffn_setup()
    _L0_ffn_in = {k: v for k, v in _L0_ffn_all.items() if k in ('ln_in_g', 'ln_in_b', 'router_w', 'router_b', 'ew1', 'eb1', 'ew2', 'eb2', 'sw1', 'sb1', 'sw2', 'sb2', 'ff_ln_g', 'ff_ln_b', 'ff_w1', 'ff_b1', 'ff_w2', 'ff_b2')}
    del _L0_ffn_all

    def _L1_attn_setup():
        import jax, jax.numpy as jnp
        import numpy as np
        import math
        _DENSE_LOCAL_W = 32
        _DYADIC = [48, 64, 96, 128, 192, 64, 96, 128, 192, 256, 384, 512, 768, 1024]
        OFFSETS = np.array(sorted(set(range(0, _DENSE_LOCAL_W + 1)) | set(_DYADIC)), dtype=np.int32)
        NUM_OFFSETS = len(OFFSETS)
        H = 8
        _LOG_MAX = math.log(1.0 + 4096.0)
        _HEAD_OMEGAS = [0.0, 0.0, 1 * math.pi / _LOG_MAX, 1 * math.pi / _LOG_MAX, 4 * math.pi / _LOG_MAX, 4 * math.pi / _LOG_MAX, 6 * math.pi / _LOG_MAX, 6 * math.pi / _LOG_MAX]
        _log_d = np.log(1.0 + OFFSETS.astype(np.float64))
        _CK = np.zeros((NUM_OFFSETS, H), dtype=np.float32)
        for _h, _om in enumerate(_HEAD_OMEGAS):
            if _om > 0.0:
                _CK[:, _h] = np.cos(_om * _log_d)
        DISP_COS_KERNEL = jnp.asarray(_CK)
        B, N, D = (1, 512, 128)
        HD = D // H
        key = jax.random.key(seed)
        ks = jax.random.split(key, 8)
        s = 0.02
        return {'x': jax.random.normal(ks[0], (B, N, D), jnp.float32), 'W_qkv': jax.random.normal(ks[1], (D, 3 * D), jnp.float32) * s, 'b_qkv': jax.random.normal(ks[2], (3 * D,), jnp.float32) * s, 'W_out': jax.random.normal(ks[3], (D, D), jnp.float32) * s, 'b_out': jax.random.normal(ks[4], (D,), jnp.float32) * s, 'W_gate': jax.random.normal(ks[5], (D, D), jnp.float32) * s, 'b_gate': jnp.zeros((D,), jnp.float32), 'pos_bias': jnp.zeros((NUM_OFFSETS, H), jnp.float32) + 0.001, 'scale_embed': jnp.zeros((NUM_OFFSETS, HD), jnp.float32), 'if_gain': jnp.ones((H,), jnp.float32), 'disp_amp': jnp.full((H,), 0.1, jnp.float32)}
    _L1_attn_all = _L1_attn_setup()
    _L1_attn_in = {k: v for k, v in _L1_attn_all.items() if k in ('W_qkv', 'b_qkv', 'W_out', 'b_out', 'W_gate', 'b_gate', 'pos_bias', 'scale_embed', 'if_gain', 'disp_amp')}
    del _L1_attn_all

    def _L1_ffn_setup():
        import jax, jax.numpy as jnp
        import numpy as np
        B, S, D, H, O, E, TOPK = (4, 512, 128, 256, 128, 8, 2)
        key = jax.random.key(seed)
        ks = jax.random.split(key, 6)
        s = lambda d: 1.0 / np.sqrt(d)
        return {'x': jax.random.normal(ks[0], (B, S, D), dtype=jnp.float32), 'Wg': jax.random.normal(ks[1], (D, E), dtype=jnp.float32) * s(D), 'W1': jax.random.normal(ks[2], (E, D, H), dtype=jnp.float32) * s(D), 'b1': jnp.zeros((E, H), dtype=jnp.float32), 'W2': jax.random.normal(ks[3], (E, H, O), dtype=jnp.float32) * s(H), 'b2': jnp.zeros((E, O), dtype=jnp.float32)}
    _L1_ffn_all = _L1_ffn_setup()
    _L1_ffn_in = {k: v for k, v in _L1_ffn_all.items() if k in ('Wg', 'W1', 'b1', 'W2', 'b2')}
    del _L1_ffn_all
    return {'x': x, 'x_txt': x_txt, 'L0_tok_conv_w': _L0_tok_in['conv_w'], 'L0_tok_conv_b': _L0_tok_in['conv_b'], 'L0_tok_cls_token': _L0_tok_in['cls_token'], 'L0_tok_pos_embed': _L0_tok_in['pos_embed'], 'L0_tok_ln1_w': _L0_tok_in['ln1_w'], 'L0_tok_ln1_b': _L0_tok_in['ln1_b'], 'L0_tok_qkv_w': _L0_tok_in['qkv_w'], 'L0_tok_qkv_b': _L0_tok_in['qkv_b'], 'L0_tok_proj_w': _L0_tok_in['proj_w'], 'L0_tok_proj_b': _L0_tok_in['proj_b'], 'L0_tok_ln2_w': _L0_tok_in['ln2_w'], 'L0_tok_ln2_b': _L0_tok_in['ln2_b'], 'L0_tok_fc1_w': _L0_tok_in['fc1_w'], 'L0_tok_fc1_b': _L0_tok_in['fc1_b'], 'L0_tok_fc2_w': _L0_tok_in['fc2_w'], 'L0_tok_fc2_b': _L0_tok_in['fc2_b'], 'L0_tok_norm_w': _L0_tok_in['norm_w'], 'L0_tok_norm_b': _L0_tok_in['norm_b'], 'L0_txt_word2sememe': _L0_txt_in['word2sememe'], 'L0_txt_W': _L0_txt_in['W'], 'L0_attn_w_qkv': _L0_attn_in['w_qkv'], 'L0_attn_w_agg': _L0_attn_in['w_agg'], 'L0_attn_b_agg': _L0_attn_in['b_agg'], 'L0_ffn_ln_in_g': _L0_ffn_in['ln_in_g'], 'L0_ffn_ln_in_b': _L0_ffn_in['ln_in_b'], 'L0_ffn_router_w': _L0_ffn_in['router_w'], 'L0_ffn_router_b': _L0_ffn_in['router_b'], 'L0_ffn_ew1': _L0_ffn_in['ew1'], 'L0_ffn_eb1': _L0_ffn_in['eb1'], 'L0_ffn_ew2': _L0_ffn_in['ew2'], 'L0_ffn_eb2': _L0_ffn_in['eb2'], 'L0_ffn_sw1': _L0_ffn_in['sw1'], 'L0_ffn_sb1': _L0_ffn_in['sb1'], 'L0_ffn_sw2': _L0_ffn_in['sw2'], 'L0_ffn_sb2': _L0_ffn_in['sb2'], 'L0_ffn_ff_ln_g': _L0_ffn_in['ff_ln_g'], 'L0_ffn_ff_ln_b': _L0_ffn_in['ff_ln_b'], 'L0_ffn_ff_w1': _L0_ffn_in['ff_w1'], 'L0_ffn_ff_b1': _L0_ffn_in['ff_b1'], 'L0_ffn_ff_w2': _L0_ffn_in['ff_w2'], 'L0_ffn_ff_b2': _L0_ffn_in['ff_b2'], 'L1_attn_W_qkv': _L1_attn_in['W_qkv'], 'L1_attn_b_qkv': _L1_attn_in['b_qkv'], 'L1_attn_W_out': _L1_attn_in['W_out'], 'L1_attn_b_out': _L1_attn_in['b_out'], 'L1_attn_W_gate': _L1_attn_in['W_gate'], 'L1_attn_b_gate': _L1_attn_in['b_gate'], 'L1_attn_pos_bias': _L1_attn_in['pos_bias'], 'L1_attn_scale_embed': _L1_attn_in['scale_embed'], 'L1_attn_if_gain': _L1_attn_in['if_gain'], 'L1_attn_disp_amp': _L1_attn_in['disp_amp'], 'L1_ffn_Wg': _L1_ffn_in['Wg'], 'L1_ffn_W1': _L1_ffn_in['W1'], 'L1_ffn_b1': _L1_ffn_in['b1'], 'L1_ffn_W2': _L1_ffn_in['W2'], 'L1_ffn_b2': _L1_ffn_in['b2']}

def reference(x, x_txt, L0_tok_conv_w, L0_tok_conv_b, L0_tok_cls_token, L0_tok_pos_embed, L0_tok_ln1_w, L0_tok_ln1_b, L0_tok_qkv_w, L0_tok_qkv_b, L0_tok_proj_w, L0_tok_proj_b, L0_tok_ln2_w, L0_tok_ln2_b, L0_tok_fc1_w, L0_tok_fc1_b, L0_tok_fc2_w, L0_tok_fc2_b, L0_tok_norm_w, L0_tok_norm_b, L0_txt_word2sememe, L0_txt_W, L0_attn_w_qkv, L0_attn_w_agg, L0_attn_b_agg, L0_ffn_ln_in_g, L0_ffn_ln_in_b, L0_ffn_router_w, L0_ffn_router_b, L0_ffn_ew1, L0_ffn_eb1, L0_ffn_ew2, L0_ffn_eb2, L0_ffn_sw1, L0_ffn_sb1, L0_ffn_sw2, L0_ffn_sb2, L0_ffn_ff_ln_g, L0_ffn_ff_ln_b, L0_ffn_ff_w1, L0_ffn_ff_b1, L0_ffn_ff_w2, L0_ffn_ff_b2, L1_attn_W_qkv, L1_attn_b_qkv, L1_attn_W_out, L1_attn_b_out, L1_attn_W_gate, L1_attn_b_gate, L1_attn_pos_bias, L1_attn_scale_embed, L1_attn_if_gain, L1_attn_disp_amp, L1_ffn_Wg, L1_ffn_W1, L1_ffn_b1, L1_ffn_W2, L1_ffn_b2):
    import jax
    import jax.numpy as jnp

    def _L0_tok_ref(x, conv_w, conv_b, cls_token, pos_embed, ln1_w, ln1_b, qkv_w, qkv_b, proj_w, proj_b, ln2_w, ln2_b, fc1_w, fc1_b, fc2_w, fc2_b, norm_w, norm_b):
        import jax, jax.numpy as jnp
        import numpy as np
        DEPTH = 4
        HEADS = 8
        DIM = 128
        HID = 256
        P = 16
        IMG = 224
        GRID = IMG // P
        NPATCH = GRID * GRID
        NTOK = NPATCH + 1
        BATCH = 64
        EPS = 1e-05

        def layernorm(x, w, b):
            mu = jnp.mean(x, axis=-1, keepdims=True)
            var = jnp.mean(jnp.square(x - mu), axis=-1, keepdims=True)
            return (x - mu) * jax.lax.rsqrt(var + EPS) * w + b
        B = x.shape[0]
        hd = DIM // HEADS
        scale = hd ** (-0.5)
        patches = x.reshape(B, 3, GRID, P, GRID, P)
        patches = patches.transpose(0, 2, 4, 1, 3, 5).reshape(B, NPATCH, 3 * P * P)
        tok = patches @ conv_w + conv_b
        cls = jnp.broadcast_to(cls_token, (B, 1, DIM))
        h = jnp.concatenate([cls, tok], axis=1) + pos_embed
        for i in range(DEPTH):
            y = layernorm(h, ln1_w[i], ln1_b[i])
            qkv = (y @ qkv_w[i] + qkv_b[i]).reshape(B, NTOK, 3, HEADS, hd)
            qkv = qkv.transpose(2, 0, 3, 1, 4)
            q, k, v = (qkv[0], qkv[1], qkv[2])
            attn = jax.nn.softmax(jnp.einsum('bhnd,bhmd->bhnm', q, k) * scale, axis=-1)
            o = jnp.einsum('bhnm,bhmd->bhnd', attn, v)
            o = o.transpose(0, 2, 1, 3).reshape(B, NTOK, DIM)
            h = h + (o @ proj_w[i] + proj_b[i])
            y = layernorm(h, ln2_w[i], ln2_b[i])
            y = jax.nn.gelu(y @ fc1_w[i] + fc1_b[i], approximate=False)
            h = h + (y @ fc2_w[i] + fc2_b[i])
        return layernorm(h, norm_w, norm_b)

    def _L0_txt_ref(x, word2sememe, W):
        import jax, jax.numpy as jnp
        import numpy as np
        import math
        VOCAB = 8000
        SEMEME_SIZE = 512
        D_MODEL = 128
        B, S = (8, 512)
        SPARSITY = 0.005
        onehot = word2sememe[x]
        scalar = onehot.sum(-1) + 1e-06
        embed = jnp.einsum('bsk,kd->bsd', onehot, W)
        return embed * (math.sqrt(D_MODEL) / scalar)[..., None]

    def _L0_attn_ref(z, w_qkv, w_agg, b_agg):
        import jax, jax.numpy as jnp
        import numpy as np
        from math import sqrt
        bs, N, D = z.shape
        H = 8
        Dh = D // H
        qkv = jnp.einsum('bnd,ed->bne', z, w_qkv).reshape(bs, N, 3, H, Dh)
        q, k, v = jnp.moveaxis(qkv, 2, 0)
        q = q.transpose(0, 2, 1, 3)
        k = k.transpose(0, 2, 1, 3)
        v = v.transpose(0, 2, 1, 3)
        scores = jnp.einsum('bhnd,bhmd->bhnm', q, k) / sqrt(Dh)
        attn = jax.nn.softmax(scores, axis=-1)
        sa = jnp.einsum('bhnm,bhmd->bhnd', attn, v)
        sa = sa.transpose(0, 2, 1, 3).reshape(bs, N, H * Dh)
        out = jnp.einsum('bnd,ed->bne', sa, w_agg) + b_agg
        return out

    def _L0_ffn_ref(x, ln_in_g, ln_in_b, router_w, router_b, ew1, eb1, ew2, eb2, sw1, sb1, sw2, sb2, ff_ln_g, ff_ln_b, ff_w1, ff_b1, ff_w2, ff_b2):
        import jax, jax.numpy as jnp
        import numpy as np
        B, S, D = (4, 256, 128)
        E = 16
        DH = 4 * D
        DS = 2 * D
        TOP_K = 2
        TEMP = 0.7
        SHARED_SCALE = 0.25
        EPS = 1e-05

        def layer_norm(x, g, b):
            mu = jnp.mean(x, axis=-1, keepdims=True)
            var = jnp.mean(jnp.square(x - mu), axis=-1, keepdims=True)
            return (x - mu) * jax.lax.rsqrt(var + EPS) * g + b
        h = layer_norm(x, ln_in_g, ln_in_b)
        gate = jax.nn.softmax((h @ router_w + router_b) / TEMP, axis=-1)
        vals, idx = jax.lax.top_k(gate, TOP_K)
        comb = jnp.sum(jax.nn.one_hot(idx, E, dtype=h.dtype) * vals[..., None], axis=-2)
        eh = jax.nn.silu(jnp.einsum('bsd,edh->ebsh', h, ew1) + eb1[:, None, None, :])
        ey = jnp.einsum('ebsh,ehd->ebsd', eh, ew2) + eb2[:, None, None, :]
        mix = jnp.einsum('bse,ebsd->bsd', comb, ey)
        shared = (jax.nn.silu(h @ sw1 + sb1) @ sw2 + sb2) * SHARED_SCALE
        moe_out = mix + shared
        fh = layer_norm(moe_out, ff_ln_g, ff_ln_b)
        ff_out = jax.nn.silu(fh @ ff_w1 + ff_b1) @ ff_w2 + ff_b2
        return x + moe_out + ff_out

    def _L1_attn_ref(x, W_qkv, b_qkv, W_out, b_out, W_gate, b_gate, pos_bias, scale_embed, if_gain, disp_amp):
        import jax, jax.numpy as jnp
        import numpy as np
        import math
        _DENSE_LOCAL_W = 32
        _DYADIC = [48, 64, 96, 128, 192, 64, 96, 128, 192, 256, 384, 512, 768, 1024]
        OFFSETS = np.array(sorted(set(range(0, _DENSE_LOCAL_W + 1)) | set(_DYADIC)), dtype=np.int32)
        NUM_OFFSETS = len(OFFSETS)
        H = 8
        _LOG_MAX = math.log(1.0 + 4096.0)
        _HEAD_OMEGAS = [0.0, 0.0, 1 * math.pi / _LOG_MAX, 1 * math.pi / _LOG_MAX, 4 * math.pi / _LOG_MAX, 4 * math.pi / _LOG_MAX, 6 * math.pi / _LOG_MAX, 6 * math.pi / _LOG_MAX]
        _log_d = np.log(1.0 + OFFSETS.astype(np.float64))
        _CK = np.zeros((NUM_OFFSETS, H), dtype=np.float32)
        for _h, _om in enumerate(_HEAD_OMEGAS):
            if _om > 0.0:
                _CK[:, _h] = np.cos(_om * _log_d)
        DISP_COS_KERNEL = jnp.asarray(_CK)
        B, N, D = (1, 512, 128)
        HD = D // H
        Bx, Nx, Dx = x.shape
        qkv = x @ W_qkv + b_qkv
        q, k, v = jnp.split(qkv, 3, axis=-1)
        q = q.reshape(Bx, Nx, H, HD).transpose(0, 2, 1, 3)
        k = k.reshape(Bx, Nx, H, HD).transpose(0, 2, 1, 3)
        v = v.reshape(Bx, Nx, H, HD).transpose(0, 2, 1, 3)
        deltas = jnp.asarray(OFFSETS)
        pos = jnp.arange(Nx)
        j = pos[None, :] - deltas[:, None]
        valid = j >= 0
        jc = jnp.maximum(j, 0)
        kg = k[:, :, jc]
        vg = v[:, :, jc]
        km = kg * (1.0 + scale_embed)[None, None, :, None, :]
        eff_pb = pos_bias + DISP_COS_KERNEL * disp_amp[None, :]
        scores = jnp.einsum('bhnd,bhond->bhon', q, km) / math.sqrt(HD)
        scores = scores + eff_pb.T[None, :, :, None]
        scores = jnp.where(valid[None, None], scores, -jnp.inf)
        attn = jax.nn.softmax(scores, axis=2)
        out = jnp.einsum('bhon,bhond->bhnd', attn, vg)
        out = out * if_gain[None, :, None, None]
        out_flat = out.transpose(0, 2, 1, 3).reshape(Bx, Nx, Dx)
        gate = jax.nn.sigmoid(x @ W_gate + b_gate)
        return out_flat * gate @ W_out + b_out

    def _L1_ffn_ref(x, Wg, W1, b1, W2, b2):
        import jax, jax.numpy as jnp
        import numpy as np
        B, S, D, H, O, E, TOPK = (4, 512, 128, 256, 128, 8, 2)
        Bsz, Seq, Din = x.shape
        T = Bsz * Seq
        xm = x.reshape(T, Din)
        probs = jax.nn.softmax(xm @ Wg, axis=-1)
        top_p, top_i = jax.lax.top_k(probs, TOPK)
        gates = jnp.zeros((T, E), dtype=probs.dtype).at[jnp.arange(T)[:, None], top_i].set(top_p)
        h = jax.nn.gelu(jnp.einsum('td,edh->teh', xm, W1) + b1[None])
        y = jnp.einsum('teh,eho->teo', h, W2) + b2[None]
        out = jnp.einsum('te,teo->to', gates, y)
        return out.reshape(Bsz, Seq, O)
    h = _L0_tok_ref(x, L0_tok_conv_w, L0_tok_conv_b, L0_tok_cls_token, L0_tok_pos_embed, L0_tok_ln1_w, L0_tok_ln1_b, L0_tok_qkv_w, L0_tok_qkv_b, L0_tok_proj_w, L0_tok_proj_b, L0_tok_ln2_w, L0_tok_ln2_b, L0_tok_fc1_w, L0_tok_fc1_b, L0_tok_fc2_w, L0_tok_fc2_b, L0_tok_norm_w, L0_tok_norm_b)
    h = jnp.concatenate([h, _L0_txt_ref(x_txt, L0_txt_word2sememe, L0_txt_W)], axis=1)
    h = h + _L0_attn_ref(_layernorm(h, axis=-1), L0_attn_w_qkv, L0_attn_w_agg, L0_attn_b_agg)
    h = h + _L0_ffn_ref(_layernorm(h, axis=-1), L0_ffn_ln_in_g, L0_ffn_ln_in_b, L0_ffn_router_w, L0_ffn_router_b, L0_ffn_ew1, L0_ffn_eb1, L0_ffn_ew2, L0_ffn_eb2, L0_ffn_sw1, L0_ffn_sb1, L0_ffn_sw2, L0_ffn_sb2, L0_ffn_ff_ln_g, L0_ffn_ff_ln_b, L0_ffn_ff_w1, L0_ffn_ff_b1, L0_ffn_ff_w2, L0_ffn_ff_b2)
    h = h + _L1_attn_ref(_layernorm(h, axis=-1), L1_attn_W_qkv, L1_attn_b_qkv, L1_attn_W_out, L1_attn_b_out, L1_attn_W_gate, L1_attn_b_gate, L1_attn_pos_bias, L1_attn_scale_embed, L1_attn_if_gain, L1_attn_disp_amp)
    h = h + _L1_ffn_ref(_layernorm(h, axis=-1), L1_ffn_Wg, L1_ffn_W1, L1_ffn_b1, L1_ffn_W2, L1_ffn_b2)
    return h

_drawn_inputs = setup_inputs


def setup_inputs(seed=0):
    import zlib

    import numpy as np

    out = dict(_drawn_inputs(seed))
    spreads = {'L0_tok_conv_b': (0.0, 0.1),
     'L0_tok_ln1_w': (1.0, 0.6),
     'L0_tok_ln1_b': (0.0, 0.8),
     'L0_tok_qkv_b': (0.0, 0.1),
     'L0_tok_proj_b': (0.0, 0.1),
     'L0_tok_ln2_w': (1.0, 0.6),
     'L0_tok_ln2_b': (0.0, 0.8),
     'L0_tok_fc1_b': (0.0, 0.305),
     'L0_tok_fc2_b': (0.0, 0.1),
     'L0_tok_norm_w': (1.0, 0.2),
     'L0_tok_norm_b': (0.0, 0.1),
     'L0_ffn_ln_in_g': (1.0, 0.6),
     'L0_ffn_ln_in_b': (0.0, 0.8),
     'L0_ffn_router_b': (0.0, 0.8),
     'L0_ffn_eb1': (0.0, 0.8),
     'L0_ffn_eb2': (0.0, 0.8),
     'L0_ffn_sb1': (0.0, 0.8),
     'L0_ffn_sb2': (0.0, 1.855),
     'L0_ffn_ff_ln_g': (1.0, 0.6),
     'L0_ffn_ff_ln_b': (0.0, 0.8),
     'L0_ffn_ff_b1': (0.0, 0.8),
     'L0_ffn_ff_b2': (0.0, 0.342),
     'L1_attn_b_gate': (0.0, 0.8),
     'L1_attn_pos_bias': (0.0010000000474974513, 0.6),
     'L1_attn_scale_embed': (0.0, 0.8),
     'L1_attn_if_gain': (1.0, 0.6),
     'L1_attn_disp_amp': (0.10000000149011612, 0.6),
     'L1_ffn_b1': (0.0, 2.0),
     'L1_ffn_b2': (0.0, 0.694)}
    factors = {'L0_tok_cls_token': 8.0,
     'L0_tok_pos_embed': 4.495,
     'L0_attn_b_agg': 8.0,
     'L0_ffn_router_w': 8.0,
     'L0_ffn_ew1': 8.0,
     'L0_ffn_ew2': 8.0,
     'L0_ffn_sw1': 8.0,
     'L0_ffn_sw2': 8.0,
     'L0_ffn_ff_w1': 5.048,
     'L0_ffn_ff_w2': 4.676,
     'L1_attn_W_qkv': 8.0,
     'L1_attn_b_qkv': 8.0,
     'L1_attn_W_out': 8.0,
     'L1_attn_b_out': 24.218,
     'L1_attn_W_gate': 8.0}
    for name, (base, spread) in spreads.items():
        noise = np.random.default_rng([zlib.crc32(name.encode()), seed]).standard_normal(out[name].shape)
        drawn = base * np.exp(spread * noise) if base else spread * noise
        out[name] = jnp.asarray(drawn.astype(out[name].dtype))
    for name, factor in factors.items():
        out[name] = (out[name] * factor).astype(out[name].dtype)
    return out
```

```python
import math
from contextlib import ExitStack

import concourse.bass as bass
from concourse import mybir

F32 = mybir.dt.float32
BF16 = mybir.dt.bfloat16
I32 = mybir.dt.int32
ACT = mybir.ActivationFunctionType
ALU = mybir.AluOpType
AX = mybir.AxisListType

P = 128
BATCH = 32
HEADS, HD = 8, 16
SLOT = 32
EPS = 1e-5
LN_LINKS = 13
RSQRT_MAGIC = float(0x5F3759DF)


class Semaphores:

    FIRST = 110

    def __init__(self, nc, ctx):
        self.nc, self.ctx, self.next = nc, ctx, self.FIRST

    def take(self, name):
        self.next += 1
        return self.ctx.enter_context(self.nc.semaphore(name, num=self.next - 1))

    def finish(self):
        self.nc.all_engine_barrier(sems_to_clear=range(self.FIRST, self.next))


class Geometry:

    def __init__(self, tokens):
        self.tokens = tokens
        self.tiles = -(-tokens // P)
        self.start = [t * P for t in range(self.tiles - 1)] + [tokens - P]
        self.own = [0] * (self.tiles - 1) + [P - (tokens - (self.tiles - 1) * P)]


def rsqrt(e, linked, v, y, s):
    linked(e.tensor_scalar(y.bitcast(I32), v.bitcast(I32), -0.5, RSQRT_MAGIC, ALU.mult, ALU.add))
    for _ in range(3):
        linked(e.tensor_tensor(s, y, y, ALU.mult))
        linked(e.scalar_tensor_tensor(s, s, -0.5, v, ALU.mult, ALU.mult))
        linked(e.scalar_tensor_tensor(y, s, 1.5, y, ALU.add, ALU.mult))


def chain(e, sig):
    count = [0]

    def linked(ins):
        count[0] += 1
        ins.then_inc(sig, 1)
        e.wait_ge(sig, count[0])

    return linked, count


def attention_phase(nc, tag, H, tokens, group, layers, w, ident, identb, consts, scratch):
    geo = Geometry(tokens)
    T, nt = tokens, geo.tiles
    G, rounds = group, BATCH // group
    mlp = "fc1" in w
    wide = nt * T <= 512
    jobs = [[(h, list(range(nt)))] for h in range(HEADS)] if wide else \
        [[(h, [t])] for h in range(HEADS) for t in range(nt)]
    jobs = [j[0] for j in jobs]
    Jb = len(jobs)
    J = G * Jb
    lag = Jb + (5 if wide else 10)
    JW = (nt if wide else 1) * T

    order = [("ln1", g, 0) for g in range(G)]
    for g in range(G):
        order += [("yT", g, 0), ("qk", g, 0), ("v", g, 0)]
    tick = [[] for _ in range(J + lag + 16)]
    for j in range(J):
        tick[j].append(("s", j // Jb, j))
        tick[j + lag].append(("st", j // Jb, j))
        tick[j + lag + 1].append(("pv", j // Jb, j))
    for g in range(G):
        tick[(g + 1) * Jb + 1].append(("m", g, 0))
        end = (g + 1) * Jb + lag
        tick[end].append(("os", g, 0))
        tick[end + 1].append(("o", g, 0))
        tick[end + 3].append(("oT", g, 0))
        tick[end + 4].append(("proj", g, 0))
        if mlp:
            tick[end + 7].append(("y2T", g, 0))
    for t in tick:
        order += t
    if mlp:
        for g in range(G):
            order += [("fc1", g, 0)]
            if g:
                order += [("fc2", g - 1, 0)]
        order += [("fc2", G - 1, 0)]

    needs = {"yT": 1, "qk": 2, "v": 1, "m": 1, "o": 2, "oT": 1, "proj": 1, "y2T": 1, "fc1": 2, "fc2": 1}
    use, uses = {}, 0
    for ev, g, _ in order:
        for i in range(needs.get(ev, 0)):
            use[ev, g, i] = (uses % 2, uses // 2)
            uses += 1
    assert uses % 2 == 0

    with ExitStack() as ctx:
        sems = Semaphores(nc, ctx)

        def sb(name, shape, dt=F32):
            return ctx.enter_context(nc.sbuf_tensor(f"{tag}_{name}", shape, dt))

        def signal(name):
            return sems.take(f"{tag}_{name}")

        Wqk = sb("Wqk", [P, 2 * P])
        Wv = sb("Wv", [P, P])
        Wp = sb("Wp", [P, P])
        cols = sb("cols", [P, 8])
        rows = sb("rows", [P, 3, P])
        if mlp:
            W1 = sb("W1", [P, 2 * P])
            W2 = sb("W2", [P, 2, P])
        bvm = sb("bvm", [P, nt, P])
        mask = sb("mask", [P, nt])
        Z = sb("Z", [P, G, nt, P])
        yT = sb("yT", [P, G, T])
        qk32 = sb("qk32", [P, G, 2, T])
        rest = sb("rest", [P, G, 2, T])
        parts = sb("parts", [P, G, 3, 2, T], BF16)
        QS = sb("QS", [P, G, HEADS, T], BF16)
        KS = sb("KS", [P, G, HEADS, T], BF16)
        VA = sb("VA", [P, G, nt, HEADS, SLOT])
        PR = sb("PR", [P, 4, JW])
        Mx = sb("Mx", [P, G, nt, HEADS])
        Mr = sb("Mr", [P, G, nt, HEADS])
        Mp = sb("Mp", [P, G, nt, 3, HEADS], BF16)
        MT = sb("MT", [3 * HEADS, G, T], BF16)
        OS = sb("OS", [P, 2, T])
        RD = sb("RD", [P, 2, nt, 4])
        ON = sb("ON", [P, G, nt, P])
        OT = sb("OT", [P, G, nt, P])
        hid = sb("hid", [P, G, 2, T]) if mlp else None
        st6 = sb("st6", [P, G, nt, 6])
        mv = sb("mv", [P, G, nt, 2])
        var = sb("var", [P, G * nt])
        rs = sb("rs", [P, G * nt])
        tmp = sb("tmp", [P, G * nt])
        banks = [ctx.enter_context(nc.psum_tensor(f"{tag}_ps{i}", [P, 512], F32)) for i in range(8)]
        S, ST, OB, GB = banks[0:2], banks[2:4], banks[4:6], banks[6:8]
        scr = nc.dram_tensor(f"{tag}_scr", (G, 2, HEADS, 3 * HD, T), BF16).ap()

        gready = [signal(f"gready{i}") for i in range(2)]
        gfree = [signal(f"gfree{i}") for i in range(2)]
        z_ready = signal("z_ready")
        z2_ready = signal("z2_ready")
        yT_ready = signal("yT_ready")
        y2T_ready = signal("y2T_ready")
        qk_ready = signal("qk_ready")
        p1_ready = signal("p1_ready")
        r1_ready = signal("r1_ready")
        p2_ready = signal("p2_ready")
        p3_ready = signal("p3_ready")
        spilled = [signal(f"spilled{g}") for g in range(G)]
        stacked = [signal(f"stacked{g}") for g in range(G)]
        v_ready = signal("v_ready")
        s_ready = signal("s_ready")
        s_maxed = signal("s_maxed")
        mp_ready = signal("mp_ready")
        mT_ready = signal("mT_ready")
        m_stacked = [signal(f"m_stacked{g}") for g in range(G)]
        st_ready = signal("st_ready")
        p_ready = signal("p_ready")
        pv_done = signal("pv_done")
        os_ready = signal("os_ready")
        o_turned = signal("o_turned")
        on_ready = signal("on_ready")
        oT_ready = signal("oT_ready")
        h_biased = signal("h_biased")
        h_attn = signal("h_attn")
        h2_biased = signal("h2_biased")
        h_done = signal("h_done")
        hid_ready = signal("hid_ready")
        fc2_done = signal("fc2_done")
        own = signal("own")
        last = signal("last")
        numbers = range(gready[0].num, last.num + 1)
        weights_in = sems.take(f"{tag}_weights_in")
        ready = sems.take(f"{tag}_ready")
        bvm_ready = sems.take(f"{tag}_bvm_ready")
        n_loads = 5 + 2 * mlp

        def hb(r, g):
            return H[:, bass.ds(r * G + g, 1), :, :].rearrange("p o t c -> p (o t) c")

        with nc.Block() as block:
            @block.vector
            def _(e):
                e.memset(KS[96:128, :, :, :], -1.0)
                e.memset(VA[:, :, :, :, :], 0.0)

            @block.sync
            def _(e):
                e.dma_start(mask[:, :], consts["mask"]).then_inc(ready, 16)
                e.wait_ge(ready, 16)
        with nc.Block() as block:
            @block.vector
            def _(e):
                for t in range(nt):
                    e.tensor_copy(VA[:, :, t, :, HD],
                                  mask[:, t:t + 1].unsqueeze(2).to_broadcast([P, G, HEADS]))

        def load_weights(layer):
            with nc.Block() as block:
                @block.sync
                def _(e):
                    loads = [(Wqk[:, :], w["qkv"][bass.ds(layer, 1), :, 0:2 * P].rearrange("o a b -> (o a) b")),
                             (Wv[:, :], w["qkv"][bass.ds(layer, 1), :, 2 * P:3 * P].rearrange("o a b -> (o a) b")),
                             (Wp[:, :], w["proj"][bass.ds(layer, 1)].rearrange("o a b -> (o a) b")),
                             (cols[:, :], w["cols"][bass.ds(layer, 1)].rearrange("o a b -> (o a) b")),
                             (rows[:, :, :], w["rows"][bass.ds(layer, 1)].rearrange("o a b -> o (a b)")
                              .to_broadcast([P, 3 * P]))]
                    if mlp:
                        loads += [(W1[:, :], w["fc1"][bass.ds(layer, 1)].rearrange("o a b -> (o a) b")),
                                  (W2[:, :, :], w["fc2"][bass.ds(layer, 1)].rearrange("o (c a) b -> (o a) c b", a=P))]
                    assert len(loads) == n_loads
                    for dst, src in loads:
                        e.dma_start(dst, src).then_inc(weights_in, 16)
                    e.wait_ge(weights_in, 16 * n_loads)

                @block.vector
                def _(e):
                    e.wait_ge(weights_in, 16 * n_loads)
                    for t in range(nt):
                        e.tensor_scalar(bvm[:, t, :], rows[:, 0, :], mask[:, t:t + 1], None, ALU.mult)
            nc.all_engine_barrier(sems_to_clear=range(weights_in.num, weights_in.num + 1))

        def one_round(block, r):
            @block.sync
            def _(e):
                for ev, g, j in order:
                    if ev == "v":
                        e.wait_ge(p3_ready, g + 1)
                        for p in range(3):
                            for x in range(2):
                                slot = p if x == 0 else 2 - p
                                e.dma_start(scr[g, x, :, slot * HD:(slot + 1) * HD, :],
                                            parts[:, g, p, x, :]).then_inc(spilled[g], 16)
                        e.wait_ge(spilled[g], 96)
                        for x, dst in ((0, QS), (1, KS)):
                            for row, at, length in ((0, 0, 48), (48, 0 if x == 0 else 16, 32),
                                                    (80, 0 if x == 0 else 32, 16)):
                                e.dma_start(dst[row:row + length, g, :, :],
                                            scr[g, x, :, at:at + length, :].rearrange("h r t -> r h t"))\
                                    .then_inc(stacked[g], 16)
                    if ev == "m":
                        e.wait_ge(mT_ready, g + 1)
                        for p in range(3):
                            e.dma_start(QS[96 + p:97 + p, g, :, :], MT[p * HEADS:(p + 1) * HEADS, g, :])\
                                .then_inc(m_stacked[g], 16)


            def bank_of(e, key):
                b, k = use[key]
                if k > 0:
                    e.wait_ge(gfree[b], k)
                return GB[b], gready[b]

            def filled(e, key):
                b, k = use[key]
                e.wait_ge(gready[b], k + 1)
                return GB[b], gfree[b]

            @block.tensor
            def _(e):
                for ev, g, j in order:
                    if ev in ("yT", "y2T"):
                        s = z_ready if ev == "yT" else z2_ready
                        e.wait_ge(s, g + 1)
                        bank, done = bank_of(e, (ev, g, 0))
                        for t in range(nt):
                            mm = e.transpose(bank[:, t * P:(t + 1) * P], Z[:, g, t, :], ident[:, :])
                        mm.then_inc(done, 1)
                    if ev == "qk":
                        e.wait_ge(yT_ready, g + 1)
                        for x in range(2):
                            bank, done = bank_of(e, (ev, g, x))
                            e.matmul(bank[:, 0:T], Wqk[:, x * P:(x + 1) * P], yT[:, g, :],
                                     start=True, stop=True).then_inc(done, 1)
                    if ev == "v":
                        bank, done = bank_of(e, (ev, g, 0))
                        for t in range(nt):
                            mm = e.matmul(bank[:, t * P:(t + 1) * P], yT[:, g, geo.start[t]:geo.start[t] + P],
                                          Wv[:, :], start=True, stop=True)
                        mm.then_inc(done, 1)
                    if ev in ("s", "st"):
                        h, ts = jobs[j % Jb]
                        if j % Jb == 0:
                            if ev == "s":
                                e.wait_ge(stacked[g], 96)
                            else:
                                e.wait_ge(m_stacked[g], 48)
                        done, read, bank = (s_ready, s_maxed, S[j % 2]) if ev == "s" else \
                            (st_ready, p_ready, ST[j % 2])
                        if j > 1:
                            e.wait_ge(read, j - 1)
                        for i, t in enumerate(ts):
                            at = slice(geo.start[t], geo.start[t] + P)
                            if ev == "s":
                                lhs, rhs = QS[0:96, g, h, at], KS[0:96, g, h, :]
                            else:
                                lhs, rhs = KS[0:99, g, h, at], QS[0:99, g, h, :]
                            mm = e.matmul(bank[:, i * T:(i + 1) * T], lhs, rhs, start=True, stop=True)
                        mm.then_inc(done, 1)
                    if ev == "m":
                        e.wait_ge(mp_ready, g + 1)
                        bank, done = bank_of(e, (ev, g, 0))
                        bb = bank[:, :].bitcast(BF16)
                        for t in range(nt):
                            mm = e.transpose(bb[0:3 * HEADS, t * P:(t + 1) * P],
                                             Mp[:, g, t, :, :].rearrange("p a h -> p (a h)"), identb[:, :])
                        mm.then_inc(done, 1)
                    if ev == "pv":
                        h, ts = jobs[j % Jb]
                        if j % Jb == 0:
                            e.wait_ge(v_ready, g + 1)
                            if g > 0:
                                e.wait_ge(os_ready, g)
                        e.wait_ge(p_ready, j + 1)
                        for i, t in enumerate(ts):
                            mm = e.matmul(OB[h // 4][SLOT * (h % 4):SLOT * (h % 4 + 1), 0:T],
                                          VA[:, g, t, h, :], PR[:, j % 4, i * T:(i + 1) * T],
                                          start=(t == 0), stop=(t == nt - 1))
                        mm.then_inc(pv_done, 1)
                    if ev == "o":
                        e.wait_ge(os_ready, g + 1)
                        for x in range(2):
                            bank, done = bank_of(e, (ev, g, x))
                            for t in range(nt):
                                mm = e.transpose(bank[:, t * P:(t + 1) * P],
                                                 OS[:, x, geo.start[t]:geo.start[t] + P], ident[:, :])
                            mm.then_inc(done, 1)
                    if ev == "oT":
                        e.wait_ge(on_ready, g + 1)
                        bank, done = bank_of(e, (ev, g, 0))
                        for t in range(nt):
                            mm = e.transpose(bank[:, t * P:(t + 1) * P], ON[:, g, t, :], ident[:, :])
                        mm.then_inc(done, 1)
                    if ev == "proj":
                        e.wait_ge(oT_ready, g + 1)
                        bank, done = bank_of(e, (ev, g, 0))
                        for t in range(nt):
                            mm = e.matmul(bank[:, t * P:(t + 1) * P], OT[:, g, t, :], Wp[:, :],
                                          start=True, stop=True)
                        mm.then_inc(done, 1)
                    if ev == "fc1":
                        e.wait_ge(y2T_ready, g + 1)
                        for x in range(2):
                            bank, done = bank_of(e, (ev, g, x))
                            e.matmul(bank[:, 0:T], W1[:, x * P:(x + 1) * P], yT[:, g, :],
                                     start=True, stop=True).then_inc(done, 1)
                    if ev == "fc2":
                        e.wait_ge(hid_ready, g + 1)
                        bank, done = bank_of(e, (ev, g, 0))
                        for t in range(nt):
                            for x in range(2):
                                mm = e.matmul(bank[:, t * P:(t + 1) * P],
                                              hid[:, g, x, geo.start[t]:geo.start[t] + P], W2[:, x, :],
                                              start=(x == 0), stop=(x == 1))
                        mm.then_inc(done, 1)


            @block.scalar
            def _(e):
                def turned(g, ev, wcol, bcol, ready):
                    bank, free = filled(e, (ev, g, 0))
                    for t in range(nt):
                        o = geo.own[t]
                        a = e.activation(yT[:, g, geo.start[t] + o:geo.start[t] + P],
                                         bank[:, t * P + o:(t + 1) * P], ACT.Identity,
                                         scale=cols[:, wcol:wcol + 1], bias=cols[:, bcol:bcol + 1])
                    a.then_inc(ready, 1)
                    e.wait_ge(ready, g + 1)
                    e.sem_inc(free, 1)

                for ev, g, j in order:
                    if ev == "yT":
                        turned(g, ev, 2, 3, yT_ready)
                    if ev == "y2T":
                        e.wait_ge(v_ready, g + 1)
                        turned(g, ev, 4, 5, y2T_ready)
                    if ev == "qk":
                        for x in range(2):
                            bank, free = filled(e, (ev, g, x))
                            a = e.activation(qk32[:, g, x, :], bank[:, 0:T], ACT.Identity,
                                             bias=cols[:, x:x + 1])
                            a.then_inc(free, 1)
                        e.wait_ge(gfree[use[ev, g, 1][0]], use[ev, g, 1][1] + 1)
                        e.sem_inc(qk_ready, 1)
                    if ev == "st":
                        if j > 3:
                            e.wait_ge(pv_done, j - 3)
                        e.wait_ge(st_ready, j + 1)
                        e.activation(PR[:, j % 4, :], ST[j % 2][:, 0:JW], ACT.Exp, scale=HD ** -0.5)\
                            .then_inc(p_ready, 1)
                    if ev == "oT":
                        bank, free = filled(e, (ev, g, 0))
                        e.activation(OT[:, g, :, :].rearrange("p t c -> p (t c)"), bank[:, 0:nt * P],
                                     ACT.Identity).then_inc(oT_ready, 1)
                        e.wait_ge(oT_ready, g + 1)
                        e.sem_inc(free, 1)
                    if ev == "fc1":
                        for x in range(2):
                            bank, free = filled(e, (ev, g, x))
                            e.activation(hid[:, g, x, :], bank[:, 0:T], ACT.Gelu,
                                         bias=cols[:, 6 + x:7 + x]).then_inc(free, 1)
                        e.wait_ge(gfree[use[ev, g, 1][0]], use[ev, g, 1][1] + 1)
                        e.sem_inc(hid_ready, 1)


            @block.gpsimd
            def _(e):
                for ev, g, j in order:
                    if ev == "qk":
                        e.wait_ge(qk_ready, g + 1)
                        e.tensor_copy(parts[:, g, 0, :, :], qk32[:, g, :, :]).then_inc(p1_ready, 1)
                        e.wait_ge(r1_ready, g + 1)
                        e.tensor_copy(parts[:, g, 1, :, :], rest[:, g, :, :]).then_inc(p2_ready, 1)
                    if ev == "v":
                        e.wait_ge(z_ready, g + 1)
                        e.tensor_tensor(hb(r, g), hb(r, g),
                                        rows[:, 1:2, :].to_broadcast([P, nt, P]), ALU.add)\
                            .then_inc(h_biased, 1)
                    if ev == "y2T":
                        e.wait_ge(z2_ready, g + 1)
                        e.tensor_tensor(hb(r, g), hb(r, g),
                                        rows[:, 2:3, :].to_broadcast([P, nt, P]), ALU.add)\
                            .then_inc(h2_biased, 1)


            @block.vector
            def _(e):
                def layer_norm(linked, gs, ready):
                    k = len(gs) * nt
                    for i, g in enumerate(gs):
                        for t in range(nt):
                            ins = e.bn_stats(st6[:, g, t, :], hb(r, g)[:, t, :])
                    linked(ins)
                    for g in gs:
                        for t in range(nt):
                            ins = e.bn_aggr(mv[:, g, t, :], st6[:, g, t, :])
                    linked(ins)
                    linked(e.tensor_scalar(var[:, 0:k], mv[:, gs[0]:gs[-1] + 1, :, 1].rearrange("p g t -> p (g t)"),
                                           EPS, None, ALU.add))
                    rsqrt(e, linked, var[:, 0:k], rs[:, 0:k], tmp[:, 0:k])
                    for i, g in enumerate(gs):
                        if ready is z_ready:
                            last = y2T_ready if mlp else yT_ready
                        else:
                            e.wait_ge(yT_ready, g + 1)
                        for t in range(nt):
                            ins = e.tensor_scalar(Z[:, g, t, :], hb(r, g)[:, t, :], mv[:, g, t, 0:1],
                                                  rs[:, i * nt + t:i * nt + t + 1], ALU.subtract, ALU.mult)
                        ins.then_inc(ready, 1)

                linked, links = chain(e, own)
                for ev, g, j in order:
                    if ev == "ln1" and g == 0:
                        layer_norm(linked, list(range(G)), z_ready)
                    if ev == "qk":
                        e.wait_ge(p1_ready, g + 1)
                        e.tensor_tensor(rest[:, g, :, :], qk32[:, g, :, :], parts[:, g, 0, :, :],
                                        ALU.subtract).then_inc(r1_ready, 1)
                        e.wait_ge(p2_ready, g + 1)
                        e.wait_ge(r1_ready, g + 1)
                        e.tensor_tensor(parts[:, g, 2, :, :], rest[:, g, :, :], parts[:, g, 1, :, :],
                                        ALU.subtract).then_inc(p3_ready, 1)
                    if ev == "v":
                        bank, free = filled(e, (ev, g, 0))
                        for t in range(nt):
                            ins = e.scalar_tensor_tensor(
                                VA[:, g, t, :, 0:HD],
                                bank[:, t * P:(t + 1) * P].rearrange("p (h d) -> p h d", d=HD),
                                mask[:, t:t + 1], bvm[:, t, :].rearrange("p (h d) -> p h d", d=HD),
                                ALU.mult, ALU.add)
                        ins.then_inc(v_ready, 1)
                        e.wait_ge(v_ready, g + 1)
                        e.sem_inc(free, 1)
                    if ev == "s":
                        h, ts = jobs[j % Jb]
                        e.wait_ge(s_ready, j + 1)
                        e.tensor_reduce(Mx[:, g, ts[0]:ts[-1] + 1, h],
                                        S[j % 2][:, 0:JW].rearrange("p (t k) -> p t k", k=T),
                                        AX.X, ALU.max).then_inc(s_maxed, 1)
                        if j % Jb == Jb - 1:
                            e.wait_ge(s_maxed, j + 1)
                            linked(e.tensor_copy(Mp[:, g, :, 0, :], Mx[:, g, :, :]))
                            linked(e.tensor_tensor(Mr[:, g, :, :], Mx[:, g, :, :], Mp[:, g, :, 0, :], ALU.subtract))
                            linked(e.tensor_copy(Mp[:, g, :, 1, :], Mr[:, g, :, :]))
                            e.tensor_tensor(Mp[:, g, :, 2, :], Mr[:, g, :, :], Mp[:, g, :, 1, :],
                                            ALU.subtract).then_inc(mp_ready, 1)
                    if ev == "m":
                        bank, free = filled(e, (ev, g, 0))
                        bb = bank[:, :].bitcast(BF16)
                        for t in range(nt):
                            o = geo.own[t]
                            ins = e.tensor_copy(MT[:, g, geo.start[t] + o:geo.start[t] + P],
                                                bb[0:3 * HEADS, t * P + o:(t + 1) * P])
                        ins.then_inc(mT_ready, 1)
                        e.wait_ge(mT_ready, g + 1)
                        e.sem_inc(free, 1)
                    if ev == "os":
                        e.wait_ge(pv_done, (g + 1) * Jb)
                        for x in range(2):
                            ins = e.tensor_copy(OS[:, x, :], OB[x][:, 0:T])
                        ins.then_inc(os_ready, 1)
                    if ev == "o":
                        for x in range(2):
                            bank, free = filled(e, (ev, g, x))
                            o4 = bank[:, 0:nt * P].rearrange("p (t h s) -> p t h s", t=nt, s=SLOT)
                            linked(e.reciprocal(RD[:, x, :, :], o4[:, :, :, HD]))
                            ins = e.tensor_tensor(
                                ON[:, g, :, x * 64:(x + 1) * 64].rearrange("p t (h d) -> p t h d", d=HD),
                                o4[:, :, :, 0:HD], RD[:, x, :, :].unsqueeze(3).to_broadcast([P, nt, 4, HD]),
                                ALU.mult)
                            ins.then_inc(free, 1)
                        b, k = use[ev, g, 1]
                        e.wait_ge(gfree[b], k + 1)
                        e.sem_inc(on_ready, 1)
                    if ev == "proj":
                        e.wait_ge(h_biased, g + 1)
                        bank, free = filled(e, (ev, g, 0))
                        e.tensor_tensor(hb(r, g), bank[:, 0:nt * P].rearrange("p (t c) -> p t c", c=P),
                                        hb(r, g), ALU.add).then_inc(h_attn, 1)
                        e.wait_ge(h_attn, g + 1)
                        e.sem_inc(free, 1)
                        if mlp:
                            layer_norm(linked, [g], z2_ready)
                    if ev == "fc2":
                        e.wait_ge(h2_biased, g + 1)
                        bank, free = filled(e, (ev, g, 0))
                        e.tensor_tensor(hb(r, g), bank[:, 0:nt * P].rearrange("p (t c) -> p t c", c=P),
                                        hb(r, g), ALU.add).then_inc(h_done, 1)
                        e.wait_ge(h_done, g + 1)
                        e.sem_inc(free, 1)


        with nc.Fori(0, layers) as layer:
            load_weights(layer)
            with nc.Fori(0, rounds) as r:
                with nc.Block(no_gpsimd_drain=True) as block:
                    one_round(block, r)
                nc.all_engine_barrier(sems_to_clear=numbers)
        sems.finish()


def ffn_phase(nc, tag, src, dst, cfg, w, ident):
    E, chunks, act, act_ff = cfg["experts"], cfg["chunks"], cfg["act"], cfg.get("ff_chunks", 0)
    shared = cfg.get("shared", 0)
    inner, ffc = cfg["inner"], cfg.get("ff_chunks", 0)
    units = [(e * chunks, chunks) for e in range(E)] + ([(E * chunks, shared)] if shared else [])
    K = E + (1 if shared else 0)
    NCH = sum(n for _, n in units)
    tokens = src.shape[0]
    GT = 4
    full = tokens // (GT * P)
    left = tokens - full * GT * P
    assert 0 < left <= P

    with ExitStack() as ctx:
        sems = Semaphores(nc, ctx)

        def sb(name, shape, dt=F32):
            return ctx.enter_context(nc.sbuf_tensor(f"{tag}_{name}", shape, dt))

        def signal(name):
            return sems.take(f"{tag}_{name}")

        W1 = sb("W1", [P, NCH * P])
        W2 = sb("W2", [P, NCH, P])
        B1 = sb("B1", [P, NCH])
        WR = sb("WR", [P, E])
        RB = sb("RB", [P, E])
        B2 = sb("B2", [K, P])
        col = sb("col", [P, 4])
        if ffc:
            F1 = sb("F1", [P, ffc * P])
            F2 = sb("F2", [P, ffc, P])
            FB1 = sb("FB1", [P, ffc])
            FB2 = sb("FB2", [P, P])
        number = sb("number", [P, E])
        X = sb("X", [P, full * GT + 1, P])
        Y = sb("Y", [P, GT, P])
        Z = sb("Z", [P, GT, P])
        yT = sb("yT", [P, GT * P])
        lg = sb("lg", [P, GT, E])
        pe_ = sb("expd", [P, GT, E])
        gate = sb("gate", [P, GT, E])
        comb = sb("comb", [P, GT, K])
        pick = sb("pick", [P, GT, E])
        top = sb("top", [P, GT, 8])
        topi = sb("topi", [P, GT, 8], mybir.dt.uint32)
        topf = sb("topf", [P, GT, 2])
        big = sb("big", [P, GT])
        tot = sb("tot", [P, GT])
        combT = sb("combT", [K, GT * P])
        hid = sb("hid", [P, 2, max(chunks, ffc), GT * P])
        acc = sb("acc", [P, GT, P])
        out = sb("out", [P, GT, P])
        st6 = sb("st6", [P, GT, 6])
        mv = sb("mv", [P, GT, 2])
        var = sb("var", [P, GT])
        rs = sb("rs", [P, GT])
        tmp = sb("tmp", [P, GT])
        banks = [ctx.enter_context(nc.psum_tensor(f"{tag}_ps{i}", [P, 512], F32)) for i in range(8)]
        HB, YB, GB = banks[0:4], banks[4:6], banks[6]

        first = signal("first")
        z_ready = signal("z_ready")
        gready = signal("gready")
        gfree = signal("gfree")
        yT_ready = signal("yT_ready")
        lg_ready = signal("lg_ready")
        e_ready = signal("e_ready")
        comb_ready = signal("comb_ready")
        cT_ready = signal("cT_ready")
        h_filled = signal("h_filled")
        h_ready = signal("h_ready")
        y_filled = signal("y_filled")
        y_added = signal("y_added")
        x_ready = signal("x_ready")
        out_ready = signal("out_ready")
        own = signal("own")
        numbers = range(first.num, own.num + 1)
        loaded = sems.take(f"{tag}_loaded")
        stored = sems.take(f"{tag}_stored")

        loads = [(X[:, 0:full * GT, :], src[0:full * GT * P, :].rearrange("(t p) c -> p t c", p=P)),
                 (X[0:left, full * GT, :], src[full * GT * P:tokens, :]),
                 (W1[:, :], w["w1"]), (W2[:, :, :], w["w2"].rearrange("(k p) c -> p k c", p=P)),
                 (B1[:, :], w["b1"]), (WR[:, :], w["router"]), (RB[:, :], w["router_b"].to_broadcast([P, E])),
                 (B2[:, :], w["b2"]), (number[:, :], w["number"].to_broadcast([P, E])),
                 (col[:, :], w["cols"])]
        if ffc:
            loads += [(F1[:, :], w["f1"]), (F2[:, :, :], w["f2"].rearrange("(k p) c -> p k c", p=P)),
                      (FB1[:, :], w["fb1"]), (FB2[:, :], w["fb2"].to_broadcast([P, P]))]

        with nc.Block() as block:
            @block.sync
            def _(e):
                for to, fr in loads:
                    e.dma_start(to, fr).then_inc(loaded, 16)
                e.wait_ge(loaded, 16 * len(loads))

            @block.vector
            def _(e):
                if shared:
                    e.memset(comb[:, :, E:K], cfg["shared_scale"])

        def one_round(block, r, nt, rows):
            N = (nt - 1) * P + rows
            steps = []
            for u in range(len(units)):
                steps.append(("up", u))
                if u:
                    steps.append(("down", u - 1))
            steps.append(("down", len(units) - 1))
            hb_count = {}
            k = 0
            for u, (_, n) in enumerate(units):
                hb_count[u] = k
                k += n
            U = len(units)
            hb_count[U] = k

            def x_of():
                if isinstance(r, int):
                    return X[0:rows, GT * r:GT * r + nt, :]
                return X[0:rows, bass.ds(r * GT, nt), :]

            def chunk_list(u):
                return units[u] if u < U else (0, ffc)

            @block.tensor
            def _(e):
                use = [0]

                def general():
                    if use[0] > 0:
                        e.wait_ge(gfree, use[0])
                    use[0] += 1

                def turn(count):
                    e.wait_ge(z_ready, count)
                    general()
                    for t in range(nt):
                        mm = e.transpose(GB[:, t * P:t * P + rows], Z[0:rows, t, :], ident[0:rows, 0:rows])
                    mm.then_inc(gready, 1)

                def up(u):
                    w1 = W1 if u < U else F1
                    at, n = chunk_list(u)
                    for c in range(n):
                        k = hb_count[u] + c
                        if k > 3:
                            e.wait_ge(h_ready, k - 3)
                        e.matmul(HB[k % 4][:, 0:N], w1[:, (at + c) * P:(at + c + 1) * P], yT[:, 0:N],
                                 start=True, stop=True).then_inc(h_filled, 1)

                def down(u):
                    w2 = W2 if u < U else F2
                    at, n = chunk_list(u)
                    e.wait_ge(h_ready, hb_count[u] + n)
                    e.wait_ge(y_added, u)
                    for t in range(nt):
                        for c in range(n):
                            mm = e.matmul(YB[u % 2][0:rows, t * P:(t + 1) * P],
                                          hid[:, u % 2, c, t * P:t * P + rows], w2[:, at + c, :],
                                          start=(c == 0), stop=(c == n - 1))
                    mm.then_inc(y_filled, 1)

                turn(1)
                e.wait_ge(yT_ready, 1)
                general()
                for t in range(nt):
                    mm = e.matmul(GB[0:rows, t * E:(t + 1) * E], yT[:, t * P:t * P + rows], WR[:, :],
                                  start=True, stop=True)
                mm.then_inc(gready, 1)
                for n, (what, u) in enumerate(steps):
                    if n == 1:
                        e.wait_ge(comb_ready, 1)
                        general()
                        for t in range(nt):
                            mm = e.transpose(GB[0:K, t * P:t * P + rows], comb[0:rows, t, :],
                                             ident[0:rows, 0:rows])
                        mm.then_inc(gready, 1)
                        e.wait_ge(cT_ready, 1)
                        general()
                        for t in range(nt):
                            mm = e.matmul(GB[0:rows, t * P:(t + 1) * P], combT[:, t * P:t * P + rows],
                                          B2[:, :], start=True, stop=True)
                        mm.then_inc(gready, 1)
                    (up if what == "up" else down)(u)
                if ffc:
                    turn(2)
                    e.wait_ge(yT_ready, 2)
                    up(U)
                    down(U)

            @block.scalar
            def _(e):
                def turned(count, use, c0):
                    e.wait_ge(gready, use)
                    if count == 2:
                        e.wait_ge(h_filled, hb_count[U])
                    if inner or count == 2:
                        ins = e.activation(yT[:, 0:N], GB[:, 0:N], ACT.Identity,
                                           scale=col[:, c0:c0 + 1], bias=col[:, c0 + 1:c0 + 2])
                    else:
                        ins = e.activation(yT[:, 0:N], GB[:, 0:N], ACT.Identity)
                    ins.then_inc(yT_ready, 1)
                    e.wait_ge(yT_ready, count)
                    e.sem_inc(gfree, 1)

                def hidden(u):
                    b1 = B1 if u < U else FB1
                    at, n = chunk_list(u)
                    if u > 1:
                        e.wait_ge(y_filled, u - 1)
                    for c in range(n):
                        k = hb_count[u] + c
                        e.wait_ge(h_filled, k + 1)
                        e.activation(hid[:, u % 2, c, 0:N], HB[k % 4][:, 0:N], act,
                                     bias=b1[:, at + c:at + c + 1]).then_inc(h_ready, 1)

                turned(1, 1, 0)
                e.wait_ge(lg_ready, 1)
                e.activation(pe_[0:rows, 0:nt, :], lg[0:rows, 0:nt, :], ACT.Exp,
                             scale=1.0 / cfg["temperature"]).then_inc(e_ready, 1)
                hidden(0)
                e.wait_ge(gready, 3)
                e.activation(combT[:, 0:N], GB[0:K, 0:N], ACT.Identity).then_inc(cT_ready, 1)
                e.wait_ge(cT_ready, 1)
                e.sem_inc(gfree, 1)
                for u in range(1, U):
                    hidden(u)
                if ffc:
                    turned(2, 5, 2)
                    hidden(U)

            @block.gpsimd
            def _(e):
                if inner:
                    e.wait_ge(z_ready, 1)
                    e.tensor_tensor(out[0:rows, 0:nt, :], x_of(), Y[0:rows, 0:nt, :], ALU.add)\
                        .then_inc(x_ready, 1)
                    e.wait_ge(x_ready, 1)
                    e.tensor_tensor(out[0:rows, 0:nt, :], out[0:rows, 0:nt, :],
                                    FB2[0:rows, :].unsqueeze(1).to_broadcast([rows, nt, P]), ALU.add)\
                        .then_inc(x_ready, 1)

            @block.vector
            def _(e):
                linked, _n = chain(e, own)

                def norm(x, y):
                    for t in range(nt):
                        ins = e.bn_stats(st6[0:rows, t, :], x[:, t, :])
                    linked(ins)
                    for t in range(nt):
                        ins = e.bn_aggr(mv[0:rows, t, :], st6[0:rows, t, :])
                    linked(ins)
                    linked(e.tensor_scalar(var[0:rows, 0:nt], mv[0:rows, 0:nt, 1], EPS, None, ALU.add))
                    rsqrt(e, linked, var[0:rows, 0:nt], rs[0:rows, 0:nt], tmp[0:rows, 0:nt])
                    for t in range(nt):
                        ins = e.tensor_scalar(y[0:rows, t, :], x[:, t, :], mv[0:rows, t, 0:1],
                                              rs[0:rows, t:t + 1], ALU.subtract, ALU.mult)
                    return ins

                if inner:
                    linked(norm(x_of(), Y))
                    norm(Y[0:rows, 0:nt, :], Z).then_inc(z_ready, 1)
                else:
                    norm(x_of(), Z).then_inc(z_ready, 1)
                L, G_, C, PK = (a[0:rows, 0:nt, :] for a in (lg, gate, comb, pick))
                e.wait_ge(gready, 2)
                linked(e.tensor_tensor(L, GB[0:rows, 0:nt * E].rearrange("p (t e) -> p t e", e=E),
                                       RB[0:rows, :].unsqueeze(1).to_broadcast([rows, nt, E]), ALU.add))
                e.sem_inc(gfree, 1)
                linked(e.tensor_reduce(big[0:rows, 0:nt], L, AX.X, ALU.max))
                e.tensor_tensor(L, L, big[0:rows, 0:nt].unsqueeze(2).to_broadcast([rows, nt, E]),
                                ALU.subtract).then_inc(lg_ready, 1)
                e.wait_ge(e_ready, 1)
                linked(e.tensor_reduce(tot[0:rows, 0:nt], pe_[0:rows, 0:nt, :], AX.X, ALU.add))
                linked(e.reciprocal(tot[0:rows, 0:nt], tot[0:rows, 0:nt]))
                linked(e.tensor_tensor(G_, pe_[0:rows, 0:nt, :],
                                       tot[0:rows, 0:nt].unsqueeze(2).to_broadcast([rows, nt, E]), ALU.mult))
                for t in range(nt):
                    ins = e.max(top[0:rows, t, :], gate[0:rows, t, :])
                linked(ins)
                for t in range(nt):
                    ins = e.max_index(topi[0:rows, t, :], top[0:rows, t, :], gate[0:rows, t, :])
                linked(ins)
                linked(e.tensor_copy(topf[0:rows, 0:nt, :], topi[0:rows, 0:nt, 0:2]))
                nb = number[0:rows, :].unsqueeze(1).to_broadcast([rows, nt, E])
                for i in range(2):
                    linked(e.tensor_tensor(PK if i == 0 else L, nb,
                                           topf[0:rows, 0:nt, i:i + 1].to_broadcast([rows, nt, E]),
                                           ALU.is_equal))
                linked(e.tensor_tensor(PK, PK, L, ALU.add))
                e.tensor_tensor(comb[0:rows, 0:nt, 0:E], PK, G_, ALU.mult).then_inc(comb_ready, 1)
                e.wait_ge(gready, 4)
                e.wait_ge(comb_ready, 1)
                e.tensor_copy(acc[0:rows, 0:nt, :],
                              GB[0:rows, 0:nt * P].rearrange("p (t c) -> p t c", c=P)).then_inc(y_added, 1)
                e.wait_ge(y_added, 1)
                e.sem_inc(gfree, 1)
                for u in range(U):
                    e.wait_ge(y_filled, u + 1)
                    e.wait_ge(y_added, u + 1)
                    for t in range(nt):
                        ins = e.scalar_tensor_tensor(acc[0:rows, t, :], YB[u % 2][0:rows, t * P:(t + 1) * P],
                                                     comb[0:rows, t, u:u + 1], acc[0:rows, t, :],
                                                     ALU.mult, ALU.add)
                    ins.then_inc(y_added, 1)
                e.wait_ge(y_added, U + 1)
                if ffc:
                    norm(acc[0:rows, 0:nt, :], Z).then_inc(z_ready, 1)
                    e.wait_ge(x_ready, 2)
                    linked(e.tensor_tensor(out[0:rows, 0:nt, :], out[0:rows, 0:nt, :], acc[0:rows, 0:nt, :], ALU.add))
                    e.wait_ge(y_filled, U + 1)
                    e.tensor_tensor(out[0:rows, 0:nt, :],
                                    YB[U % 2][0:rows, 0:nt * P].rearrange("p (t c) -> p t c", c=P),
                                    out[0:rows, 0:nt, :], ALU.add).then_inc(out_ready, 1)
                else:
                    e.tensor_tensor(out[0:rows, 0:nt, :], acc[0:rows, 0:nt, :], x_of(), ALU.add)\
                        .then_inc(out_ready, 1)

            @block.sync
            def _(e):
                e.wait_ge(out_ready, 1)
                if isinstance(r, int):
                    to = dst[GT * P * r:GT * P * r + N, :]
                    e.dma_start(to, out[0:rows, 0, :]).then_inc(stored, 16)
                else:
                    to = dst[bass.ds(r * (GT * P), GT * P), :].rearrange("(t p) c -> p t c", p=P)
                    e.dma_start(to, out[:, :, :]).then_inc(stored, 16)
                e.wait_ge(stored, 16)

        clear = range(min(numbers[0], stored.num), max(numbers[-1], stored.num) + 1)
        with nc.Fori(0, full) as r:
            with nc.Block(no_gpsimd_drain=True) as block:
                one_round(block, r, GT, P)
            nc.all_engine_barrier(sems_to_clear=clear)
        with nc.Block(no_gpsimd_drain=True) as block:
            one_round(block, full, 1, left)
        nc.all_engine_barrier(sems_to_clear=clear)
        sems.finish()


def offsets_of(tokens):
    far = (48, 64, 96, 128, 192, 256, 384, 512, 768, 1024)
    return [o for o in list(range(33)) + list(far) if o < tokens]


def dilated_phase(nc, tag, src, dst, w, ident, group=2):
    T = w["tokens"]
    geo = Geometry(T)
    nt = geo.tiles
    OFF = offsets_of(T)
    NO = len(OFF)
    STRIP = P // HEADS
    NS = -(-NO // STRIP)
    PAD = OFF[-1]
    G, rounds = group, BATCH // group
    KO = NO * HEADS

    with ExitStack() as ctx:
        sems = Semaphores(nc, ctx)

        def sb(name, shape, dt=F32):
            return ctx.enter_context(nc.sbuf_tensor(f"{tag}_{name}", shape, dt))

        def signal(name):
            return sems.take(f"{tag}_{name}")

        Wqkvg = sb("Wqkvg", [P, 4, P])
        Wo = sb("Wo", [P, P])
        cols = sb("cols", [P, 8])
        bo = sb("bo", [P, P])
        se = sb("se", [P, NO])
        heads = sb("heads", [P, HEADS])
        sel = sb("sel", [P, NO, P])
        spread = sb("spread", [P, STRIP, P])
        pb = sb("pb", [P, NS, 3])
        eff = sb("eff", [P, NS])
        mask = sb("mask", [P, nt, NO])
        X = sb("X", [P, BATCH, nt, P])
        Z = sb("Z", [P, G, nt, P])
        yT = sb("yT", [P, G, T])
        q = sb("q", [P, G, T])
        kpad = sb("kpad", [P, G, PAD + T])
        vpad = sb("vpad", [P, G, PAD + T])
        gt = sb("gt", [P, G, T])
        PR = sb("PR", [P, 4, T])
        SC = sb("SC", [P, NS, T])
        sm = sb("sm", [P, nt, NS * P])
        big = sb("big", [P, nt, HEADS])
        tot = sb("tot", [P, nt, HEADS])
        AT = sb("AT", [P, G, NS, T])
        AV = sb("AV", [P, 3, T])
        og = sb("og", [P, G, T])
        out = sb("out", [P, G, nt, P])
        st6 = sb("st6", [P, G, nt, 6])
        mv = sb("mv", [P, G, nt, 2])
        var = sb("var", [P, G * nt])
        rs = sb("rs", [P, G * nt])
        tmp = sb("tmp", [P, G * nt])
        banks = [ctx.enter_context(nc.psum_tensor(f"{tag}_ps{i}", [P, 512], F32)) for i in range(8)]
        SB, GB, BB, AB = banks[0:3], banks[3:5], banks[5:7], banks[7]

        order = [("ln", g, 0) for g in range(G)]
        order += [(ev, g, 0) for g in range(G) for ev in ("yT", "qkv")]
        for g in range(G):
            for i in range(NO):
                order.append(("sc", g, i))
                if g and i in (4, 14, 20):
                    order.append((("soft", "norm", "AT")[(4, 14, 20).index(i)], g - 1, 0))
            order.append(("strips", g, 0))
        for g in range(G):
            for i in range(NO):
                order.append(("pv", g, i))
                if g == 0 and G > 1 and i in (4, 14, 20):
                    order.append((("soft", "norm", "AT")[(4, 14, 20).index(i)], G - 1, 0))
            order.append(("gated", g, 0))
            order.append(("proj", g, 0))

        needs = {"yT": 1, "qkv": 4, "soft": nt, "AT": NS, "proj": 1}
        use, uses = {}, 0
        for ev, g, _ in order:
            for i in range(needs.get(ev, 0)):
                use[ev, g, i] = (uses % 2, uses // 2)
                uses += 1

        gready = [signal(f"gready{i}") for i in range(2)]
        gfree = [signal(f"gfree{i}") for i in range(2)]
        z_ready = signal("z_ready")
        yT_ready = signal("yT_ready")
        qkv_ready = signal("qkv_ready")
        prod_ready = signal("prod_ready")
        prod_used = signal("prod_used")
        SC_ready = signal("SC_ready")
        lg_ready = signal("lg_ready")
        e_ready = signal("e_ready")
        A_ready = signal("A_ready")
        AT_ready = signal("AT_ready")
        b_ready = signal("b_ready")
        av_ready = signal("av_ready")
        av_used = signal("av_used")
        og_ready = signal("og_ready")
        x_ready = signal("x_ready")
        out_ready = signal("out_ready")
        own = signal("own")
        numbers = range(gready[0].num, own.num + 1)
        stored = sems.take(f"{tag}_stored")
        clear = range(numbers[0], stored.num + 1)
        loaded = sems.take(f"{tag}_loaded")
        built = sems.take(f"{tag}_built")

        srcb = src.rearrange("(b t) c -> b t c", b=BATCH)
        dstb = dst.rearrange("(b t) c -> b t c", b=BATCH)
        loads = [(X[:, :, t, :], srcb[:, geo.start[t]:geo.start[t] + P, :].rearrange("b p c -> p b c"))
                 for t in range(nt)]
        loads += [(Wqkvg[:, 0:3, :], w["qkv"].rearrange("a (x b) -> a x b", x=3)), (Wqkvg[:, 3, :], w["gate"]),
                  (Wo[:, :], w["out"]), (cols[:, 0:5], w["cols"]), (bo[:, :], w["b_out"].to_broadcast([P, P])),
                  (se[:, :], w["scale_embed"]), (heads[:, :], w["heads"]), (spread[:, :, :], w["spread"]),
                  (pb[:, :, :], w["pb"]), (mask[:, :, :], w["mask"])]
        with nc.Block() as block:
            @block.sync
            def _(e):
                for to, fr in loads:
                    e.dma_start(to, fr).then_inc(loaded, 16)
                e.wait_ge(loaded, 16 * len(loads))

            @block.vector
            def _(e):
                e.memset(kpad[:, :, 0:PAD], 0.0)
                e.memset(vpad[:, :, 0:PAD], 0.0)
                e.memset(sm[:, :, :], 0.0)
                e.memset(sel[:, :, :], 0.0).then_inc(built, 1)
                e.wait_ge(loaded, 16 * len(loads))
                e.tensor_scalar(cols[:, 5:7], cols[:, 3:5], 0.5, None, ALU.mult)
                e.tensor_scalar(se[:, :], se[:, :], 1.0, HD ** -0.5, ALU.add, ALU.mult).then_inc(built, 1)
                e.tensor_tensor(eff[:, :], pb[:, :, 1], pb[:, :, 2], ALU.mult).then_inc(built, 1)
                e.wait_ge(built, 3)
                e.tensor_tensor(eff[:, :], eff[:, :], pb[:, :, 0], ALU.add)
                for i in range(NO):
                    at = (i % STRIP) * HEADS
                    e.tensor_scalar(sel[:, i, at:at + HEADS], heads[:, :], se[:, i:i + 1], None, ALU.mult)

        def one_round(block, r):
            def xb(g):
                return X[:, bass.ds(r * G + g, 1), :, :].rearrange("p o t c -> p (o t) c")

            def cut(i):
                return 0 if i % STRIP == 0 else OFF[i]

            def filled(e, key):
                b, k = use[key]
                e.wait_ge(gready[b], k + 1)
                return GB[b], gfree[b]

            @block.tensor
            def _(e):
                def bank_of(key):
                    b, k = use[key]
                    if k > 0:
                        e.wait_ge(gfree[b], k)
                    return GB[b], gready[b]

                def add_up(j):
                    g, i = divmod(j, NO)
                    e.wait_ge(av_ready, j + 1)
                    if i == 0:
                        if g > 0:
                            e.wait_ge(og_ready, g)
                    c = OFF[i]
                    e.matmul(AB[:, c:T], ident[:, :], AV[:, j % 3, c:T], start=(i == 0), stop=(i == NO - 1),
                             skip_group_check=True).then_inc(av_used, 1)

                for ev, g, i in order:
                    if ev == "yT":
                        e.wait_ge(z_ready, g + 1)
                        bank, done = bank_of((ev, g, 0))
                        for t in range(nt):
                            mm = e.transpose(bank[:, t * P:(t + 1) * P], Z[:, g, t, :], ident[:, :])
                        mm.then_inc(done, 1)
                    if ev == "qkv":
                        e.wait_ge(yT_ready, g + 1)
                        for x in range(4):
                            bank, done = bank_of((ev, g, x))
                            e.matmul(bank[:, 0:T], Wqkvg[:, x, :], yT[:, g, :], start=True, stop=True)\
                                .then_inc(done, 1)
                    if ev == "sc":
                        j = g * NO + i
                        e.wait_ge(prod_ready, j + 1)
                        if i == 0:
                            if g > 0:
                                e.wait_ge(SC_ready, g)
                        c = cut(i)
                        e.matmul(SB[i // STRIP][:, c:T], sel[:, i, :], PR[:, j % 4, c:T],
                                 start=(i % STRIP == 0), stop=(i % STRIP == STRIP - 1 or i == NO - 1),
                                 skip_group_check=True).then_inc(prod_used, 1)
                    if ev == "soft":
                        e.wait_ge(SC_ready, g + 1)
                        for t in range(nt):
                            bank, done = bank_of((ev, g, t))
                            for s in range(NS):
                                mm = e.transpose(bank[:, s * P:(s + 1) * P],
                                                 SC[:, s, geo.start[t]:geo.start[t] + P], ident[:, :])
                            mm.then_inc(done, 1)
                    if ev == "AT":
                        e.wait_ge(A_ready, g + 1)
                        for s in range(NS):
                            bank, done = bank_of((ev, g, s))
                            for t in range(nt):
                                mm = e.transpose(bank[:, t * P:(t + 1) * P], sm[:, t, s * P:(s + 1) * P],
                                                 ident[:, :])
                            mm.then_inc(done, 1)
                    if ev == "pv":
                        j = g * NO + i
                        if i == 0:
                            e.wait_ge(AT_ready, g + 1)
                        if j > 1:
                            e.wait_ge(av_ready, j - 1)
                        c = OFF[i]
                        e.matmul(BB[j % 2][:, c:T], spread[:, i % STRIP, :], AT[:, g, i // STRIP, c:T],
                                 start=True, stop=True).then_inc(b_ready, 1)
                        if i:
                            add_up(j - 1)
                    if ev == "gated":
                        add_up(g * NO + NO - 1)
                    if ev == "proj":
                        e.wait_ge(og_ready, g + 1)
                        bank, done = bank_of((ev, g, 0))
                        for t in range(nt):
                            mm = e.matmul(bank[:, t * P:(t + 1) * P], og[:, g, geo.start[t]:geo.start[t] + P],
                                          Wo[:, :], start=True, stop=True)
                        mm.then_inc(done, 1)

            @block.scalar
            def _(e):
                for ev, g, i in order:
                    if ev == "yT":
                        bank, free = filled(e, (ev, g, 0))
                        for t in range(nt):
                            o = geo.own[t]
                            a = e.activation(yT[:, g, geo.start[t] + o:geo.start[t] + P],
                                             bank[:, t * P + o:(t + 1) * P], ACT.Identity)
                        a.then_inc(yT_ready, 1)
                        e.wait_ge(yT_ready, g + 1)
                        e.sem_inc(free, 1)
                    if ev == "qkv":
                        for x in range(4):
                            bank, free = filled(e, (ev, g, x))
                            if x < 3:
                                to = (q[:, g, :], kpad[:, g, PAD:], vpad[:, g, PAD:])[x]
                                a = e.activation(to, bank[:, 0:T], ACT.Identity, bias=cols[:, x:x + 1])
                            else:
                                a = e.activation(gt[:, g, :], bank[:, 0:T], ACT.Tanh, scale=0.5,
                                                 bias=cols[:, 5:6])
                            a.then_inc(free, 1)
                        b, k = use[ev, g, 3]
                        e.wait_ge(gfree[b], k + 1)
                        e.sem_inc(qkv_ready, 1)
                    if ev == "strips":
                        e.wait_ge(prod_used, (g + 1) * NO)
                        if g:
                            b, k = use["soft", g - 1, nt - 1]
                            e.wait_ge(gready[b], k + 1)
                        for s in range(NS):
                            a = e.activation(SC[:, s, :], SB[s][:, 0:T], ACT.Identity, bias=eff[:, s:s + 1])
                        a.then_inc(SC_ready, 1)
                    if ev == "norm":
                        e.wait_ge(lg_ready, g + 1)
                        e.activation(sm[:, :, 0:KO], sm[:, :, 0:KO], ACT.Exp).then_inc(e_ready, 1)
                    if ev == "AT":
                        for s in range(NS):
                            bank, free = filled(e, (ev, g, s))
                            for t in range(nt):
                                o = geo.own[t]
                                a = e.activation(AT[:, g, s, geo.start[t] + o:geo.start[t] + P],
                                                 bank[:, t * P + o:(t + 1) * P], ACT.Identity)
                            a.then_inc(free, 1)
                        b, k = use[ev, g, NS - 1]
                        e.wait_ge(gfree[b], k + 1)
                        e.sem_inc(AT_ready, 1)

            @block.gpsimd
            def _(e):
                for g in range(G):
                    e.wait_ge(z_ready, g + 1)
                    e.tensor_tensor(out[:, g, :, :], xb(g), bo[:, :].unsqueeze(1).to_broadcast([P, nt, P]),
                                    ALU.add).then_inc(x_ready, 1)

            @block.vector
            def _(e):
                linked, _n = chain(e, own)
                sm4 = sm[:, :, 0:KO].rearrange("p t (o h) -> p t o h", h=HEADS)
                smh = sm[:, :, 0:KO].rearrange("p t (o h) -> p t h o", h=HEADS)
                for ev, g, i in order:
                    if ev == "ln" and g == 0:
                        for x in range(G):
                            for t in range(nt):
                                ins = e.bn_stats(st6[:, x, t, :], xb(x)[:, t, :])
                        linked(ins)
                        for x in range(G):
                            for t in range(nt):
                                ins = e.bn_aggr(mv[:, x, t, :], st6[:, x, t, :])
                        linked(ins)
                        linked(e.tensor_scalar(var[:, :], mv[:, :, :, 1].rearrange("p g t -> p (g t)"),
                                               EPS, None, ALU.add))
                        rsqrt(e, linked, var[:, :], rs[:, :], tmp[:, :])
                        for x in range(G):
                            for t in range(nt):
                                ins = e.tensor_scalar(Z[:, x, t, :], xb(x)[:, t, :], mv[:, x, t, 0:1],
                                                      rs[:, x * nt + t:x * nt + t + 1], ALU.subtract, ALU.mult)
                            ins.then_inc(z_ready, 1)
                    if ev == "sc":
                        j = g * NO + i
                        if i == 0:
                            e.wait_ge(qkv_ready, g + 1)
                        if j > 3:
                            e.wait_ge(prod_used, j - 3)
                        c = cut(i)
                        at = PAD - OFF[i]
                        e.tensor_tensor(PR[:, j % 4, c:T], q[:, g, c:T], kpad[:, g, at + c:at + T], ALU.mult)\
                            .then_inc(prod_ready, 1)
                    if ev == "soft":
                        if g > 0:
                            e.wait_ge(AT_ready, g)
                        for t in range(nt):
                            bank, free = filled(e, (ev, g, t))
                            e.tensor_tensor(sm4[:, t], bank[:, 0:KO].rearrange("p (o h) -> p o h", h=HEADS),
                                            mask[:, t, :].unsqueeze(2).to_broadcast([P, NO, HEADS]),
                                            ALU.add).then_inc(free, 1)
                        b, k = use[ev, g, nt - 1]
                        e.wait_ge(gfree[b], k + 1)
                        linked(e.tensor_reduce(big[:, :, :], smh, AX.X, ALU.max))
                        for t in range(nt):
                            ins = e.tensor_tensor(sm4[:, t], sm4[:, t],
                                                  big[:, t, :].unsqueeze(1).to_broadcast([P, NO, HEADS]),
                                                  ALU.subtract)
                        ins.then_inc(lg_ready, 1)
                    if ev == "norm":
                        e.wait_ge(e_ready, g + 1)
                        linked(e.tensor_reduce(tot[:, :, :], smh, AX.X, ALU.add))
                        linked(e.reciprocal(tot[:, :, :], tot[:, :, :]))
                        for t in range(nt):
                            ins = e.tensor_tensor(sm4[:, t], sm4[:, t],
                                                  tot[:, t, :].unsqueeze(1).to_broadcast([P, NO, HEADS]), ALU.mult)
                        ins.then_inc(A_ready, 1)
                    if ev == "pv":
                        j = g * NO + i
                        e.wait_ge(b_ready, j + 1)
                        if j > 2:
                            e.wait_ge(av_used, j - 2)
                        c = OFF[i]
                        at = PAD - c
                        e.tensor_tensor(AV[:, j % 3, c:T], BB[j % 2][:, c:T], vpad[:, g, at + c:at + T],
                                        ALU.mult).then_inc(av_ready, 1)
                    if ev == "gated":
                        linked(e.tensor_scalar(gt[:, g, :], gt[:, g, :], cols[:, 6:7], cols[:, 6:7],
                                               ALU.mult, ALU.add))
                        e.wait_ge(av_used, (g + 1) * NO)
                        e.tensor_tensor(og[:, g, :], AB[:, 0:T], gt[:, g, :], ALU.mult)\
                            .then_inc(og_ready, 1)
                    if ev == "proj":
                        e.wait_ge(x_ready, g + 1)
                        bank, free = filled(e, (ev, g, 0))
                        e.tensor_tensor(out[:, g, :, :], bank[:, 0:nt * P].rearrange("p (t c) -> p t c", c=P),
                                        out[:, g, :, :], ALU.add).then_inc(out_ready, 1)
                        e.wait_ge(out_ready, g + 1)
                        e.sem_inc(free, 1)

            @block.sync
            def _(e):
                for g in range(G):
                    e.wait_ge(out_ready, g + 1)
                    to = dstb[bass.ds(r * G + g, 1)].rearrange("o t c -> (o t) c")
                    e.dma_start(to[0:(nt - 1) * P, :].rearrange("(t p) c -> p t c", p=P),
                                out[:, g, 0:nt - 1, :]).then_inc(stored, 16)
                    e.dma_start(to[(nt - 1) * P:T, :], out[geo.own[-1]:P, g, nt - 1, :]).then_inc(stored, 16)
                e.wait_ge(stored, 32 * G)

        with nc.Fori(0, rounds) as r:
            with nc.Block(no_gpsimd_drain=True) as block:
                one_round(block, r)
            nc.all_engine_barrier(sems_to_clear=clear)
        sems.finish()


def embed_phase(nc, H, hA, w, ident, group=4):
    GRID, PX, CH = 14, 16, 3
    geo = Geometry(GRID * GRID + 1)
    nt, T = geo.tiles, geo.tokens
    K = CH * PX
    S, SEM = 77, 512
    NC = SEM // P
    G, rounds = group, BATCH // group

    with ExitStack() as ctx:
        sems = Semaphores(nc, ctx)

        def sb(name, shape, dt=F32):
            return ctx.enter_context(nc.sbuf_tensor(f"emb_{name}", shape, dt))

        def signal(name):
            return sems.take(f"emb_{name}")

        CW = sb("CW", [K, PX, P])
        cols = sb("cols", [P, 2])
        pos = sb("pos", [P, nt, P])
        WT = sb("WT", [P, NC, P])
        idx = sb("idx", [S, BATCH], I32)
        low = sb("low", [S, BATCH], I32)
        idg = sb("idg", [S, G], I32)
        XI = sb("XI", [K, G, GRID, GRID * PX])
        ET = sb("ET", [P, G, T])
        TX = sb("TX", [S, G, SEM])
        TXT = sb("TXT", [P, G, NC, S])
        sums = sb("sums", [S, G])
        TO = sb("TO", [S, G, P])
        banks = [ctx.enter_context(nc.psum_tensor(f"emb_ps{i}", [P, 512], F32)) for i in range(8)]
        EB, TB, XB, YB = banks[0:2], banks[2:4], banks[4:6], banks[6:8]

        arrived = [signal(f"arrived{g}") for g in range(G)]
        gathered = [signal(f"gathered{g}") for g in range(G)]
        emb_filled = signal("emb_filled")
        ET_ready = signal("ET_ready")
        tb_filled = signal("tb_filled")
        h_ready = signal("h_ready")
        id_ready = signal("id_ready")
        sum_ready = signal("sum_ready")
        xb_filled = signal("xb_filled")
        TXT_ready = signal("TXT_ready")
        yb_filled = signal("yb_filled")
        TO_ready = signal("TO_ready")
        own = signal("own")
        stored = sems.take("emb_stored")
        clear = range(arrived[0].num, stored.num + 1)
        loaded = sems.take("emb_loaded")
        set_up = sems.take("emb_set_up")

        rowsA = hA.rearrange("(b t) c -> b t c", b=BATCH)
        loads = [(CW[:, :, :], w["conv"].rearrange("(k x) d -> k x d", x=PX)), (cols[:, :], w["cols"]),
                 (WT[:, :, :], w["W"].rearrange("(k p) d -> p k d", p=P)), (idx[:, :], w["idx"])]
        loads += [(pos[:, t, :], w["pos"][geo.start[t]:geo.start[t] + P, :]) for t in range(nt)]
        with nc.Block() as block:
            @block.sync
            def _(e):
                for to, fr in loads:
                    e.dma_start(to, fr).then_inc(loaded, 16)
                e.wait_ge(loaded, 16 * len(loads))

            @block.vector
            def _(e):
                e.wait_ge(loaded, 16 * len(loads))
                e.tensor_scalar(low[:, :], idx[:, :], 0.0, float(w["vocab"]), ALU.is_lt, ALU.mult)\
                    .then_inc(set_up, 1)
                e.wait_ge(set_up, 1)
                e.tensor_tensor(idx[:, :], idx[:, :], low[:, :], ALU.add).then_inc(set_up, 1)
                e.wait_ge(set_up, 2)
                e.tensor_scalar(idx[:, :], idx[:, :], 0.0, float(w["vocab"] - 1), ALU.max, ALU.min)

        def one_round(block, r):
            order = []
            for i in range(G + 2):
                if i < G:
                    order.append(("emb", i))
                    order.append(("txt", i))
                if 1 <= i <= G:
                    order.append(("turn", i - 1))
                    order.append(("prod", i - 1))

            @block.sync
            def _(e):
                for g in range(G):
                    for c in range(CH):
                        src = w["x"][bass.ds(r * G + g, 1), c].rearrange("o (a p) x -> p (o a) x", p=PX)
                        e.dma_start(XI[c * PX:(c + 1) * PX, g, :, :], src).then_inc(arrived[g], 16)
                for g in range(G):
                    e.wait_ge(TO_ready, g + 1)
                    e.dma_start(rowsA[bass.ds(r * G + g, 1), T:T + S, :].rearrange("o t c -> (o t) c"),
                                TO[:, g, :]).then_inc(stored, 16)
                e.wait_ge(stored, 16 * G)

            @block.gpsimd
            def _(e):
                e.wait_ge(id_ready, 1)
                for g in range(G):
                    e.indirect_dma_start(TX[:, g, :], None, w["table"],
                                         bass.IndirectOffsetOnAxis(ap=idg[:, g:g + 1], axis=0))\
                        .then_inc(gathered[g], 16)
                for g in range(G):
                    e.wait_ge(gathered[g], 16)
                e.dma_reset(range(gathered[0].num, gathered[-1].num + 1))

            @block.tensor
            def _(e):
                for ev, g in order:
                    if ev == "emb":
                        e.wait_ge(arrived[g], 16 * CH)
                        if g > 1:
                            e.wait_ge(ET_ready, g - 1)
                        for x in range(PX):
                            mm = e.matmul(EB[g % 2][:, 0:T - 1], CW[:, x, :],
                                          XI[:, g, :, :].rearrange("k a (b x) -> k a b x", x=PX)[:, :, :, x],
                                          start=(x == 0), stop=(x == PX - 1))
                        mm.then_inc(emb_filled, 1)
                    if ev == "txt":
                        e.wait_ge(gathered[g], 16)
                        if g > 1:
                            e.wait_ge(TXT_ready, g - 1)
                        for c in range(NC):
                            mm = e.transpose(XB[g % 2][:, c * S:(c + 1) * S], TX[:, g, c * P:(c + 1) * P],
                                             ident[0:S, 0:S])
                        mm.then_inc(xb_filled, 1)
                    if ev == "turn":
                        e.wait_ge(ET_ready, g + 1)
                        if g > 1:
                            e.wait_ge(h_ready, g - 1)
                        for t in range(nt):
                            mm = e.transpose(TB[g % 2][:, t * P:(t + 1) * P],
                                             ET[:, g, geo.start[t]:geo.start[t] + P], ident[:, :])
                        mm.then_inc(tb_filled, 1)
                    if ev == "prod":
                        e.wait_ge(TXT_ready, g + 1)
                        if g > 1:
                            e.wait_ge(TO_ready, g - 1)
                        for c in range(NC):
                            mm = e.matmul(YB[g % 2][0:S, 0:P], TXT[:, g, c, :], WT[:, c, :],
                                          start=(c == 0), stop=(c == NC - 1))
                        mm.then_inc(yb_filled, 1)

            @block.scalar
            def _(e):
                for ev, g in order:
                    if ev == "emb":
                        e.wait_ge(emb_filled, g + 1)
                        e.activation(ET[:, g, 0:1], cols[:, 1:2], ACT.Identity)
                        e.activation(ET[:, g, 1:T], EB[g % 2][:, 0:T - 1], ACT.Identity, bias=cols[:, 0:1])\
                            .then_inc(ET_ready, 1)
                    if ev == "txt":
                        e.wait_ge(xb_filled, g + 1)
                        e.activation(TXT[:, g, :, :].rearrange("p c s -> p (c s)"), XB[g % 2][:, 0:NC * S],
                                     ACT.Identity).then_inc(TXT_ready, 1)
                    if ev == "prod":
                        e.wait_ge(yb_filled, g + 1)
                        e.wait_ge(sum_ready, g + 1)
                        e.activation(TO[:, g, :], YB[g % 2][0:S, 0:P], ACT.Identity, scale=sums[:, g:g + 1])\
                            .then_inc(TO_ready, 1)

            @block.vector
            def _(e):
                linked, _n = chain(e, own)
                e.tensor_copy(idg[:, :], idx[:, bass.ds(r * G, G)]).then_inc(id_ready, 1)
                for ev, g in order:
                    if ev == "txt":
                        e.wait_ge(gathered[g], 16)
                        linked(e.tensor_reduce(sums[:, g:g + 1], TX[:, g, :], AX.X, ALU.add))
                        linked(e.tensor_scalar(sums[:, g:g + 1], sums[:, g:g + 1], 1e-6, P ** -0.5,
                                               ALU.add, ALU.mult))
                        e.reciprocal(sums[:, g:g + 1], sums[:, g:g + 1]).then_inc(sum_ready, 1)
                    if ev == "turn":
                        e.wait_ge(tb_filled, g + 1)
                        h = H[:, bass.ds(r * G + g, 1), :, :].rearrange("p o t c -> p (o t) c")
                        e.tensor_tensor(h, TB[g % 2][:, 0:nt * P].rearrange("p (t c) -> p t c", c=P),
                                        pos[:, :, :], ALU.add).then_inc(h_ready, 1)

        with nc.Fori(0, rounds) as r:
            with nc.Block() as block:
                one_round(block, r)
            nc.all_engine_barrier(sems_to_clear=clear)
        sems.finish()


def final_norm_phase(nc, H, hA, wb, group=4):
    geo = Geometry(197)
    nt, T, G, rounds = geo.tiles, geo.tokens, group, BATCH // group
    with ExitStack() as ctx:
        sems = Semaphores(nc, ctx)

        def sb(name, shape):
            return ctx.enter_context(nc.sbuf_tensor(f"fin_{name}", shape, F32))

        W = sb("W", [P, 2, P])
        N = sb("N", [P, G, nt, P])
        st6 = sb("st6", [P, G, nt, 6])
        mv = sb("mv", [P, G, nt, 2])
        var, rs, tmp = (sb(x, [P, G * nt]) for x in ("var", "rs", "tmp"))
        n_ready = sems.take("fin_n_ready")
        out_ready = sems.take("fin_out_ready")
        own = sems.take("fin_own")
        stored = sems.take("fin_stored")
        loaded = sems.take("fin_loaded")
        rowsA = hA.rearrange("(b t) c -> b t c", b=BATCH)
        with nc.Block() as block:
            @block.sync
            def _(e):
                e.dma_start(W[:, :, :], wb.rearrange("(o a) b -> o (a b)", o=1).to_broadcast([P, 2 * P]))\
                    .then_inc(loaded, 16)
                e.wait_ge(loaded, 16)
        with nc.Fori(0, rounds) as r:
            with nc.Block(no_gpsimd_drain=True) as block:
                @block.vector
                def _(e):
                    linked, _n = chain(e, own)

                    def h(g):
                        return H[:, bass.ds(r * G + g, 1), :, :].rearrange("p o t c -> p (o t) c")

                    for g in range(G):
                        for t in range(nt):
                            ins = e.bn_stats(st6[:, g, t, :], h(g)[:, t, :])
                    linked(ins)
                    for g in range(G):
                        for t in range(nt):
                            ins = e.bn_aggr(mv[:, g, t, :], st6[:, g, t, :])
                    linked(ins)
                    linked(e.tensor_scalar(var[:, :], mv[:, :, :, 1].rearrange("p g t -> p (g t)"), EPS, None,
                                           ALU.add))
                    rsqrt(e, linked, var[:, :], rs[:, :], tmp[:, :])
                    for g in range(G):
                        for t in range(nt):
                            ins = e.tensor_scalar(N[:, g, t, :], h(g)[:, t, :], mv[:, g, t, 0:1],
                                                  rs[:, g * nt + t:g * nt + t + 1], ALU.subtract, ALU.mult)
                        linked(ins)
                        e.tensor_tensor(N[:, g, :, :], N[:, g, :, :],
                                        W[:, 0:1, :].to_broadcast([P, nt, P]), ALU.mult).then_inc(n_ready, 1)

                @block.gpsimd
                def _(e):
                    for g in range(G):
                        e.wait_ge(n_ready, g + 1)
                        e.tensor_tensor(N[:, g, :, :], N[:, g, :, :], W[:, 1:2, :].to_broadcast([P, nt, P]),
                                        ALU.add).then_inc(out_ready, 1)

                @block.sync
                def _(e):
                    for g in range(G):
                        e.wait_ge(out_ready, g + 1)
                        to = rowsA[bass.ds(r * G + g, 1)].rearrange("o t c -> (o t) c")
                        e.dma_start(to[0:P, :], N[:, g, 0, :]).then_inc(stored, 16)
                        e.dma_start(to[P:T, :], N[geo.own[1]:P, g, 1, :]).then_inc(stored, 16)
                    e.wait_ge(stored, 32 * G)
            nc.all_engine_barrier(sems_to_clear=range(n_ready.num, stored.num + 1))
        sems.finish()


def move_phase(nc, tag, H, geo, rows, store):
    with ExitStack() as ctx:
        sems = Semaphores(nc, ctx)
        moved = sems.take(f"{tag}_moved")
        r = rows.rearrange("(b t) c -> b t c", b=BATCH)
        with nc.Block() as block:
            @block.sync
            def _(e):
                for t in range(geo.tiles):
                    s, o = geo.start[t], geo.own[t] if store else 0
                    out = r[:, s + o:s + P, :].rearrange("b p c -> p b c")
                    sb = H[o:P, :, t, :]
                    e.dma_start(*((out, sb) if store else (sb, out))).then_inc(moved, 16)
                e.wait_ge(moved, 16 * geo.tiles)
        sems.finish()


IMAGE, TEXT = 197, 77
TOKENS = IMAGE + TEXT


def build(nc, d, out):
    hA, hB, hC, hD = (nc.dram_tensor(f"h{x}", (BATCH * TOKENS, P), F32).ap() for x in "ABCD")
    flat = out.rearrange("b t c -> (b t) c")
    with ExitStack() as ctx:
        ident = ctx.enter_context(nc.sbuf_tensor("ident", [P, P], F32))
        identb = ctx.enter_context(nc.sbuf_tensor("identb", [P, P], BF16))
        ident_in = ctx.enter_context(nc.semaphore("ident_in"))
        with nc.Block() as block:
            @block.sync
            def _(e):
                e.dma_start(ident[:, :], d["ident"]).then_inc(ident_in, 16)

            @block.vector
            def _(e):
                e.wait_ge(ident_in, 16)
                e.tensor_copy(identb[:, :], ident[:, :])

        with nc.sbuf_tensor("H", [P, BATCH, 2, P], F32) as H:
            embed_phase(nc, H, hA, dict(conv=d["conv_w"], cols=d["emb_cols"], pos=d["pos"], W=d["txt_W"],
                                        idx=d["idx"], table=d["table"], vocab=d["table"].shape[0],
                                        x=d["x"]), ident)
            attention_phase(nc, "vit", H, IMAGE, 4, 4,
                            dict(qkv=d["vit_qkv"], proj=d["vit_proj"], cols=d["vit_cols"], rows=d["vit_rows"],
                                 fc1=d["vit_fc1"], fc2=d["vit_fc2"]), ident, identb, dict(mask=d["mask_image"]), None)
            final_norm_phase(nc, H, hA, d["norm_wb"])
        with nc.sbuf_tensor("H3", [P, BATCH, 3, P], F32) as H:
            move_phase(nc, "in0", H, Geometry(TOKENS), hA, False)
            attention_phase(nc, "att", H, TOKENS, 2, 1,
                            dict(qkv=d["att_qkv"], proj=d["att_proj"], cols=d["att_cols"], rows=d["att_rows"]),
                            ident, identb, dict(mask=d["mask_all"]), None)
            move_phase(nc, "out0", H, Geometry(TOKENS), hB, True)
        ffn_phase(nc, "moe0", hB, hC, dict(experts=16, chunks=4, act=ACT.Silu, inner=True, shared=2,
                                           shared_scale=0.25, ff_chunks=4, temperature=0.7),
                  {k[5:]: v for k, v in d.items() if k.startswith("moe0_")}, ident)
        dilated_phase(nc, "dil", hC, hD, {**{k[4:]: v for k, v in d.items() if k.startswith("dil_")},
                                          "tokens": TOKENS}, ident)
        ffn_phase(nc, "moe1", hD, flat, dict(experts=8, chunks=2, act=ACT.Gelu_apprx_tanh, inner=False,
                                             temperature=1.0),
                  {k[5:]: v for k, v in d.items() if k.startswith("moe1_")}, ident)


def kernel(**inputs):
    import numpy as np
    import concourse.bacc as bacc
    from concourse.bass_utils import run_bass_kernel_spmd

    a = {k: np.asarray(v) for k, v in inputs.items()}
    t0, t1, m0, m1 = "L0_tok_", "L1_attn_", "L0_ffn_", "L1_ffn_"
    zero, one = np.zeros(P, np.float32), np.ones(P, np.float32)

    def columns(v):
        return v.reshape(-1, P).T

    def keys_mask(tokens):
        geo = Geometry(tokens)
        m = np.ones((P, geo.tiles), np.float32)
        m[:geo.own[-1], -1] = 0.0
        return m

    OFF = offsets_of(TOKENS)
    NO, STRIP = len(OFF), P // HEADS
    NS = -(-NO // STRIP)
    geo = Geometry(TOKENS)
    log_max = math.log(1.0 + 4096.0)
    omega = [x * math.pi / log_max for x in (0, 0, 1, 1, 4, 4, 6, 6)]
    cosine = np.array([[math.cos(om * math.log(1.0 + o)) if om > 0 else 0.0 for om in omega] for o in OFF],
                      np.float32)
    pb = np.zeros((3, NS * STRIP, HEADS), np.float32)
    pb[0, :NO] = a[t1 + "pos_bias"][:NO]
    pb[1, :NO] = cosine
    pb[2, :NO] = np.broadcast_to(a[t1 + "disp_amp"], (NO, HEADS))
    token = np.array([[geo.start[t] + p for t in range(geo.tiles)] for p in range(P)])
    far = np.where(token[:, :, None] >= np.array(OFF), 0.0, -1e30).astype(np.float32)
    spread = np.zeros((P, STRIP, P), np.float32)
    for i in range(STRIP):
        for h in range(HEADS):
            spread[i * HEADS + h, i, h * HD:(h + 1) * HD] = 1.0

    layers = range(4)
    d = {
        "ident": np.eye(P, dtype=np.float32),
        "x": a["x"], "idx": a["x_txt"].T, "table": a["L0_txt_word2sememe"], "txt_W": a["L0_txt_W"],
        "conv_w": a[t0 + "conv_w"], "emb_cols": np.stack([a[t0 + "conv_b"], a[t0 + "cls_token"][0, 0]], -1),
        "pos": a[t0 + "pos_embed"][0],
        "vit_qkv": a[t0 + "qkv_w"], "vit_proj": a[t0 + "proj_w"], "vit_fc1": a[t0 + "fc1_w"],
        "vit_fc2": a[t0 + "fc2_w"],
        "vit_cols": np.stack([np.stack([a[t0 + "qkv_b"][l, :P], a[t0 + "qkv_b"][l, P:2 * P], a[t0 + "ln1_w"][l],
                                        a[t0 + "ln1_b"][l], a[t0 + "ln2_w"][l], a[t0 + "ln2_b"][l],
                                        a[t0 + "fc1_b"][l, :P], a[t0 + "fc1_b"][l, P:]], -1) for l in layers]),
        "vit_rows": np.stack([np.stack([a[t0 + "qkv_b"][l, 2 * P:], a[t0 + "proj_b"][l], a[t0 + "fc2_b"][l]])
                              for l in layers]),
        "mask_image": keys_mask(IMAGE), "mask_all": keys_mask(TOKENS),
        "norm_wb": np.stack([a[t0 + "norm_w"], a[t0 + "norm_b"]]),
        "att_qkv": a["L0_attn_w_qkv"].T[None], "att_proj": a["L0_attn_w_agg"].T[None],
        "att_cols": np.stack([zero, zero, one, zero, one, zero, zero, zero], -1)[None],
        "att_rows": np.stack([zero, a["L0_attn_b_agg"], zero])[None],
        "moe0_w1": np.concatenate([*a[m0 + "ew1"], a[m0 + "sw1"]], 1),
        "moe0_w2": np.concatenate([*a[m0 + "ew2"], a[m0 + "sw2"]], 0),
        "moe0_b1": columns(np.concatenate([a[m0 + "eb1"].reshape(-1), a[m0 + "sb1"]])),
        "moe0_b2": np.concatenate([a[m0 + "eb2"], a[m0 + "sb2"][None]]),
        "moe0_router": a[m0 + "router_w"], "moe0_router_b": a[m0 + "router_b"][None],
        "moe0_number": np.arange(16, dtype=np.float32)[None],
        "moe0_cols": np.stack([a[m0 + "ln_in_g"], a[m0 + "ln_in_b"], a[m0 + "ff_ln_g"], a[m0 + "ff_ln_b"]], -1),
        "moe0_f1": a[m0 + "ff_w1"], "moe0_f2": a[m0 + "ff_w2"], "moe0_fb1": columns(a[m0 + "ff_b1"]),
        "moe0_fb2": a[m0 + "ff_b2"][None],
        "dil_qkv": a[t1 + "W_qkv"], "dil_gate": a[t1 + "W_gate"], "dil_out": a[t1 + "W_out"],
        "dil_cols": np.stack([*a[t1 + "b_qkv"].reshape(3, P), a[t1 + "b_gate"], np.repeat(a[t1 + "if_gain"], HD)], -1),
        "dil_b_out": a[t1 + "b_out"][None],
        "dil_scale_embed": np.tile(a[t1 + "scale_embed"][:NO].T, (HEADS, 1)),
        "dil_heads": np.repeat(np.eye(HEADS, dtype=np.float32), HD, axis=0), "dil_spread": spread,
        "dil_pb": pb.reshape(3, NS, P).transpose(2, 1, 0), "dil_mask": far,
        "moe1_w1": np.concatenate([*a[m1 + "W1"]], 1), "moe1_w2": np.concatenate([*a[m1 + "W2"]], 0),
        "moe1_b1": columns(a[m1 + "b1"].reshape(-1)), "moe1_b2": a[m1 + "b2"],
        "moe1_router": a[m1 + "Wg"], "moe1_router_b": np.zeros((1, 8), np.float32),
        "moe1_number": np.arange(8, dtype=np.float32)[None],
        "moe1_cols": np.stack([one, zero, one, zero], -1),
    }
    nc = bacc.Bacc("TRN2", target_bir_lowering=False, num_devices=1)
    arrays, aps = {}, {}
    for name, v in d.items():
        v = np.ascontiguousarray(v)
        arrays[f"in_{name}"] = v
        aps[name] = nc.dram_tensor(f"in_{name}", v.shape, mybir.dt.from_np(v.dtype), kind="ExternalInput").ap()
    out = nc.dram_tensor("out_dram", (BATCH, TOKENS, P), F32, kind="ExternalOutput").ap()
    build(nc, aps, out)
    r = run_bass_kernel_spmd(nc, [arrays], core_ids=[0])
    return r.results[0]["out_dram"]
```

```python
import math
from contextlib import ExitStack

import concourse.bass as bass
from concourse import mybir

F32 = mybir.dt.float32
BF16 = mybir.dt.bfloat16
I32 = mybir.dt.int32
ACT = mybir.ActivationFunctionType
ALU = mybir.AluOpType
AX = mybir.AxisListType

P = 128
BATCH = 32
HEADS, HD = 8, 16
SLOT = 32
EPS = 1e-5
LN_LINKS = 13
RSQRT_MAGIC = float(0x5F3759DF)


class Semaphores:

    FIRST = 110

    def __init__(self, nc, ctx):
        self.nc, self.ctx, self.next = nc, ctx, self.FIRST

    def take(self, name):
        self.next += 1
        return self.ctx.enter_context(self.nc.semaphore(name, num=self.next - 1))

    def finish(self):
        self.nc.all_engine_barrier(sems_to_clear=range(self.FIRST, self.next))


class Geometry:

    def __init__(self, tokens):
        self.tokens = tokens
        self.tiles = -(-tokens // P)
        self.start = [t * P for t in range(self.tiles - 1)] + [tokens - P]
        self.own = [0] * (self.tiles - 1) + [P - (tokens - (self.tiles - 1) * P)]


def rsqrt(e, linked, v, y, s):
    linked(e.tensor_scalar(y.bitcast(I32), v.bitcast(I32), -0.5, RSQRT_MAGIC, ALU.mult, ALU.add))
    for _ in range(3):
        linked(e.tensor_tensor(s, y, y, ALU.mult))
        linked(e.scalar_tensor_tensor(s, s, -0.5, v, ALU.mult, ALU.mult))
        linked(e.scalar_tensor_tensor(y, s, 1.5, y, ALU.add, ALU.mult))


def chain(e, sig):
    count = [0]

    def linked(ins):
        count[0] += 1
        ins.then_inc(sig, 1)
        e.wait_ge(sig, count[0])

    return linked, count


def attention_phase(nc, tag, H, tokens, group, layers, w, ident, identb, mask_in):
    geo = Geometry(tokens)
    T, nt = tokens, geo.tiles
    G, rounds = group, BATCH // group
    N = layers * rounds
    mlp = "fc1" in w
    wide = nt * T <= 512
    jobs = [(h, list(range(nt))) for h in range(HEADS)] if wide else \
        [(h, [t]) for h in range(HEADS) for t in range(nt)]
    Jb = len(jobs)
    J = G * Jb
    JW = (nt if wide else 1) * T
    PV_LAG = 2 if wide else 3
    FIRST_S, PER_G = (18, 10) if wide else (32, 26)

    def order_of(stages):
        tick = [[] for _ in range(J + FIRST_S + PER_G * G + 40)]
        b_end = J if "B" in stages else 0
        if "A" in stages:
            lead = FIRST_S - (10 if wide else 18) if "B" in stages else 0
            for g in range(G):
                at = lead + g * (3 if wide else 6)
                tick[at].append(("yT", g, 0))
                tick[at + 1].append(("qk", g, 0))
                tick[at + 2].append(("v", g, 0))
                tick[at + 5].append(("split", g, 0))
                for j in range(Jb):
                    tick[FIRST_S + g * PER_G + j].append(("s", g, g * Jb + j))
                tick[FIRST_S + g * PER_G + Jb + 2].append(("m", g, 0))
        if "B" in stages:
            for j in range(J):
                tick[j].append(("st", j // Jb, j))
                tick[j + PV_LAG].append(("pv", j // Jb, j))
            for g in range(G):
                end = (g + 1) * Jb + PV_LAG
                tick[end - 1].append(("os", g, 0))
                tick[end + 1].append(("o", g, 0))
                tick[end + 4].append(("oT", g, 0))
                tick[end + 6].append(("proj", g, 0))
        if "C" in stages:
            for g in range(G):
                at = max(b_end, 4) + 1 + 4 * g
                tick[at - 5].append(("z2", g, 0))
                tick[at].append(("y2T", g, 0))
                tick[at + 2].append(("fc1", g, 0))
                tick[at + 7].append(("fc2", g, 0))
        order = [("ln", 0, 0)] if stages != "B" else []
        for t in tick:
            order += t
        return order

    needs = {"yT": 1, "qk": 2, "v": 1, "m": 1, "o": 2, "oT": 1, "proj": 1, "y2T": 1, "fc1": 2, "fc2": 1}

    with ExitStack() as ctx:
        sems = Semaphores(nc, ctx)

        def sb(name, shape, dt=F32):
            return ctx.enter_context(nc.sbuf_tensor(f"{tag}_{name}", shape, dt))

        def signal(name):
            return sems.take(f"{tag}_{name}")

        Wqk = sb("Wqk", [P, 2, 2 * P])
        Wv = sb("Wv", [P, 2, P])
        bvm = sb("bvm", [P, 2, nt, P])
        colsA = sb("colsA", [P, 2, 8])
        rowp = sb("rowp", [P, 2, P])
        Wp = sb("Wp", [P, 2, P])
        if mlp:
            W1 = sb("W1", [P, 2, 2 * P])
            W2 = sb("W2", [P, 2, 2, P])
            colsC = sb("colsC", [P, 2, 8])
            rowf = sb("rowf", [P, 2, P])
        mask = sb("mask", [P, nt])
        Z = sb("Z", [P, G, nt, P])
        yT = sb("yT", [P, G, T])
        qk32 = sb("qk32", [P, G, 2, T])
        rest = sb("rest", [P, G, 2, T])
        parts = sb("parts", [P, G, 3, 2, T], BF16)
        Mx = sb("Mx", [P, G, nt, HEADS])
        Mr = sb("Mr", [P, G, nt, HEADS])
        Mp = sb("Mp", [P, G, nt, 3, HEADS], BF16)
        MT = sb("MT", [3 * HEADS, G, T], BF16)
        QS = sb("QS", [P, 2, G, HEADS, T], BF16)
        KS = sb("KS", [P, 2, G, HEADS, T], BF16)
        VA = sb("VA", [P, 2, G, nt, HEADS, SLOT])
        PR = sb("PR", [P, 4, JW])
        OS = sb("OS", [P, 2, T])
        RD = sb("RD", [P, 2, nt, 4])
        ON = sb("ON", [P, G, nt, P])
        OT = sb("OT", [P, G, nt, P])
        if mlp:
            Z2 = sb("Z2", [P, 2, nt, P])
            y2T = sb("y2T", [P, 2, T])
            hid = sb("hid", [P, 2, 2, T])
        K2 = (2 if mlp else 1) * G * nt
        st6 = sb("st6", [P, K2, 6])
        mv = sb("mv", [P, K2, 2])
        var = sb("var", [P, K2])
        rs = sb("rs", [P, K2])
        tmp = sb("tmp", [P, K2])
        banks = [ctx.enter_context(nc.psum_tensor(f"{tag}_ps{i}", [P, 512], F32)) for i in range(8)]
        S, ST, OB, GB = banks[0:2], banks[2:4], banks[4:6], banks[6:8]
        scr = nc.dram_tensor(f"{tag}_scr", (G, 2, HEADS, 3 * HD, T), BF16).ap()

        gready = [signal(f"gready{i}") for i in range(2)]
        gfree = [signal(f"gfree{i}") for i in range(2)]
        z_ready = signal("z_ready")
        z2_ready = signal("z2_ready")
        yT_ready = signal("yT_ready")
        y2T_ready = signal("y2T_ready")
        qk_ready = signal("qk_ready")
        split1 = signal("split1")
        split2 = signal("split2")
        split3 = signal("split3")
        parts_ready = signal("parts_ready")
        spilled = [signal(f"spilled{g}") for g in range(G)]
        stacked = [signal(f"stacked{g}") for g in range(G)]
        v_ready = signal("v_ready")
        s_ready = signal("s_ready")
        s_maxed = signal("s_maxed")
        mp_ready = signal("mp_ready")
        mT_ready = signal("mT_ready")
        m_stacked = signal("m_stacked")
        st_ready = signal("st_ready")
        p_ready = signal("p_ready")
        pv_done = signal("pv_done")
        os_ready = signal("os_ready")
        o_turned = signal("o_turned")
        on_ready = signal("on_ready")
        oT_ready = signal("oT_ready")
        h_biased = signal("h_biased")
        h_attn = signal("h_attn")
        h2_biased = signal("h2_biased")
        h_done = signal("h_done")
        hid_ready = signal("hid_ready")
        fc2_done = signal("fc2_done")
        own = signal("own")
        weights_in = signal("weights_in")
        numbers = range(gready[0].num, weights_in.num + 1)
        ready = sems.take(f"{tag}_ready")

        def group_of(r):
            return H[:, bass.ds(r * G, G), :, :]

        def weight_loads(to, stages, layers_of):
            def one(name, stage):
                return w[name][bass.ds(layers_of[stage], 1)]

            loads = []
            if "A" in stages:
                loads += [(Wqk[:, to, :], one("qkv", "A")[:, :, 0:2 * P].rearrange("o a b -> (o a) b")),
                          (Wv[:, to, :], one("qkv", "A")[:, :, 2 * P:3 * P].rearrange("o a b -> (o a) b")),
                          (bvm[:, to, :, :], one("bvm", "A").rearrange("o p t c -> (o p) t c")),
                          (colsA[:, to, :], one("cols", "A").rearrange("o a b -> (o a) b")),
                          (rowp[:, to, :], one("rows", "A")[:, 0, :].to_broadcast([P, P]))]
            if "B" in stages:
                loads += [(Wp[:, to, :], one("proj", "B").rearrange("o a b -> (o a) b"))]
            if "C" in stages:
                loads += [(W1[:, to, :], one("fc1", "C").rearrange("o a b -> (o a) b")),
                          (W2[:, to, :, :], one("fc2", "C").rearrange("o (c a) b -> (o a) c b", a=P)),
                          (colsC[:, to, :], one("cols", "C").rearrange("o a b -> (o a) b")),
                          (rowf[:, to, :], one("rows", "C")[:, 1, :].to_broadcast([P, P]))]
            return loads

        first = weight_loads(0, "A", {"A": 0})
        with nc.Block() as block:
            @block.vector
            def _(e):
                e.memset(KS[96:128, :, :, :, :], -1.0)
                e.memset(VA[:, :, :, :, :, :], 0.0)

            @block.sync
            def _(e):
                e.dma_start(mask[:, :], mask_in).then_inc(ready, 16)
                for dst, src in first:
                    e.dma_start(dst, src).then_inc(ready, 16)
                e.wait_ge(ready, 16 * (1 + len(first)))
        with nc.Block() as block:
            @block.vector
            def _(e):
                for b in range(2):
                    for t in range(nt):
                        e.tensor_copy(VA[:, b, :, t, :, HD],
                                      mask[:, t:t + 1].unsqueeze(2).to_broadcast([P, G, HEADS]))

        def one_round(block, stages, q, groups, upcoming, layers_of):
            order = order_of(stages)
            use, uses = {}, 0
            for ev, g, _ in order:
                for i in range(needs.get(ev, 0)):
                    use[ev, g, i] = (uses % 2, uses // 2)
                    uses += 1
            qb = 1 - q

            @block.sync
            def _(e):
                loads = weight_loads(1 - q, upcoming, layers_of)
                for dst, src in loads:
                    e.dma_start(dst, src).then_inc(weights_in, 16)
                for ev, g, j in order:
                    if ev == "split":
                        e.wait_ge(parts_ready, g + 1)
                        for p in range(3):
                            for x in range(2):
                                slot = p if x == 0 else 2 - p
                                e.dma_start(scr[g, x, :, slot * HD:(slot + 1) * HD, :],
                                            parts[:, g, p, x, :]).then_inc(spilled[g], 16)
                        e.wait_ge(spilled[g], 96)
                        for x, dst in ((0, QS), (1, KS)):
                            for row, at, length in ((0, 0, 48), (48, 0 if x == 0 else 16, 32),
                                                    (80, 0 if x == 0 else 32, 16)):
                                e.dma_start(dst[row:row + length, q, g, :, :],
                                            scr[g, x, :, at:at + length, :].rearrange("h r t -> r h t"))\
                                    .then_inc(stacked[g], 16)
                    if ev == "m":
                        e.wait_ge(mT_ready, g + 1)
                        for p in range(3):
                            e.dma_start(QS[96 + p:97 + p, q, g, :, :], MT[p * HEADS:(p + 1) * HEADS, g, :])\
                                .then_inc(m_stacked, 16)
                if "A" in stages:
                    e.wait_ge(m_stacked, 48 * G)
                if loads:
                    e.wait_ge(weights_in, 16 * len(loads))

            def bank_of(e, key):
                b, k = use[key]
                if k > 0:
                    e.wait_ge(gfree[b], k)
                return GB[b], gready[b]

            def filled(e, key):
                b, k = use[key]
                e.wait_ge(gready[b], k + 1)
                return GB[b], gfree[b]

            @block.tensor
            def _(e):
                for ev, g, j in order:
                    if ev in ("yT", "y2T"):
                        s, z = (z_ready, Z[:, g, :, :]) if ev == "yT" else (z2_ready, Z2[:, g % 2, :, :])
                        e.wait_ge(s, g + 1)
                        bank, done = bank_of(e, (ev, g, 0))
                        for t in range(nt):
                            mm = e.transpose(bank[:, t * P:(t + 1) * P], z[:, t, :], ident[:, :])
                        mm.then_inc(done, 1)
                    if ev == "qk":
                        e.wait_ge(yT_ready, g + 1)
                        for x in range(2):
                            bank, done = bank_of(e, (ev, g, x))
                            e.matmul(bank[:, 0:T], Wqk[:, q, x * P:(x + 1) * P], yT[:, g, :],
                                     start=True, stop=True).then_inc(done, 1)
                    if ev == "v":
                        bank, done = bank_of(e, (ev, g, 0))
                        for t in range(nt):
                            mm = e.matmul(bank[:, t * P:(t + 1) * P], yT[:, g, geo.start[t]:geo.start[t] + P],
                                          Wv[:, q, :], start=True, stop=True)
                        mm.then_inc(done, 1)
                    if ev == "s":
                        h, ts = jobs[j % Jb]
                        if j % Jb == 0:
                            e.wait_ge(stacked[g], 96)
                        if j > 1:
                            e.wait_ge(s_maxed, j - 1)
                        for i, t in enumerate(ts):
                            mm = e.matmul(S[j % 2][:, i * T:(i + 1) * T],
                                          QS[0:96, q, g, h, geo.start[t]:geo.start[t] + P],
                                          KS[0:96, q, g, h, :], start=True, stop=True)
                        mm.then_inc(s_ready, 1)
                    if ev == "st":
                        h, ts = jobs[j % Jb]
                        if j > 1:
                            e.wait_ge(p_ready, j - 1)
                        for i, t in enumerate(ts):
                            mm = e.matmul(ST[j % 2][:, i * T:(i + 1) * T],
                                          KS[0:99, qb, g, h, geo.start[t]:geo.start[t] + P],
                                          QS[0:99, qb, g, h, :], start=True, stop=True)
                        mm.then_inc(st_ready, 1)
                    if ev == "m":
                        e.wait_ge(mp_ready, g + 1)
                        bank, done = bank_of(e, (ev, g, 0))
                        bb = bank[:, :].bitcast(BF16)
                        for t in range(nt):
                            mm = e.transpose(bb[0:3 * HEADS, t * P:(t + 1) * P],
                                             Mp[:, g, t, :, :].rearrange("p a h -> p (a h)"), identb[:, :])
                        mm.then_inc(done, 1)
                    if ev == "pv":
                        h, ts = jobs[j % Jb]
                        if j % Jb == 0 and g > 0:
                            e.wait_ge(os_ready, g)
                        e.wait_ge(p_ready, j + 1)
                        for i, t in enumerate(ts):
                            mm = e.matmul(OB[h // 4][SLOT * (h % 4):SLOT * (h % 4 + 1), 0:T],
                                          VA[:, qb, g, t, h, :], PR[:, j % 4, i * T:(i + 1) * T],
                                          start=(t == 0), stop=(t == nt - 1))
                        mm.then_inc(pv_done, 1)
                    if ev == "o":
                        e.wait_ge(os_ready, g + 1)
                        for x in range(2):
                            bank, done = bank_of(e, (ev, g, x))
                            for t in range(nt):
                                mm = e.transpose(bank[:, t * P:(t + 1) * P],
                                                 OS[:, x, geo.start[t]:geo.start[t] + P], ident[:, :])
                            mm.then_inc(done, 1)
                        e.wait_ge(done, use[ev, g, 1][1] + 1)
                        e.sem_inc(o_turned, 1)
                    if ev == "oT":
                        e.wait_ge(on_ready, g + 1)
                        bank, done = bank_of(e, (ev, g, 0))
                        for t in range(nt):
                            mm = e.transpose(bank[:, t * P:(t + 1) * P], ON[:, g, t, :], ident[:, :])
                        mm.then_inc(done, 1)
                    if ev == "proj":
                        e.wait_ge(oT_ready, g + 1)
                        bank, done = bank_of(e, (ev, g, 0))
                        for t in range(nt):
                            mm = e.matmul(bank[:, t * P:(t + 1) * P], OT[:, g, t, :], Wp[:, q, :],
                                          start=True, stop=True)
                        mm.then_inc(done, 1)
                    if ev == "fc1":
                        e.wait_ge(y2T_ready, g + 1)
                        for x in range(2):
                            bank, done = bank_of(e, (ev, g, x))
                            e.matmul(bank[:, 0:T], W1[:, q, x * P:(x + 1) * P], y2T[:, g % 2, :],
                                     start=True, stop=True).then_inc(done, 1)
                    if ev == "fc2":
                        e.wait_ge(hid_ready, g + 1)
                        bank, done = bank_of(e, (ev, g, 0))
                        for t in range(nt):
                            for x in range(2):
                                mm = e.matmul(bank[:, t * P:(t + 1) * P],
                                              hid[:, g % 2, x, geo.start[t]:geo.start[t] + P], W2[:, q, x, :],
                                              start=(x == 0), stop=(x == 1))
                        mm.then_inc(done, 1)

            @block.scalar
            def _(e):
                def turned(g, ev, dst, cols, wcol, bcol, ready):
                    bank, free = filled(e, (ev, g, 0))
                    for t in range(nt):
                        o = geo.own[t]
                        a = e.activation(dst[:, geo.start[t] + o:geo.start[t] + P],
                                         bank[:, t * P + o:(t + 1) * P], ACT.Identity,
                                         scale=cols[:, wcol:wcol + 1], bias=cols[:, bcol:bcol + 1])
                    a.then_inc(ready, 1)
                    e.wait_ge(ready, g + 1)
                    e.sem_inc(free, 1)

                for ev, g, j in order:
                    if ev == "yT":
                        turned(g, ev, yT[:, g, :], colsA[:, q, :], 2, 3, yT_ready)
                    if ev == "y2T":
                        turned(g, ev, y2T[:, g % 2, :], colsC[:, q, :], 4, 5, y2T_ready)
                    if ev == "qk":
                        for x in range(2):
                            bank, free = filled(e, (ev, g, x))
                            e.activation(qk32[:, g, x, :], bank[:, 0:T], ACT.Identity,
                                         bias=colsA[:, q, x:x + 1]).then_inc(free, 1)
                        e.wait_ge(gfree[use[ev, g, 1][0]], use[ev, g, 1][1] + 1)
                        e.sem_inc(qk_ready, 1)
                    if ev == "st":
                        if j > 3:
                            e.wait_ge(pv_done, j - 3)
                        e.wait_ge(st_ready, j + 1)
                        e.activation(PR[:, j % 4, :], ST[j % 2][:, 0:JW], ACT.Exp, scale=HD ** -0.5)\
                            .then_inc(p_ready, 1)
                    if ev == "os":
                        e.wait_ge(pv_done, (g + 1) * Jb)
                        if g > 0:
                            e.wait_ge(o_turned, g)
                        for x in range(2):
                            a = e.activation(OS[:, x, :], OB[x][:, 0:T], ACT.Identity)
                        a.then_inc(os_ready, 1)
                    if ev == "oT":
                        bank, free = filled(e, (ev, g, 0))
                        e.activation(OT[:, g, :, :].rearrange("p t c -> p (t c)"), bank[:, 0:nt * P],
                                     ACT.Identity).then_inc(oT_ready, 1)
                        e.wait_ge(oT_ready, g + 1)
                        e.sem_inc(free, 1)
                    if ev == "fc1":
                        if g > 1:
                            b, k = use["fc2", g - 2, 0]
                            e.wait_ge(gready[b], k + 1)
                        for x in range(2):
                            bank, free = filled(e, (ev, g, x))
                            e.activation(hid[:, g % 2, x, :], bank[:, 0:T], ACT.Gelu,
                                         bias=colsC[:, q, 6 + x:7 + x]).then_inc(free, 1)
                        e.wait_ge(gfree[use[ev, g, 1][0]], use[ev, g, 1][1] + 1)
                        e.sem_inc(hid_ready, 1)

            @block.gpsimd
            def _(e):
                if "A" in stages:
                    hA = group_of(groups["A"])
                if "C" in stages:
                    hC = group_of(groups["C"])
                for ev, g, j in order:
                    if ev == "qk":
                        e.wait_ge(qk_ready, g + 1)
                        e.tensor_copy(parts[:, g, 0, :, :], qk32[:, g, :, :]).then_inc(split1, 1)
                        e.wait_ge(split1, g + 1)
                        e.tensor_tensor(rest[:, g, :, :], qk32[:, g, :, :], parts[:, g, 0, :, :],
                                        ALU.subtract).then_inc(split2, 1)
                        e.wait_ge(split2, g + 1)
                        e.tensor_copy(parts[:, g, 1, :, :], rest[:, g, :, :]).then_inc(split3, 1)
                    if ev == "split":
                        e.wait_ge(z_ready, g + 1)
                        e.tensor_tensor(hA[:, g, :, :], hA[:, g, :, :],
                                        rowp[:, q:q + 1, :].to_broadcast([P, nt, P]), ALU.add)\
                            .then_inc(h_biased, 1)
                    if ev == "y2T":
                        e.wait_ge(z2_ready, g + 1)
                        e.tensor_tensor(hC[:, g, :, :], hC[:, g, :, :],
                                        rowf[:, q:q + 1, :].to_broadcast([P, nt, P]), ALU.add)\
                            .then_inc(h2_biased, 1)
                if "A" in stages:
                    e.wait_ge(h_biased, G)

            @block.vector
            def _(e):
                linked, links = chain(e, own)
                hs = {s: group_of(groups[s]) for s in stages}
                normed = [s for s in "AC" if s in stages]

                def normalised(at, g, stage, out, ready):
                    k = (normed.index(stage) * G + g) * nt
                    for t in range(nt):
                        ins = e.tensor_scalar(out[:, t, :], hs[stage][:, g, t, :], mv[:, k + t, 0:1],
                                              rs[:, k + t:k + t + 1], ALU.subtract, ALU.mult)
                    ins.then_inc(ready, 1)

                for ev, g, j in order:
                    if ev == "ln":
                        k = 0
                        for s in normed:
                            for i in range(G):
                                for t in range(nt):
                                    ins = e.bn_stats(st6[:, k, :], hs[s][:, i, t, :])
                                    k += 1
                        linked(ins)
                        for i in range(k):
                            ins = e.bn_aggr(mv[:, i, :], st6[:, i, :])
                        linked(ins)
                        linked(e.tensor_scalar(var[:, 0:k], mv[:, 0:k, 1], EPS, None, ALU.add))
                        rsqrt(e, linked, var[:, 0:k], rs[:, 0:k], tmp[:, 0:k])
                        if "A" in stages:
                            for i in range(G):
                                normalised(ev, i, "A", Z[:, i, :, :], z_ready)
                    if ev == "z2":
                        if g > 1:
                            e.wait_ge(y2T_ready, g - 1)
                        normalised(ev, g, "C", Z2[:, g % 2, :, :], z2_ready)
                    if ev == "split":
                        e.wait_ge(split3, g + 1)
                        e.tensor_tensor(parts[:, g, 2, :, :], rest[:, g, :, :], parts[:, g, 1, :, :],
                                        ALU.subtract).then_inc(parts_ready, 1)
                    if ev == "v":
                        bank, free = filled(e, (ev, g, 0))
                        for t in range(nt):
                            ins = e.scalar_tensor_tensor(
                                VA[:, q, g, t, :, 0:HD],
                                bank[:, t * P:(t + 1) * P].rearrange("p (h d) -> p h d", d=HD),
                                mask[:, t:t + 1], bvm[:, q, t, :].rearrange("p (h d) -> p h d", d=HD),
                                ALU.mult, ALU.add)
                        ins.then_inc(free, 1)
                    if ev == "s":
                        h, ts = jobs[j % Jb]
                        e.wait_ge(s_ready, j + 1)
                        e.tensor_reduce(Mx[:, g, ts[0]:ts[-1] + 1, h],
                                        S[j % 2][:, 0:JW].rearrange("p (t k) -> p t k", k=T),
                                        AX.X, ALU.max).then_inc(s_maxed, 1)
                        if j % Jb == Jb - 1:
                            e.wait_ge(s_maxed, j + 1)
                            linked(e.tensor_copy(Mp[:, g, :, 0, :], Mx[:, g, :, :]))
                            linked(e.tensor_tensor(Mr[:, g, :, :], Mx[:, g, :, :], Mp[:, g, :, 0, :], ALU.subtract))
                            linked(e.tensor_copy(Mp[:, g, :, 1, :], Mr[:, g, :, :]))
                            e.tensor_tensor(Mp[:, g, :, 2, :], Mr[:, g, :, :], Mp[:, g, :, 1, :],
                                            ALU.subtract).then_inc(mp_ready, 1)
                    if ev == "m":
                        bank, free = filled(e, (ev, g, 0))
                        bb = bank[:, :].bitcast(BF16)
                        for t in range(nt):
                            o = geo.own[t]
                            ins = e.tensor_copy(MT[:, g, geo.start[t] + o:geo.start[t] + P],
                                                bb[0:3 * HEADS, t * P + o:(t + 1) * P])
                        ins.then_inc(mT_ready, 1)
                        e.wait_ge(mT_ready, g + 1)
                        e.sem_inc(free, 1)
                    if ev == "o":
                        for x in range(2):
                            bank, free = filled(e, (ev, g, x))
                            o4 = bank[:, 0:nt * P].rearrange("p (t h s) -> p t h s", t=nt, s=SLOT)
                            linked(e.reciprocal(RD[:, x, :, :], o4[:, :, :, HD]))
                            e.tensor_tensor(
                                ON[:, g, :, x * 64:(x + 1) * 64].rearrange("p t (h d) -> p t h d", d=HD),
                                o4[:, :, :, 0:HD], RD[:, x, :, :].unsqueeze(3).to_broadcast([P, nt, 4, HD]),
                                ALU.mult).then_inc(free, 1)
                        b, k = use[ev, g, 1]
                        e.wait_ge(gfree[b], k + 1)
                        e.sem_inc(on_ready, 1)
                    if ev == "proj":
                        bank, free = filled(e, (ev, g, 0))
                        e.tensor_tensor(hs["B"][:, g, :, :], bank[:, 0:nt * P].rearrange("p (t c) -> p t c", c=P),
                                        hs["B"][:, g, :, :], ALU.add).then_inc(free, 1)
                    if ev == "fc2":
                        e.wait_ge(h2_biased, g + 1)
                        bank, free = filled(e, (ev, g, 0))
                        e.tensor_tensor(hs["C"][:, g, :, :], bank[:, 0:nt * P].rearrange("p (t c) -> p t c", c=P),
                                        hs["C"][:, g, :, :], ALU.add).then_inc(free, 1)

        def in_flight(n):
            return ("A" if n < N else "") + ("B" if 0 <= n - 1 < N else "") + ("C" if mlp and 0 <= n - 2 < N else "")

        def round_at(n, stages, q, upcoming):
            groups = {"A": (n + 2) % rounds, "B": (n + 1) % rounds, "C": n % rounds}
            layers_of = {"A": (n + 3) // rounds % layers, "B": (n + 2) // rounds % layers,
                         "C": (n + 1) // rounds % layers}
            with nc.Block(no_gpsimd_drain=True) as block:
                one_round(block, stages, q, groups, upcoming, layers_of)
            nc.all_engine_barrier(sems_to_clear=numbers)

        for n in (0, 1):
            round_at(n - 2, in_flight(n), n % 2, in_flight(n + 1))
        with nc.Fori(0, N // 2 - 1) as i:
            for p in range(2):
                stages = "ABC" if mlp else "AB"
                round_at(i * 2 + p, stages, p, stages)
        for n in (N, N + 1):
            if in_flight(n):
                round_at(n - 2, in_flight(n), n % 2, in_flight(n + 1))
        sems.finish()


def ffn_phase(nc, tag, src, dst, cfg, w, ident):
    E, chunks, act, act_ff = cfg["experts"], cfg["chunks"], cfg["act"], cfg.get("ff_chunks", 0)
    shared = cfg.get("shared", 0)
    inner, ffc = cfg["inner"], cfg.get("ff_chunks", 0)
    units = [(e * chunks, chunks) for e in range(E)] + ([(E * chunks, shared)] if shared else [])
    K = E + (1 if shared else 0)
    NCH = sum(n for _, n in units)
    tokens = src.shape[0]
    GT = 4
    full = tokens // (GT * P)
    left = tokens - full * GT * P
    assert 0 < left <= P

    with ExitStack() as ctx:
        sems = Semaphores(nc, ctx)

        def sb(name, shape, dt=F32):
            return ctx.enter_context(nc.sbuf_tensor(f"{tag}_{name}", shape, dt))

        def signal(name):
            return sems.take(f"{tag}_{name}")

        W1 = sb("W1", [P, NCH * P])
        W2 = sb("W2", [P, NCH, P])
        B1 = sb("B1", [P, NCH])
        WR = sb("WR", [P, E])
        RB = sb("RB", [P, E])
        B2 = sb("B2", [K, P])
        col = sb("col", [P, 4])
        if ffc:
            F1 = sb("F1", [P, ffc * P])
            F2 = sb("F2", [P, ffc, P])
            FB1 = sb("FB1", [P, ffc])
            FB2 = sb("FB2", [P, P])
        number = sb("number", [P, E])
        X = sb("X", [P, full * GT + 1, P])
        Y = sb("Y", [P, GT, P])
        Z = sb("Z", [P, GT, P])
        yT = sb("yT", [P, GT * P])
        lg = sb("lg", [P, GT, E])
        pe_ = sb("expd", [P, GT, E])
        gate = sb("gate", [P, GT, E])
        comb = sb("comb", [P, GT, K])
        pick = sb("pick", [P, GT, E])
        top = sb("top", [P, GT, 8])
        topi = sb("topi", [P, GT, 8], mybir.dt.uint32)
        topf = sb("topf", [P, GT, 2])
        big = sb("big", [P, GT])
        tot = sb("tot", [P, GT])
        combT = sb("combT", [K, GT * P])
        hid = sb("hid", [P, 2, max(chunks, ffc), GT * P])
        acc = sb("acc", [P, GT, P])
        out = sb("out", [P, GT, P])
        st6 = sb("st6", [P, GT, 6])
        mv = sb("mv", [P, GT, 2])
        var = sb("var", [P, GT])
        rs = sb("rs", [P, GT])
        tmp = sb("tmp", [P, GT])
        banks = [ctx.enter_context(nc.psum_tensor(f"{tag}_ps{i}", [P, 512], F32)) for i in range(8)]
        HB, YB, GB = banks[0:4], banks[4:6], banks[6]

        first = signal("first")
        z_ready = signal("z_ready")
        gready = signal("gready")
        gfree = signal("gfree")
        yT_ready = signal("yT_ready")
        lg_ready = signal("lg_ready")
        e_ready = signal("e_ready")
        comb_ready = signal("comb_ready")
        cT_ready = signal("cT_ready")
        h_filled = signal("h_filled")
        h_ready = signal("h_ready")
        y_filled = signal("y_filled")
        y_added = signal("y_added")
        x_ready = signal("x_ready")
        out_ready = signal("out_ready")
        own = signal("own")
        numbers = range(first.num, own.num + 1)
        loaded = sems.take(f"{tag}_loaded")
        stored = sems.take(f"{tag}_stored")

        loads = [(X[:, 0:full * GT, :], src[0:full * GT * P, :].rearrange("(t p) c -> p t c", p=P)),
                 (X[0:left, full * GT, :], src[full * GT * P:tokens, :]),
                 (W1[:, :], w["w1"]), (W2[:, :, :], w["w2"].rearrange("(k p) c -> p k c", p=P)),
                 (B1[:, :], w["b1"]), (WR[:, :], w["router"]), (RB[:, :], w["router_b"].to_broadcast([P, E])),
                 (B2[:, :], w["b2"]), (number[:, :], w["number"].to_broadcast([P, E])),
                 (col[:, :], w["cols"])]
        if ffc:
            loads += [(F1[:, :], w["f1"]), (F2[:, :, :], w["f2"].rearrange("(k p) c -> p k c", p=P)),
                      (FB1[:, :], w["fb1"]), (FB2[:, :], w["fb2"].to_broadcast([P, P]))]

        with nc.Block() as block:
            @block.sync
            def _(e):
                for to, fr in loads:
                    e.dma_start(to, fr).then_inc(loaded, 16)
                e.wait_ge(loaded, 16 * len(loads))

            @block.vector
            def _(e):
                if shared:
                    e.memset(comb[:, :, E:K], cfg["shared_scale"])

        def one_round(block, r, nt, rows):
            N = (nt - 1) * P + rows
            steps = []
            for u in range(len(units)):
                steps.append(("up", u))
                if u:
                    steps.append(("down", u - 1))
            steps.append(("down", len(units) - 1))
            hb_count = {}
            k = 0
            for u, (_, n) in enumerate(units):
                hb_count[u] = k
                k += n
            U = len(units)
            hb_count[U] = k

            def x_of():
                if isinstance(r, int):
                    return X[0:rows, GT * r:GT * r + nt, :]
                return X[0:rows, bass.ds(r * GT, nt), :]

            def chunk_list(u):
                return units[u] if u < U else (0, ffc)

            @block.tensor
            def _(e):
                use = [0]

                def general():
                    if use[0] > 0:
                        e.wait_ge(gfree, use[0])
                    use[0] += 1

                def turn(count):
                    e.wait_ge(z_ready, count)
                    general()
                    for t in range(nt):
                        mm = e.transpose(GB[:, t * P:t * P + rows], Z[0:rows, t, :], ident[0:rows, 0:rows])
                    mm.then_inc(gready, 1)

                def up(u):
                    w1 = W1 if u < U else F1
                    at, n = chunk_list(u)
                    for c in range(n):
                        k = hb_count[u] + c
                        if k > 3:
                            e.wait_ge(h_ready, k - 3)
                        e.matmul(HB[k % 4][:, 0:N], w1[:, (at + c) * P:(at + c + 1) * P], yT[:, 0:N],
                                 start=True, stop=True).then_inc(h_filled, 1)

                def down(u):
                    w2 = W2 if u < U else F2
                    at, n = chunk_list(u)
                    e.wait_ge(h_ready, hb_count[u] + n)
                    e.wait_ge(y_added, u)
                    for t in range(nt):
                        for c in range(n):
                            mm = e.matmul(YB[u % 2][0:rows, t * P:(t + 1) * P],
                                          hid[:, u % 2, c, t * P:t * P + rows], w2[:, at + c, :],
                                          start=(c == 0), stop=(c == n - 1))
                    mm.then_inc(y_filled, 1)

                turn(1)
                e.wait_ge(yT_ready, 1)
                general()
                for t in range(nt):
                    mm = e.matmul(GB[0:rows, t * E:(t + 1) * E], yT[:, t * P:t * P + rows], WR[:, :],
                                  start=True, stop=True)
                mm.then_inc(gready, 1)
                for n, (what, u) in enumerate(steps):
                    if n == 1:
                        e.wait_ge(comb_ready, 1)
                        general()
                        for t in range(nt):
                            mm = e.transpose(GB[0:K, t * P:t * P + rows], comb[0:rows, t, :],
                                             ident[0:rows, 0:rows])
                        mm.then_inc(gready, 1)
                        e.wait_ge(cT_ready, 1)
                        general()
                        for t in range(nt):
                            mm = e.matmul(GB[0:rows, t * P:(t + 1) * P], combT[:, t * P:t * P + rows],
                                          B2[:, :], start=True, stop=True)
                        mm.then_inc(gready, 1)
                    (up if what == "up" else down)(u)
                if ffc:
                    turn(2)
                    e.wait_ge(yT_ready, 2)
                    up(U)
                    down(U)

            @block.scalar
            def _(e):
                def turned(count, use, c0):
                    e.wait_ge(gready, use)
                    if count == 2:
                        e.wait_ge(h_filled, hb_count[U])
                    if inner or count == 2:
                        ins = e.activation(yT[:, 0:N], GB[:, 0:N], ACT.Identity,
                                           scale=col[:, c0:c0 + 1], bias=col[:, c0 + 1:c0 + 2])
                    else:
                        ins = e.activation(yT[:, 0:N], GB[:, 0:N], ACT.Identity)
                    ins.then_inc(yT_ready, 1)
                    e.wait_ge(yT_ready, count)
                    e.sem_inc(gfree, 1)

                def hidden(u):
                    b1 = B1 if u < U else FB1
                    at, n = chunk_list(u)
                    if u > 1:
                        e.wait_ge(y_filled, u - 1)
                    for c in range(n):
                        k = hb_count[u] + c
                        e.wait_ge(h_filled, k + 1)
                        e.activation(hid[:, u % 2, c, 0:N], HB[k % 4][:, 0:N], act,
                                     bias=b1[:, at + c:at + c + 1]).then_inc(h_ready, 1)

                turned(1, 1, 0)
                e.wait_ge(lg_ready, 1)
                e.activation(pe_[0:rows, 0:nt, :], lg[0:rows, 0:nt, :], ACT.Exp,
                             scale=1.0 / cfg["temperature"]).then_inc(e_ready, 1)
                hidden(0)
                e.wait_ge(gready, 3)
                e.activation(combT[:, 0:N], GB[0:K, 0:N], ACT.Identity).then_inc(cT_ready, 1)
                e.wait_ge(cT_ready, 1)
                e.sem_inc(gfree, 1)
                for u in range(1, U):
                    hidden(u)
                if ffc:
                    turned(2, 5, 2)
                    hidden(U)

            @block.gpsimd
            def _(e):
                if inner:
                    e.wait_ge(z_ready, 1)
                    e.tensor_tensor(out[0:rows, 0:nt, :], x_of(), Y[0:rows, 0:nt, :], ALU.add)\
                        .then_inc(x_ready, 1)
                    e.wait_ge(x_ready, 1)
                    e.tensor_tensor(out[0:rows, 0:nt, :], out[0:rows, 0:nt, :],
                                    FB2[0:rows, :].unsqueeze(1).to_broadcast([rows, nt, P]), ALU.add)\
                        .then_inc(x_ready, 1)

            @block.vector
            def _(e):
                linked, _n = chain(e, own)

                def norm(x, y):
                    for t in range(nt):
                        ins = e.bn_stats(st6[0:rows, t, :], x[:, t, :])
                    linked(ins)
                    for t in range(nt):
                        ins = e.bn_aggr(mv[0:rows, t, :], st6[0:rows, t, :])
                    linked(ins)
                    linked(e.tensor_scalar(var[0:rows, 0:nt], mv[0:rows, 0:nt, 1], EPS, None, ALU.add))
                    rsqrt(e, linked, var[0:rows, 0:nt], rs[0:rows, 0:nt], tmp[0:rows, 0:nt])
                    for t in range(nt):
                        ins = e.tensor_scalar(y[0:rows, t, :], x[:, t, :], mv[0:rows, t, 0:1],
                                              rs[0:rows, t:t + 1], ALU.subtract, ALU.mult)
                    return ins

                if inner:
                    linked(norm(x_of(), Y))
                    norm(Y[0:rows, 0:nt, :], Z).then_inc(z_ready, 1)
                else:
                    norm(x_of(), Z).then_inc(z_ready, 1)
                L, G_, C, PK = (a[0:rows, 0:nt, :] for a in (lg, gate, comb, pick))
                e.wait_ge(gready, 2)
                linked(e.tensor_tensor(L, GB[0:rows, 0:nt * E].rearrange("p (t e) -> p t e", e=E),
                                       RB[0:rows, :].unsqueeze(1).to_broadcast([rows, nt, E]), ALU.add))
                e.sem_inc(gfree, 1)
                linked(e.tensor_reduce(big[0:rows, 0:nt], L, AX.X, ALU.max))
                e.tensor_tensor(L, L, big[0:rows, 0:nt].unsqueeze(2).to_broadcast([rows, nt, E]),
                                ALU.subtract).then_inc(lg_ready, 1)
                e.wait_ge(e_ready, 1)
                linked(e.tensor_reduce(tot[0:rows, 0:nt], pe_[0:rows, 0:nt, :], AX.X, ALU.add))
                linked(e.reciprocal(tot[0:rows, 0:nt], tot[0:rows, 0:nt]))
                linked(e.tensor_tensor(G_, pe_[0:rows, 0:nt, :],
                                       tot[0:rows, 0:nt].unsqueeze(2).to_broadcast([rows, nt, E]), ALU.mult))
                for t in range(nt):
                    ins = e.max(top[0:rows, t, :], gate[0:rows, t, :])
                linked(ins)
                for t in range(nt):
                    ins = e.max_index(topi[0:rows, t, :], top[0:rows, t, :], gate[0:rows, t, :])
                linked(ins)
                linked(e.tensor_copy(topf[0:rows, 0:nt, :], topi[0:rows, 0:nt, 0:2]))
                nb = number[0:rows, :].unsqueeze(1).to_broadcast([rows, nt, E])
                for i in range(2):
                    linked(e.tensor_tensor(PK if i == 0 else L, nb,
                                           topf[0:rows, 0:nt, i:i + 1].to_broadcast([rows, nt, E]),
                                           ALU.is_equal))
                linked(e.tensor_tensor(PK, PK, L, ALU.add))
                e.tensor_tensor(comb[0:rows, 0:nt, 0:E], PK, G_, ALU.mult).then_inc(comb_ready, 1)
                e.wait_ge(gready, 4)
                e.wait_ge(comb_ready, 1)
                e.tensor_copy(acc[0:rows, 0:nt, :],
                              GB[0:rows, 0:nt * P].rearrange("p (t c) -> p t c", c=P)).then_inc(y_added, 1)
                e.wait_ge(y_added, 1)
                e.sem_inc(gfree, 1)
                for u in range(U):
                    e.wait_ge(y_filled, u + 1)
                    e.wait_ge(y_added, u + 1)
                    for t in range(nt):
                        ins = e.scalar_tensor_tensor(acc[0:rows, t, :], YB[u % 2][0:rows, t * P:(t + 1) * P],
                                                     comb[0:rows, t, u:u + 1], acc[0:rows, t, :],
                                                     ALU.mult, ALU.add)
                    ins.then_inc(y_added, 1)
                e.wait_ge(y_added, U + 1)
                if ffc:
                    norm(acc[0:rows, 0:nt, :], Z).then_inc(z_ready, 1)
                    e.wait_ge(x_ready, 2)
                    linked(e.tensor_tensor(out[0:rows, 0:nt, :], out[0:rows, 0:nt, :], acc[0:rows, 0:nt, :], ALU.add))
                    e.wait_ge(y_filled, U + 1)
                    e.tensor_tensor(out[0:rows, 0:nt, :],
                                    YB[U % 2][0:rows, 0:nt * P].rearrange("p (t c) -> p t c", c=P),
                                    out[0:rows, 0:nt, :], ALU.add).then_inc(out_ready, 1)
                else:
                    e.tensor_tensor(out[0:rows, 0:nt, :], acc[0:rows, 0:nt, :], x_of(), ALU.add)\
                        .then_inc(out_ready, 1)

            @block.sync
            def _(e):
                e.wait_ge(out_ready, 1)
                if isinstance(r, int):
                    to = dst[GT * P * r:GT * P * r + N, :]
                    e.dma_start(to, out[0:rows, 0, :]).then_inc(stored, 16)
                else:
                    to = dst[bass.ds(r * (GT * P), GT * P), :].rearrange("(t p) c -> p t c", p=P)
                    e.dma_start(to, out[:, :, :]).then_inc(stored, 16)
                e.wait_ge(stored, 16)

        clear = range(min(numbers[0], stored.num), max(numbers[-1], stored.num) + 1)
        with nc.Fori(0, full) as r:
            with nc.Block(no_gpsimd_drain=True) as block:
                one_round(block, r, GT, P)
            nc.all_engine_barrier(sems_to_clear=clear)
        with nc.Block(no_gpsimd_drain=True) as block:
            one_round(block, full, 1, left)
        nc.all_engine_barrier(sems_to_clear=clear)
        sems.finish()


def offsets_of(tokens):
    far = (48, 64, 96, 128, 192, 256, 384, 512, 768, 1024)
    return [o for o in list(range(33)) + list(far) if o < tokens]


def dilated_phase(nc, tag, src, dst, w, ident, group=2):
    T = w["tokens"]
    geo = Geometry(T)
    nt = geo.tiles
    OFF = offsets_of(T)
    NO = len(OFF)
    STRIP = P // HEADS
    NS = -(-NO // STRIP)
    PAD = OFF[-1]
    G, rounds = group, BATCH // group
    KO = NO * HEADS

    with ExitStack() as ctx:
        sems = Semaphores(nc, ctx)

        def sb(name, shape, dt=F32):
            return ctx.enter_context(nc.sbuf_tensor(f"{tag}_{name}", shape, dt))

        def signal(name):
            return sems.take(f"{tag}_{name}")

        Wqkvg = sb("Wqkvg", [P, 4, P])
        Wo = sb("Wo", [P, P])
        cols = sb("cols", [P, 8])
        bo = sb("bo", [P, P])
        se = sb("se", [P, NO])
        heads = sb("heads", [P, HEADS])
        sel = sb("sel", [P, NO, P])
        spread = sb("spread", [P, STRIP, P])
        pb = sb("pb", [P, NS, 3])
        eff = sb("eff", [P, NS])
        mask = sb("mask", [P, nt, NO])
        X = sb("X", [P, BATCH, nt, P])
        Z = sb("Z", [P, G, nt, P])
        yT = sb("yT", [P, G, T])
        q = sb("q", [P, G, T])
        kpad = sb("kpad", [P, G, PAD + T])
        vpad = sb("vpad", [P, G, PAD + T])
        gt = sb("gt", [P, G, T])
        PR = sb("PR", [P, 4, T])
        SC = sb("SC", [P, NS, T])
        sm = sb("sm", [P, nt, NS * P])
        big = sb("big", [P, nt, HEADS])
        tot = sb("tot", [P, nt, HEADS])
        AT = sb("AT", [P, G, NS, T])
        AV = sb("AV", [P, 3, T])
        og = sb("og", [P, G, T])
        out = sb("out", [P, G, nt, P])
        st6 = sb("st6", [P, G, nt, 6])
        mv = sb("mv", [P, G, nt, 2])
        var = sb("var", [P, G * nt])
        rs = sb("rs", [P, G * nt])
        tmp = sb("tmp", [P, G * nt])
        banks = [ctx.enter_context(nc.psum_tensor(f"{tag}_ps{i}", [P, 512], F32)) for i in range(8)]
        SB, GB, BB, AB = banks[0:3], banks[3:5], banks[5:7], banks[7]

        order = [("ln", g, 0) for g in range(G)]
        order += [(ev, g, 0) for g in range(G) for ev in ("yT", "qkv")]
        for g in range(G):
            for i in range(NO):
                order.append(("sc", g, i))
                if g and i in (4, 14, 20):
                    order.append((("soft", "norm", "AT")[(4, 14, 20).index(i)], g - 1, 0))
            order.append(("strips", g, 0))
        for g in range(G):
            for i in range(NO):
                order.append(("pv", g, i))
                if g == 0 and G > 1 and i in (4, 14, 20):
                    order.append((("soft", "norm", "AT")[(4, 14, 20).index(i)], G - 1, 0))
            order.append(("gated", g, 0))
            order.append(("proj", g, 0))

        needs = {"yT": 1, "qkv": 4, "soft": nt, "AT": NS, "proj": 1}
        use, uses = {}, 0
        for ev, g, _ in order:
            for i in range(needs.get(ev, 0)):
                use[ev, g, i] = (uses % 2, uses // 2)
                uses += 1

        gready = [signal(f"gready{i}") for i in range(2)]
        gfree = [signal(f"gfree{i}") for i in range(2)]
        z_ready = signal("z_ready")
        yT_ready = signal("yT_ready")
        qkv_ready = signal("qkv_ready")
        prod_ready = signal("prod_ready")
        prod_used = signal("prod_used")
        SC_ready = signal("SC_ready")
        lg_ready = signal("lg_ready")
        e_ready = signal("e_ready")
        A_ready = signal("A_ready")
        AT_ready = signal("AT_ready")
        b_ready = signal("b_ready")
        av_ready = signal("av_ready")
        av_used = signal("av_used")
        og_ready = signal("og_ready")
        x_ready = signal("x_ready")
        out_ready = signal("out_ready")
        own = signal("own")
        numbers = range(gready[0].num, own.num + 1)
        stored = sems.take(f"{tag}_stored")
        clear = range(numbers[0], stored.num + 1)
        loaded = sems.take(f"{tag}_loaded")
        built = sems.take(f"{tag}_built")

        srcb = src.rearrange("(b t) c -> b t c", b=BATCH)
        dstb = dst.rearrange("(b t) c -> b t c", b=BATCH)
        loads = [(X[:, :, t, :], srcb[:, geo.start[t]:geo.start[t] + P, :].rearrange("b p c -> p b c"))
                 for t in range(nt)]
        loads += [(Wqkvg[:, 0:3, :], w["qkv"].rearrange("a (x b) -> a x b", x=3)), (Wqkvg[:, 3, :], w["gate"]),
                  (Wo[:, :], w["out"]), (cols[:, 0:5], w["cols"]), (bo[:, :], w["b_out"].to_broadcast([P, P])),
                  (se[:, :], w["scale_embed"]), (heads[:, :], w["heads"]), (spread[:, :, :], w["spread"]),
                  (pb[:, :, :], w["pb"]), (mask[:, :, :], w["mask"])]
        with nc.Block() as block:
            @block.sync
            def _(e):
                for to, fr in loads:
                    e.dma_start(to, fr).then_inc(loaded, 16)
                e.wait_ge(loaded, 16 * len(loads))

            @block.vector
            def _(e):
                e.memset(kpad[:, :, 0:PAD], 0.0)
                e.memset(vpad[:, :, 0:PAD], 0.0)
                e.memset(sm[:, :, :], 0.0)
                e.memset(sel[:, :, :], 0.0).then_inc(built, 1)
                e.wait_ge(loaded, 16 * len(loads))
                e.tensor_scalar(cols[:, 5:7], cols[:, 3:5], 0.5, None, ALU.mult)
                e.tensor_scalar(se[:, :], se[:, :], 1.0, HD ** -0.5, ALU.add, ALU.mult).then_inc(built, 1)
                e.tensor_tensor(eff[:, :], pb[:, :, 1], pb[:, :, 2], ALU.mult).then_inc(built, 1)
                e.wait_ge(built, 3)
                e.tensor_tensor(eff[:, :], eff[:, :], pb[:, :, 0], ALU.add)
                for i in range(NO):
                    at = (i % STRIP) * HEADS
                    e.tensor_scalar(sel[:, i, at:at + HEADS], heads[:, :], se[:, i:i + 1], None, ALU.mult)

        def one_round(block, r):
            def xb(g):
                return X[:, bass.ds(r * G + g, 1), :, :].rearrange("p o t c -> p (o t) c")

            def cut(i):
                return 0 if i % STRIP == 0 else OFF[i]

            def filled(e, key):
                b, k = use[key]
                e.wait_ge(gready[b], k + 1)
                return GB[b], gfree[b]

            @block.tensor
            def _(e):
                def bank_of(key):
                    b, k = use[key]
                    if k > 0:
                        e.wait_ge(gfree[b], k)
                    return GB[b], gready[b]

                def add_up(j):
                    g, i = divmod(j, NO)
                    e.wait_ge(av_ready, j + 1)
                    if i == 0:
                        if g > 0:
                            e.wait_ge(og_ready, g)
                    c = OFF[i]
                    e.matmul(AB[:, c:T], ident[:, :], AV[:, j % 3, c:T], start=(i == 0), stop=(i == NO - 1),
                             skip_group_check=True).then_inc(av_used, 1)

                for ev, g, i in order:
                    if ev == "yT":
                        e.wait_ge(z_ready, g + 1)
                        bank, done = bank_of((ev, g, 0))
                        for t in range(nt):
                            mm = e.transpose(bank[:, t * P:(t + 1) * P], Z[:, g, t, :], ident[:, :])
                        mm.then_inc(done, 1)
                    if ev == "qkv":
                        e.wait_ge(yT_ready, g + 1)
                        for x in range(4):
                            bank, done = bank_of((ev, g, x))
                            e.matmul(bank[:, 0:T], Wqkvg[:, x, :], yT[:, g, :], start=True, stop=True)\
                                .then_inc(done, 1)
                    if ev == "sc":
                        j = g * NO + i
                        e.wait_ge(prod_ready, j + 1)
                        if i == 0:
                            if g > 0:
                                e.wait_ge(SC_ready, g)
                        c = cut(i)
                        e.matmul(SB[i // STRIP][:, c:T], sel[:, i, :], PR[:, j % 4, c:T],
                                 start=(i % STRIP == 0), stop=(i % STRIP == STRIP - 1 or i == NO - 1),
                                 skip_group_check=True).then_inc(prod_used, 1)
                    if ev == "soft":
                        e.wait_ge(SC_ready, g + 1)
                        for t in range(nt):
                            bank, done = bank_of((ev, g, t))
                            for s in range(NS):
                                mm = e.transpose(bank[:, s * P:(s + 1) * P],
                                                 SC[:, s, geo.start[t]:geo.start[t] + P], ident[:, :])
                            mm.then_inc(done, 1)
                    if ev == "AT":
                        e.wait_ge(A_ready, g + 1)
                        for s in range(NS):
                            bank, done = bank_of((ev, g, s))
                            for t in range(nt):
                                mm = e.transpose(bank[:, t * P:(t + 1) * P], sm[:, t, s * P:(s + 1) * P],
                                                 ident[:, :])
                            mm.then_inc(done, 1)
                    if ev == "pv":
                        j = g * NO + i
                        if i == 0:
                            e.wait_ge(AT_ready, g + 1)
                        if j > 1:
                            e.wait_ge(av_ready, j - 1)
                        c = OFF[i]
                        e.matmul(BB[j % 2][:, c:T], spread[:, i % STRIP, :], AT[:, g, i // STRIP, c:T],
                                 start=True, stop=True).then_inc(b_ready, 1)
                        if i:
                            add_up(j - 1)
                    if ev == "gated":
                        add_up(g * NO + NO - 1)
                    if ev == "proj":
                        e.wait_ge(og_ready, g + 1)
                        bank, done = bank_of((ev, g, 0))
                        for t in range(nt):
                            mm = e.matmul(bank[:, t * P:(t + 1) * P], og[:, g, geo.start[t]:geo.start[t] + P],
                                          Wo[:, :], start=True, stop=True)
                        mm.then_inc(done, 1)

            @block.scalar
            def _(e):
                for ev, g, i in order:
                    if ev == "yT":
                        bank, free = filled(e, (ev, g, 0))
                        for t in range(nt):
                            o = geo.own[t]
                            a = e.activation(yT[:, g, geo.start[t] + o:geo.start[t] + P],
                                             bank[:, t * P + o:(t + 1) * P], ACT.Identity)
                        a.then_inc(yT_ready, 1)
                        e.wait_ge(yT_ready, g + 1)
                        e.sem_inc(free, 1)
                    if ev == "qkv":
                        for x in range(4):
                            bank, free = filled(e, (ev, g, x))
                            if x < 3:
                                to = (q[:, g, :], kpad[:, g, PAD:], vpad[:, g, PAD:])[x]
                                a = e.activation(to, bank[:, 0:T], ACT.Identity, bias=cols[:, x:x + 1])
                            else:
                                a = e.activation(gt[:, g, :], bank[:, 0:T], ACT.Tanh, scale=0.5,
                                                 bias=cols[:, 5:6])
                            a.then_inc(free, 1)
                        b, k = use[ev, g, 3]
                        e.wait_ge(gfree[b], k + 1)
                        e.sem_inc(qkv_ready, 1)
                    if ev == "strips":
                        e.wait_ge(prod_used, (g + 1) * NO)
                        if g:
                            b, k = use["soft", g - 1, nt - 1]
                            e.wait_ge(gready[b], k + 1)
                        for s in range(NS):
                            a = e.activation(SC[:, s, :], SB[s][:, 0:T], ACT.Identity, bias=eff[:, s:s + 1])
                        a.then_inc(SC_ready, 1)
                    if ev == "norm":
                        e.wait_ge(lg_ready, g + 1)
                        e.activation(sm[:, :, 0:KO], sm[:, :, 0:KO], ACT.Exp).then_inc(e_ready, 1)
                    if ev == "AT":
                        for s in range(NS):
                            bank, free = filled(e, (ev, g, s))
                            for t in range(nt):
                                o = geo.own[t]
                                a = e.activation(AT[:, g, s, geo.start[t] + o:geo.start[t] + P],
                                                 bank[:, t * P + o:(t + 1) * P], ACT.Identity)
                            a.then_inc(free, 1)
                        b, k = use[ev, g, NS - 1]
                        e.wait_ge(gfree[b], k + 1)
                        e.sem_inc(AT_ready, 1)

            @block.gpsimd
            def _(e):
                for g in range(G):
                    e.wait_ge(z_ready, g + 1)
                    e.tensor_tensor(out[:, g, :, :], xb(g), bo[:, :].unsqueeze(1).to_broadcast([P, nt, P]),
                                    ALU.add).then_inc(x_ready, 1)

            @block.vector
            def _(e):
                linked, _n = chain(e, own)
                sm4 = sm[:, :, 0:KO].rearrange("p t (o h) -> p t o h", h=HEADS)
                smh = sm[:, :, 0:KO].rearrange("p t (o h) -> p t h o", h=HEADS)
                for ev, g, i in order:
                    if ev == "ln" and g == 0:
                        for x in range(G):
                            for t in range(nt):
                                ins = e.bn_stats(st6[:, x, t, :], xb(x)[:, t, :])
                        linked(ins)
                        for x in range(G):
                            for t in range(nt):
                                ins = e.bn_aggr(mv[:, x, t, :], st6[:, x, t, :])
                        linked(ins)
                        linked(e.tensor_scalar(var[:, :], mv[:, :, :, 1].rearrange("p g t -> p (g t)"),
                                               EPS, None, ALU.add))
                        rsqrt(e, linked, var[:, :], rs[:, :], tmp[:, :])
                        for x in range(G):
                            for t in range(nt):
                                ins = e.tensor_scalar(Z[:, x, t, :], xb(x)[:, t, :], mv[:, x, t, 0:1],
                                                      rs[:, x * nt + t:x * nt + t + 1], ALU.subtract, ALU.mult)
                            ins.then_inc(z_ready, 1)
                    if ev == "sc":
                        j = g * NO + i
                        if i == 0:
                            e.wait_ge(qkv_ready, g + 1)
                        if j > 3:
                            e.wait_ge(prod_used, j - 3)
                        c = cut(i)
                        at = PAD - OFF[i]
                        e.tensor_tensor(PR[:, j % 4, c:T], q[:, g, c:T], kpad[:, g, at + c:at + T], ALU.mult)\
                            .then_inc(prod_ready, 1)
                    if ev == "soft":
                        if g > 0:
                            e.wait_ge(AT_ready, g)
                        for t in range(nt):
                            bank, free = filled(e, (ev, g, t))
                            e.tensor_tensor(sm4[:, t], bank[:, 0:KO].rearrange("p (o h) -> p o h", h=HEADS),
                                            mask[:, t, :].unsqueeze(2).to_broadcast([P, NO, HEADS]),
                                            ALU.add).then_inc(free, 1)
                        b, k = use[ev, g, nt - 1]
                        e.wait_ge(gfree[b], k + 1)
                        linked(e.tensor_reduce(big[:, :, :], smh, AX.X, ALU.max))
                        for t in range(nt):
                            ins = e.tensor_tensor(sm4[:, t], sm4[:, t],
                                                  big[:, t, :].unsqueeze(1).to_broadcast([P, NO, HEADS]),
                                                  ALU.subtract)
                        ins.then_inc(lg_ready, 1)
                    if ev == "norm":
                        e.wait_ge(e_ready, g + 1)
                        linked(e.tensor_reduce(tot[:, :, :], smh, AX.X, ALU.add))
                        linked(e.reciprocal(tot[:, :, :], tot[:, :, :]))
                        for t in range(nt):
                            ins = e.tensor_tensor(sm4[:, t], sm4[:, t],
                                                  tot[:, t, :].unsqueeze(1).to_broadcast([P, NO, HEADS]), ALU.mult)
                        ins.then_inc(A_ready, 1)
                    if ev == "pv":
                        j = g * NO + i
                        e.wait_ge(b_ready, j + 1)
                        if j > 2:
                            e.wait_ge(av_used, j - 2)
                        c = OFF[i]
                        at = PAD - c
                        e.tensor_tensor(AV[:, j % 3, c:T], BB[j % 2][:, c:T], vpad[:, g, at + c:at + T],
                                        ALU.mult).then_inc(av_ready, 1)
                    if ev == "gated":
                        linked(e.tensor_scalar(gt[:, g, :], gt[:, g, :], cols[:, 6:7], cols[:, 6:7],
                                               ALU.mult, ALU.add))
                        e.wait_ge(av_used, (g + 1) * NO)
                        e.tensor_tensor(og[:, g, :], AB[:, 0:T], gt[:, g, :], ALU.mult)\
                            .then_inc(og_ready, 1)
                    if ev == "proj":
                        e.wait_ge(x_ready, g + 1)
                        bank, free = filled(e, (ev, g, 0))
                        e.tensor_tensor(out[:, g, :, :], bank[:, 0:nt * P].rearrange("p (t c) -> p t c", c=P),
                                        out[:, g, :, :], ALU.add).then_inc(out_ready, 1)
                        e.wait_ge(out_ready, g + 1)
                        e.sem_inc(free, 1)

            @block.sync
            def _(e):
                for g in range(G):
                    e.wait_ge(out_ready, g + 1)
                    to = dstb[bass.ds(r * G + g, 1)].rearrange("o t c -> (o t) c")
                    e.dma_start(to[0:(nt - 1) * P, :].rearrange("(t p) c -> p t c", p=P),
                                out[:, g, 0:nt - 1, :]).then_inc(stored, 16)
                    e.dma_start(to[(nt - 1) * P:T, :], out[geo.own[-1]:P, g, nt - 1, :]).then_inc(stored, 16)
                e.wait_ge(stored, 32 * G)

        with nc.Fori(0, rounds) as r:
            with nc.Block(no_gpsimd_drain=True) as block:
                one_round(block, r)
            nc.all_engine_barrier(sems_to_clear=clear)
        sems.finish()


def embed_phase(nc, H, hA, w, ident, group=4):
    GRID, PX, CH = 14, 16, 3
    geo = Geometry(GRID * GRID + 1)
    nt, T = geo.tiles, geo.tokens
    K = CH * PX
    S, SEM = 77, 512
    NC = SEM // P
    G, rounds = group, BATCH // group

    with ExitStack() as ctx:
        sems = Semaphores(nc, ctx)

        def sb(name, shape, dt=F32):
            return ctx.enter_context(nc.sbuf_tensor(f"emb_{name}", shape, dt))

        def signal(name):
            return sems.take(f"emb_{name}")

        CW = sb("CW", [K, PX, P])
        cols = sb("cols", [P, 2])
        pos = sb("pos", [P, nt, P])
        WT = sb("WT", [P, NC, P])
        idx = sb("idx", [S, BATCH], I32)
        low = sb("low", [S, BATCH], I32)
        idg = sb("idg", [S, G], I32)
        XI = sb("XI", [K, G, GRID, GRID * PX])
        ET = sb("ET", [P, G, T])
        TX = sb("TX", [S, G, SEM])
        TXT = sb("TXT", [P, G, NC, S])
        sums = sb("sums", [S, G])
        TO = sb("TO", [S, G, P])
        banks = [ctx.enter_context(nc.psum_tensor(f"emb_ps{i}", [P, 512], F32)) for i in range(8)]
        EB, TB, XB, YB = banks[0:2], banks[2:4], banks[4:6], banks[6:8]

        arrived = [signal(f"arrived{g}") for g in range(G)]
        gathered = [signal(f"gathered{g}") for g in range(G)]
        emb_filled = signal("emb_filled")
        ET_ready = signal("ET_ready")
        tb_filled = signal("tb_filled")
        h_ready = signal("h_ready")
        id_ready = signal("id_ready")
        sum_ready = signal("sum_ready")
        xb_filled = signal("xb_filled")
        TXT_ready = signal("TXT_ready")
        yb_filled = signal("yb_filled")
        TO_ready = signal("TO_ready")
        own = signal("own")
        stored = sems.take("emb_stored")
        clear = range(arrived[0].num, stored.num + 1)
        loaded = sems.take("emb_loaded")
        set_up = sems.take("emb_set_up")

        rowsA = hA.rearrange("(b t) c -> b t c", b=BATCH)
        loads = [(CW[:, :, :], w["conv"].rearrange("(k x) d -> k x d", x=PX)), (cols[:, :], w["cols"]),
                 (WT[:, :, :], w["W"].rearrange("(k p) d -> p k d", p=P)), (idx[:, :], w["idx"])]
        loads += [(pos[:, t, :], w["pos"][geo.start[t]:geo.start[t] + P, :]) for t in range(nt)]
        with nc.Block() as block:
            @block.sync
            def _(e):
                for to, fr in loads:
                    e.dma_start(to, fr).then_inc(loaded, 16)
                e.wait_ge(loaded, 16 * len(loads))

            @block.vector
            def _(e):
                e.wait_ge(loaded, 16 * len(loads))
                e.tensor_scalar(low[:, :], idx[:, :], 0.0, float(w["vocab"]), ALU.is_lt, ALU.mult)\
                    .then_inc(set_up, 1)
                e.wait_ge(set_up, 1)
                e.tensor_tensor(idx[:, :], idx[:, :], low[:, :], ALU.add).then_inc(set_up, 1)
                e.wait_ge(set_up, 2)
                e.tensor_scalar(idx[:, :], idx[:, :], 0.0, float(w["vocab"] - 1), ALU.max, ALU.min)

        def one_round(block, r):
            order = []
            for i in range(G + 2):
                if i < G:
                    order.append(("emb", i))
                    order.append(("txt", i))
                if 1 <= i <= G:
                    order.append(("turn", i - 1))
                    order.append(("prod", i - 1))

            @block.sync
            def _(e):
                for g in range(G):
                    for c in range(CH):
                        src = w["x"][bass.ds(r * G + g, 1), c].rearrange("o (a p) x -> p (o a) x", p=PX)
                        e.dma_start(XI[c * PX:(c + 1) * PX, g, :, :], src).then_inc(arrived[g], 16)
                for g in range(G):
                    e.wait_ge(TO_ready, g + 1)
                    e.dma_start(rowsA[bass.ds(r * G + g, 1), T:T + S, :].rearrange("o t c -> (o t) c"),
                                TO[:, g, :]).then_inc(stored, 16)
                e.wait_ge(stored, 16 * G)

            @block.gpsimd
            def _(e):
                e.wait_ge(id_ready, 1)
                for g in range(G):
                    e.indirect_dma_start(TX[:, g, :], None, w["table"],
                                         bass.IndirectOffsetOnAxis(ap=idg[:, g:g + 1], axis=0))\
                        .then_inc(gathered[g], 16)
                for g in range(G):
                    e.wait_ge(gathered[g], 16)
                e.dma_reset(range(gathered[0].num, gathered[-1].num + 1))

            @block.tensor
            def _(e):
                for ev, g in order:
                    if ev == "emb":
                        e.wait_ge(arrived[g], 16 * CH)
                        if g > 1:
                            e.wait_ge(ET_ready, g - 1)
                        for x in range(PX):
                            mm = e.matmul(EB[g % 2][:, 0:T - 1], CW[:, x, :],
                                          XI[:, g, :, :].rearrange("k a (b x) -> k a b x", x=PX)[:, :, :, x],
                                          start=(x == 0), stop=(x == PX - 1))
                        mm.then_inc(emb_filled, 1)
                    if ev == "txt":
                        e.wait_ge(gathered[g], 16)
                        if g > 1:
                            e.wait_ge(TXT_ready, g - 1)
                        for c in range(NC):
                            mm = e.transpose(XB[g % 2][:, c * S:(c + 1) * S], TX[:, g, c * P:(c + 1) * P],
                                             ident[0:S, 0:S])
                        mm.then_inc(xb_filled, 1)
                    if ev == "turn":
                        e.wait_ge(ET_ready, g + 1)
                        if g > 1:
                            e.wait_ge(h_ready, g - 1)
                        for t in range(nt):
                            mm = e.transpose(TB[g % 2][:, t * P:(t + 1) * P],
                                             ET[:, g, geo.start[t]:geo.start[t] + P], ident[:, :])
                        mm.then_inc(tb_filled, 1)
                    if ev == "prod":
                        e.wait_ge(TXT_ready, g + 1)
                        if g > 1:
                            e.wait_ge(TO_ready, g - 1)
                        for c in range(NC):
                            mm = e.matmul(YB[g % 2][0:S, 0:P], TXT[:, g, c, :], WT[:, c, :],
                                          start=(c == 0), stop=(c == NC - 1))
                        mm.then_inc(yb_filled, 1)

            @block.scalar
            def _(e):
                for ev, g in order:
                    if ev == "emb":
                        e.wait_ge(emb_filled, g + 1)
                        e.activation(ET[:, g, 0:1], cols[:, 1:2], ACT.Identity)
                        e.activation(ET[:, g, 1:T], EB[g % 2][:, 0:T - 1], ACT.Identity, bias=cols[:, 0:1])\
                            .then_inc(ET_ready, 1)
                    if ev == "txt":
                        e.wait_ge(xb_filled, g + 1)
                        e.activation(TXT[:, g, :, :].rearrange("p c s -> p (c s)"), XB[g % 2][:, 0:NC * S],
                                     ACT.Identity).then_inc(TXT_ready, 1)
                    if ev == "prod":
                        e.wait_ge(yb_filled, g + 1)
                        e.wait_ge(sum_ready, g + 1)
                        e.activation(TO[:, g, :], YB[g % 2][0:S, 0:P], ACT.Identity, scale=sums[:, g:g + 1])\
                            .then_inc(TO_ready, 1)

            @block.vector
            def _(e):
                linked, _n = chain(e, own)
                e.tensor_copy(idg[:, :], idx[:, bass.ds(r * G, G)]).then_inc(id_ready, 1)
                for ev, g in order:
                    if ev == "txt":
                        e.wait_ge(gathered[g], 16)
                        linked(e.tensor_reduce(sums[:, g:g + 1], TX[:, g, :], AX.X, ALU.add))
                        linked(e.tensor_scalar(sums[:, g:g + 1], sums[:, g:g + 1], 1e-6, P ** -0.5,
                                               ALU.add, ALU.mult))
                        e.reciprocal(sums[:, g:g + 1], sums[:, g:g + 1]).then_inc(sum_ready, 1)
                    if ev == "turn":
                        e.wait_ge(tb_filled, g + 1)
                        h = H[:, bass.ds(r * G + g, 1), :, :].rearrange("p o t c -> p (o t) c")
                        e.tensor_tensor(h, TB[g % 2][:, 0:nt * P].rearrange("p (t c) -> p t c", c=P),
                                        pos[:, :, :], ALU.add).then_inc(h_ready, 1)

        with nc.Fori(0, rounds) as r:
            with nc.Block() as block:
                one_round(block, r)
            nc.all_engine_barrier(sems_to_clear=clear)
        sems.finish()


def final_norm_phase(nc, H, hA, wb, group=4):
    geo = Geometry(197)
    nt, T, G, rounds = geo.tiles, geo.tokens, group, BATCH // group
    with ExitStack() as ctx:
        sems = Semaphores(nc, ctx)

        def sb(name, shape):
            return ctx.enter_context(nc.sbuf_tensor(f"fin_{name}", shape, F32))

        W = sb("W", [P, 2, P])
        N = sb("N", [P, G, nt, P])
        st6 = sb("st6", [P, G, nt, 6])
        mv = sb("mv", [P, G, nt, 2])
        var, rs, tmp = (sb(x, [P, G * nt]) for x in ("var", "rs", "tmp"))
        n_ready = sems.take("fin_n_ready")
        out_ready = sems.take("fin_out_ready")
        own = sems.take("fin_own")
        stored = sems.take("fin_stored")
        loaded = sems.take("fin_loaded")
        rowsA = hA.rearrange("(b t) c -> b t c", b=BATCH)
        with nc.Block() as block:
            @block.sync
            def _(e):
                e.dma_start(W[:, :, :], wb.rearrange("(o a) b -> o (a b)", o=1).to_broadcast([P, 2 * P]))\
                    .then_inc(loaded, 16)
                e.wait_ge(loaded, 16)
        with nc.Fori(0, rounds) as r:
            with nc.Block(no_gpsimd_drain=True) as block:
                @block.vector
                def _(e):
                    linked, _n = chain(e, own)

                    def h(g):
                        return H[:, bass.ds(r * G + g, 1), :, :].rearrange("p o t c -> p (o t) c")

                    for g in range(G):
                        for t in range(nt):
                            ins = e.bn_stats(st6[:, g, t, :], h(g)[:, t, :])
                    linked(ins)
                    for g in range(G):
                        for t in range(nt):
                            ins = e.bn_aggr(mv[:, g, t, :], st6[:, g, t, :])
                    linked(ins)
                    linked(e.tensor_scalar(var[:, :], mv[:, :, :, 1].rearrange("p g t -> p (g t)"), EPS, None,
                                           ALU.add))
                    rsqrt(e, linked, var[:, :], rs[:, :], tmp[:, :])
                    for g in range(G):
                        for t in range(nt):
                            ins = e.tensor_scalar(N[:, g, t, :], h(g)[:, t, :], mv[:, g, t, 0:1],
                                                  rs[:, g * nt + t:g * nt + t + 1], ALU.subtract, ALU.mult)
                        linked(ins)
                        e.tensor_tensor(N[:, g, :, :], N[:, g, :, :],
                                        W[:, 0:1, :].to_broadcast([P, nt, P]), ALU.mult).then_inc(n_ready, 1)

                @block.gpsimd
                def _(e):
                    for g in range(G):
                        e.wait_ge(n_ready, g + 1)
                        e.tensor_tensor(N[:, g, :, :], N[:, g, :, :], W[:, 1:2, :].to_broadcast([P, nt, P]),
                                        ALU.add).then_inc(out_ready, 1)

                @block.sync
                def _(e):
                    for g in range(G):
                        e.wait_ge(out_ready, g + 1)
                        to = rowsA[bass.ds(r * G + g, 1)].rearrange("o t c -> (o t) c")
                        e.dma_start(to[0:P, :], N[:, g, 0, :]).then_inc(stored, 16)
                        e.dma_start(to[P:T, :], N[geo.own[1]:P, g, 1, :]).then_inc(stored, 16)
                    e.wait_ge(stored, 32 * G)
            nc.all_engine_barrier(sems_to_clear=range(n_ready.num, stored.num + 1))
        sems.finish()


def move_phase(nc, tag, H, geo, rows, store):
    with ExitStack() as ctx:
        sems = Semaphores(nc, ctx)
        moved = sems.take(f"{tag}_moved")
        r = rows.rearrange("(b t) c -> b t c", b=BATCH)
        with nc.Block() as block:
            @block.sync
            def _(e):
                for t in range(geo.tiles):
                    s, o = geo.start[t], geo.own[t] if store else 0
                    out = r[:, s + o:s + P, :].rearrange("b p c -> p b c")
                    sb = H[o:P, :, t, :]
                    e.dma_start(*((out, sb) if store else (sb, out))).then_inc(moved, 16)
                e.wait_ge(moved, 16 * geo.tiles)
        sems.finish()


IMAGE, TEXT = 197, 77
TOKENS = IMAGE + TEXT


def build(nc, d, out):
    hA, hB, hC, hD = (nc.dram_tensor(f"h{x}", (BATCH * TOKENS, P), F32).ap() for x in "ABCD")
    flat = out.rearrange("b t c -> (b t) c")
    with ExitStack() as ctx:
        ident = ctx.enter_context(nc.sbuf_tensor("ident", [P, P], F32))
        identb = ctx.enter_context(nc.sbuf_tensor("identb", [P, P], BF16))
        ident_in = ctx.enter_context(nc.semaphore("ident_in"))
        with nc.Block() as block:
            @block.sync
            def _(e):
                e.dma_start(ident[:, :], d["ident"]).then_inc(ident_in, 16)

            @block.vector
            def _(e):
                e.wait_ge(ident_in, 16)
                e.tensor_copy(identb[:, :], ident[:, :])

        with nc.sbuf_tensor("H", [P, BATCH, 2, P], F32) as H:
            embed_phase(nc, H, hA, dict(conv=d["conv_w"], cols=d["emb_cols"], pos=d["pos"], W=d["txt_W"],
                                        idx=d["idx"], table=d["table"], vocab=d["table"].shape[0],
                                        x=d["x"]), ident)
            attention_phase(nc, "vit", H, IMAGE, 4, 4,
                            dict(qkv=d["vit_qkv"], proj=d["vit_proj"], cols=d["vit_cols"], rows=d["vit_rows"],
                                 bvm=d["vit_bvm"], fc1=d["vit_fc1"], fc2=d["vit_fc2"]), ident, identb, d["mask_image"])
            final_norm_phase(nc, H, hA, d["norm_wb"])
        with nc.sbuf_tensor("H3", [P, BATCH, 3, P], F32) as H:
            move_phase(nc, "in0", H, Geometry(TOKENS), hA, False)
            attention_phase(nc, "att", H, TOKENS, 2, 1,
                            dict(qkv=d["att_qkv"], proj=d["att_proj"], cols=d["att_cols"], rows=d["att_rows"],
                                 bvm=d["att_bvm"]),
                            ident, identb, d["mask_all"])
            move_phase(nc, "out0", H, Geometry(TOKENS), hB, True)
        ffn_phase(nc, "moe0", hB, hC, dict(experts=16, chunks=4, act=ACT.Silu, inner=True, shared=2,
                                           shared_scale=0.25, ff_chunks=4, temperature=0.7),
                  {k[5:]: v for k, v in d.items() if k.startswith("moe0_")}, ident)
        dilated_phase(nc, "dil", hC, hD, {**{k[4:]: v for k, v in d.items() if k.startswith("dil_")},
                                          "tokens": TOKENS}, ident)
        ffn_phase(nc, "moe1", hD, flat, dict(experts=8, chunks=2, act=ACT.Gelu_apprx_tanh, inner=False,
                                             temperature=1.0),
                  {k[5:]: v for k, v in d.items() if k.startswith("moe1_")}, ident)


def kernel(**inputs):
    import numpy as np
    import concourse.bacc as bacc
    from concourse.bass_utils import run_bass_kernel_spmd

    a = {k: np.asarray(v) for k, v in inputs.items()}
    t0, t1, m0, m1 = "L0_tok_", "L1_attn_", "L0_ffn_", "L1_ffn_"
    zero, one = np.zeros(P, np.float32), np.ones(P, np.float32)

    def columns(v):
        return v.reshape(-1, P).T

    def keys_mask(tokens):
        geo = Geometry(tokens)
        m = np.ones((P, geo.tiles), np.float32)
        m[:geo.own[-1], -1] = 0.0
        return m

    def value_bias(bias, tokens):
        geo = Geometry(tokens)
        rows = np.zeros((P, geo.tiles, P), np.float32)
        rows[:, :-1] = bias
        rows[geo.own[-1]:, -1] = bias
        return rows

    OFF = offsets_of(TOKENS)
    NO, STRIP = len(OFF), P // HEADS
    NS = -(-NO // STRIP)
    geo = Geometry(TOKENS)
    log_max = math.log(1.0 + 4096.0)
    omega = [x * math.pi / log_max for x in (0, 0, 1, 1, 4, 4, 6, 6)]
    cosine = np.array([[math.cos(om * math.log(1.0 + o)) if om > 0 else 0.0 for om in omega] for o in OFF],
                      np.float32)
    pb = np.zeros((3, NS * STRIP, HEADS), np.float32)
    pb[0, :NO] = a[t1 + "pos_bias"][:NO]
    pb[1, :NO] = cosine
    pb[2, :NO] = np.broadcast_to(a[t1 + "disp_amp"], (NO, HEADS))
    token = np.array([[geo.start[t] + p for t in range(geo.tiles)] for p in range(P)])
    far = np.where(token[:, :, None] >= np.array(OFF), 0.0, -1e30).astype(np.float32)
    spread = np.zeros((P, STRIP, P), np.float32)
    for i in range(STRIP):
        for h in range(HEADS):
            spread[i * HEADS + h, i, h * HD:(h + 1) * HD] = 1.0

    layers = range(4)
    d = {
        "ident": np.eye(P, dtype=np.float32),
        "x": a["x"], "idx": a["x_txt"].T, "table": a["L0_txt_word2sememe"], "txt_W": a["L0_txt_W"],
        "conv_w": a[t0 + "conv_w"], "emb_cols": np.stack([a[t0 + "conv_b"], a[t0 + "cls_token"][0, 0]], -1),
        "pos": a[t0 + "pos_embed"][0],
        "vit_qkv": a[t0 + "qkv_w"], "vit_proj": a[t0 + "proj_w"], "vit_fc1": a[t0 + "fc1_w"],
        "vit_fc2": a[t0 + "fc2_w"],
        "vit_cols": np.stack([np.stack([a[t0 + "qkv_b"][l, :P], a[t0 + "qkv_b"][l, P:2 * P], a[t0 + "ln1_w"][l],
                                        a[t0 + "ln1_b"][l], a[t0 + "ln2_w"][l], a[t0 + "ln2_b"][l],
                                        a[t0 + "fc1_b"][l, :P], a[t0 + "fc1_b"][l, P:]], -1) for l in layers]),
        "vit_rows": np.stack([np.stack([a[t0 + "proj_b"][l], a[t0 + "fc2_b"][l]]) for l in layers]),
        "vit_bvm": np.stack([value_bias(a[t0 + "qkv_b"][l, 2 * P:], IMAGE) for l in layers]),
        "mask_image": keys_mask(IMAGE), "mask_all": keys_mask(TOKENS),
        "norm_wb": np.stack([a[t0 + "norm_w"], a[t0 + "norm_b"]]),
        "att_qkv": a["L0_attn_w_qkv"].T[None], "att_proj": a["L0_attn_w_agg"].T[None],
        "att_cols": np.stack([zero, zero, one, zero, one, zero, zero, zero], -1)[None],
        "att_rows": np.stack([a["L0_attn_b_agg"], zero])[None],
        "att_bvm": value_bias(zero, TOKENS)[None],
        "moe0_w1": np.concatenate([*a[m0 + "ew1"], a[m0 + "sw1"]], 1),
        "moe0_w2": np.concatenate([*a[m0 + "ew2"], a[m0 + "sw2"]], 0),
        "moe0_b1": columns(np.concatenate([a[m0 + "eb1"].reshape(-1), a[m0 + "sb1"]])),
        "moe0_b2": np.concatenate([a[m0 + "eb2"], a[m0 + "sb2"][None]]),
        "moe0_router": a[m0 + "router_w"], "moe0_router_b": a[m0 + "router_b"][None],
        "moe0_number": np.arange(16, dtype=np.float32)[None],
        "moe0_cols": np.stack([a[m0 + "ln_in_g"], a[m0 + "ln_in_b"], a[m0 + "ff_ln_g"], a[m0 + "ff_ln_b"]], -1),
        "moe0_f1": a[m0 + "ff_w1"], "moe0_f2": a[m0 + "ff_w2"], "moe0_fb1": columns(a[m0 + "ff_b1"]),
        "moe0_fb2": a[m0 + "ff_b2"][None],
        "dil_qkv": a[t1 + "W_qkv"], "dil_gate": a[t1 + "W_gate"], "dil_out": a[t1 + "W_out"],
        "dil_cols": np.stack([*a[t1 + "b_qkv"].reshape(3, P), a[t1 + "b_gate"], np.repeat(a[t1 + "if_gain"], HD)], -1),
        "dil_b_out": a[t1 + "b_out"][None],
        "dil_scale_embed": np.tile(a[t1 + "scale_embed"][:NO].T, (HEADS, 1)),
        "dil_heads": np.repeat(np.eye(HEADS, dtype=np.float32), HD, axis=0), "dil_spread": spread,
        "dil_pb": pb.reshape(3, NS, P).transpose(2, 1, 0), "dil_mask": far,
        "moe1_w1": np.concatenate([*a[m1 + "W1"]], 1), "moe1_w2": np.concatenate([*a[m1 + "W2"]], 0),
        "moe1_b1": columns(a[m1 + "b1"].reshape(-1)), "moe1_b2": a[m1 + "b2"],
        "moe1_router": a[m1 + "Wg"], "moe1_router_b": np.zeros((1, 8), np.float32),
        "moe1_number": np.arange(8, dtype=np.float32)[None],
        "moe1_cols": np.stack([one, zero, one, zero], -1),
    }
    nc = bacc.Bacc("TRN2", target_bir_lowering=False, num_devices=1)
    arrays, aps = {}, {}
    for name, v in d.items():
        v = np.ascontiguousarray(v)
        arrays[f"in_{name}"] = v
        aps[name] = nc.dram_tensor(f"in_{name}", v.shape, mybir.dt.from_np(v.dtype), kind="ExternalInput").ap()
    out = nc.dram_tensor("out_dram", (BATCH, TOKENS, P), F32, kind="ExternalOutput").ap()
    build(nc, aps, out)
    r = run_bass_kernel_spmd(nc, [arrays], core_ids=[0])
    return r.results[0]["out_dram"]
```

```python
import math
from contextlib import ExitStack

import concourse.bass as bass
from concourse import mybir

F32 = mybir.dt.float32
BF16 = mybir.dt.bfloat16
I32 = mybir.dt.int32
ACT = mybir.ActivationFunctionType
ALU = mybir.AluOpType
AX = mybir.AxisListType

P = 128
BATCH = 32
HEADS, HD = 8, 16
SLOT = 32
EPS = 1e-5
RSQRT_MAGIC = float(0x5F3759DF)


class Semaphores:

    FIRST = 110

    def __init__(self, nc, ctx):
        self.nc, self.ctx, self.next = nc, ctx, self.FIRST

    def take(self, name):
        self.next += 1
        return self.ctx.enter_context(self.nc.semaphore(name, num=self.next - 1))

    def finish(self):
        self.nc.all_engine_barrier(sems_to_clear=range(self.FIRST, self.next))


class Geometry:

    def __init__(self, tokens):
        self.tokens = tokens
        self.tiles = -(-tokens // P)
        self.start = [t * P for t in range(self.tiles - 1)] + [tokens - P]
        self.own = [0] * (self.tiles - 1) + [P - (tokens - (self.tiles - 1) * P)]


def rsqrt(e, linked, v, y, s):
    linked(e.tensor_scalar(y.bitcast(I32), v.bitcast(I32), -0.5, RSQRT_MAGIC, ALU.mult, ALU.add))
    for _ in range(3):
        linked(e.tensor_tensor(s, y, y, ALU.mult))
        linked(e.scalar_tensor_tensor(s, s, -0.5, v, ALU.mult, ALU.mult))
        linked(e.scalar_tensor_tensor(y, s, 1.5, y, ALU.add, ALU.mult))


def chain(e, sig):
    count = [0]

    def linked(ins):
        count[0] += 1
        ins.then_inc(sig, 1)
        e.wait_ge(sig, count[0])

    return linked, count


def attention_phase(nc, tag, H, tokens, group, layers, w, ident, identb, mask_in):
    geo = Geometry(tokens)
    T, nt = tokens, geo.tiles
    G, rounds = group, BATCH // group
    N = layers * rounds
    mlp = "fc1" in w
    wide = nt * T <= 512
    jobs = [(h, list(range(nt))) for h in range(HEADS)] if wide else \
        [(h, [t]) for h in range(HEADS) for t in range(nt)]
    Jb = len(jobs)
    J = G * Jb
    JW = (nt if wide else 1) * T
    PV_LAG = 3
    SLOTS = 6
    LOADS_BEFORE = ("m", 1, 0) if wide else ("m", 0, 0)
    FIRST_S = 18 if wide else 26

    def order_of(stages, upcoming):
        tick = [[] for _ in range(J + FIRST_S + Jb * G + 40)]
        b_end = J if "B" in stages else 0
        if "A" in stages:
            for g in range(G):
                at = g * (3 if wide else 5)
                tick[at].append(("yT", g, 0))
                tick[at + 1].append(("qk", g, 0))
                tick[at + 2].append(("v", g, 0))
                tick[at + 6].append(("split", g, 0))
                tick[(at if g in (0, G - 1) else at + 4) + 6].append(("stack", g, 0))
                for j in range(g * Jb, (g + 1) * Jb):
                    tick[FIRST_S + j].append(("s", g, j))
                tick[FIRST_S + (g + 1) * Jb + 2].append(("m", g, 0))
        if "B" in stages:
            for j in range(J):
                tick[j].append(("st", j // Jb, j))
                tick[j + PV_LAG].append(("pv", j // Jb, j))
            for g in range(G):
                end = (g + 1) * Jb + PV_LAG
                tick[end - 1].append(("os", g, 0))
                tick[end + 1].append(("o", g, 0))
                tick[end + 4].append(("oT", g, 0))
                tick[end + 6].append(("proj", g, 0))
        if "C" in stages:
            for g in range(G):
                tick[11 + 5 * g].append(("y2T", g, 0))
                tick[max(b_end, 16) + 1 + 4 * g].append(("fc1", g, 0))
                tick[max(b_end, 16) + 6 + 4 * g].append(("fc2", g, 0))
                tick[8 + 2 * g].append(("z2", g, 0))
            tick[0].append(("statsC", 0, 0))
        if "A" in upcoming:
            tick[3].append(("statsA", 0, 0))
            tick[max(5 * G - 5, 8)].append(("z", 0, 0))
        if "A" in upcoming or "C" in stages:
            tick[6].append(("rsqrt", 0, 0))
        order = []
        for t in tick:
            order += t
        return order

    needs = {"yT": 1, "qk": 2, "v": 1, "m": 1, "o": 2, "oT": 1, "proj": 1, "y2T": 1, "fc1": 2, "fc2": 1}

    with ExitStack() as ctx:
        sems = Semaphores(nc, ctx)

        def sb(name, shape, dt=F32):
            return ctx.enter_context(nc.sbuf_tensor(f"{tag}_{name}", shape, dt))

        def signal(name):
            return sems.take(f"{tag}_{name}")

        Wqk = sb("Wqk", [P, 2, 2 * P])
        Wv = sb("Wv", [P, 2, P])
        bvm = sb("bvm", [P, 2, nt, P])
        colsA = sb("colsA", [P, 2, 8])
        rowp = sb("rowp", [P, 2, P])
        Wp = sb("Wp", [P, 2, P])
        if mlp:
            W1 = sb("W1", [P, 2, 2 * P])
            W2 = sb("W2", [P, 2, 2, P])
            colsC = sb("colsC", [P, 2, 8])
            rowf = sb("rowf", [P, 2, P])
        mask = sb("mask", [P, nt])
        table = sb("table", [P, 2])
        Z = sb("Z", [P, G, nt, P])
        yT = sb("yT", [P, G, T])
        qk32 = sb("qk32", [P, G, 2, T])
        rest = sb("rest", [P, G, 2, T])
        parts = sb("parts", [P, G, 2, 3, T], BF16)
        Mx = sb("Mx", [P, G, nt, HEADS])
        Mr = sb("Mr", [P, G, nt, HEADS])
        Mp = sb("Mp", [P, G, nt, 3, HEADS], BF16)
        MT = sb("MT", [3 * HEADS, G, T], BF16)
        QS = sb("QS", [P, 2, G, HEADS, T], BF16)
        KS = sb("KS", [P, 2, G, HEADS, T], BF16)
        VA = sb("VA", [P, 2, G, nt, HEADS, SLOT])
        PR = sb("PR", [P, SLOTS, JW])
        OS = sb("OS", [P, 2, T])
        RD = sb("RD", [P, 2, nt, 4])
        ON = sb("ON", [P, G, nt, P])
        OT = sb("OT", [P, G, nt, P])
        if mlp:
            Z2 = sb("Z2", [P, G, nt, P])
            y2T = sb("y2T", [P, G, T])
            hid = sb("hid", [P, 2, 2, T])
        st6 = sb("st6", [P, 2 * G * nt, 6])
        mv = sb("mv", [P, 2 * G * nt, 2])
        var = sb("var", [P, 2 * G * nt])
        rs = sb("rs", [P, 2 * G * nt])
        tmp = sb("tmp", [P, 2 * G * nt])
        banks = [ctx.enter_context(nc.psum_tensor(f"{tag}_ps{i}", [P, 512], F32)) for i in range(8)]
        SB, OB, GB = banks[0:4], banks[4:6], banks[6:8]
        scr = nc.dram_tensor(f"{tag}_scr", (G, P, 2, 3, T), BF16).ap()

        gready = [signal(f"gready{i}") for i in range(2)]
        gfree = [signal(f"gfree{i}") for i in range(2)]
        z2_ready = signal("z2_ready")
        yT_ready = signal("yT_ready")
        y2T_ready = signal("y2T_ready")
        qk_ready = signal("qk_ready")
        split1 = signal("split1")
        split2 = signal("split2")
        split3 = signal("split3")
        parts_ready = signal("parts_ready")
        spilled = [signal(f"spilled{g}") for g in range(G)]
        stacked = [signal(f"stacked{g}") for g in range(G)]
        v_ready = signal("v_ready")
        sready = [signal(f"sready{i}") for i in range(4)]
        sfree = [signal(f"sfree{i}") for i in range(4)]
        mp_ready = signal("mp_ready")
        mT_ready = signal("mT_ready")
        m_stacked = signal("m_stacked")
        pv_done = signal("pv_done")
        os_ready = signal("os_ready")
        o_turned = signal("o_turned")
        on_ready = signal("on_ready")
        oT_ready = signal("oT_ready")
        h_biased = signal("h_biased")
        h_attn = signal("h_attn")
        h2_biased = signal("h2_biased")
        h_done = signal("h_done")
        hid_ready = signal("hid_ready")
        own = signal("own")
        weights_in = signal("weights_in")
        numbers = range(gready[0].num, weights_in.num + 1)
        ready = sems.take(f"{tag}_ready")

        def group_of(r):
            return H[:, bass.ds(r * G, G), :, :]

        def weight_loads(to, stages, layers_of):
            def one(name, stage):
                return w[name][bass.ds(layers_of[stage], 1)]

            loads = []
            if "A" in stages:
                loads += [(Wqk[:, to, :], one("qkv", "A")[:, :, 0:2 * P].rearrange("o a b -> (o a) b")),
                          (Wv[:, to, :], one("qkv", "A")[:, :, 2 * P:3 * P].rearrange("o a b -> (o a) b")),
                          (bvm[:, to, :, :], one("bvm", "A").rearrange("o p t c -> (o p) t c")),
                          (colsA[:, to, :], one("cols", "A").rearrange("o a b -> (o a) b")),
                          (rowp[:, to, :], one("rows", "A")[:, 0, :].to_broadcast([P, P]))]
            if "B" in stages:
                loads += [(Wp[:, to, :], one("proj", "B").rearrange("o a b -> (o a) b"))]
            if "C" in stages:
                loads += [(W1[:, to, :], one("fc1", "C").rearrange("o a b -> (o a) b")),
                          (W2[:, to, :, :], one("fc2", "C").rearrange("o (c a) b -> (o a) c b", a=P)),
                          (colsC[:, to, :], one("cols", "C").rearrange("o a b -> (o a) b")),
                          (rowf[:, to, :], one("rows", "C")[:, 1, :].to_broadcast([P, P]))]
            return loads

        with nc.Block() as block:
            @block.vector
            def _(e):
                e.memset(KS[96:128, :, :, :, :], -1.0)
                e.memset(VA[:, :, :, :, :, :], 0.0)
                e.memset(table[:, :], 0.0)

            @block.sync
            def _(e):
                e.dma_start(mask[:, :], mask_in).then_inc(ready, 16)
                e.wait_ge(ready, 16)
        with nc.Block() as block:
            @block.vector
            def _(e):
                for b in range(2):
                    for t in range(nt):
                        e.tensor_copy(VA[:, b, :, t, :, HD],
                                      mask[:, t:t + 1].unsqueeze(2).to_broadcast([P, G, HEADS]))

        def one_round(block, stages, q, groups, upcoming, next_group, layers_of):
            order = order_of(stages, upcoming)
            use, uses = {}, 0
            for ev, g, _ in order:
                for i in range(needs.get(ev, 0)):
                    use[ev, g, i] = (uses % 2, uses // 2)
                    uses += 1
            qb = 1 - q
            scores = [x for x in order if x[0] in ("s", "st")]
            suse = {(ev, j): (u % 4, u // 4) for u, (ev, g, j) in enumerate(scores)}

            @block.sync
            def _(e):
                loads = weight_loads(1 - q, upcoming, layers_of)
                loads_at = order.index(LOADS_BEFORE if "A" in stages else order[0])
                for ev, g, j in order:
                    if ev == "split":
                        e.wait_ge(parts_ready, 2 * (g + 1))
                        e.dma_start(scr[g], parts[:, g, :, :, :]).then_inc(spilled[g], 16)
                    if ev == "stack":
                        e.wait_ge(spilled[g], 16)
                        for x, dst in ((0, QS), (1, KS)):
                            for row, part in enumerate((0, 1, 2, x, x + 1, 2 * x)):
                                e.dma_start(dst[row * HD:(row + 1) * HD, q, g, :, :],
                                            scr[g, :, x, part, :].rearrange("(h d) t -> d h t", d=HD))\
                                    .then_inc(stacked[g], 16)
                    if (ev, g, j) == order[loads_at]:
                        for dst, src in loads:
                            e.dma_start(dst, src).then_inc(weights_in, 16)
                    if ev == "m":
                        e.wait_ge(mT_ready, g + 1)
                        for p in range(3):
                            e.dma_start(QS[96 + p:97 + p, q, g, :, :], MT[p * HEADS:(p + 1) * HEADS, g, :])\
                                .then_inc(m_stacked, 16)
                if "A" in stages:
                    e.wait_ge(m_stacked, 48 * G)
                if loads:
                    e.wait_ge(weights_in, 16 * len(loads))

            def bank_of(e, key):
                b, k = use[key]
                if k > 0:
                    e.wait_ge(gfree[b], k)
                return GB[b], gready[b]

            def filled(e, key):
                b, k = use[key]
                e.wait_ge(gready[b], k + 1)
                return GB[b], gfree[b]

            @block.tensor
            def _(e):
                for ev, g, j in order:
                    if ev in ("yT", "y2T"):
                        z = Z[:, g, :, :]
                        if ev == "y2T":
                            z = Z2[:, g, :, :]
                            e.wait_ge(z2_ready, g + 1)
                        bank, done = bank_of(e, (ev, g, 0))
                        for t in range(nt):
                            mm = e.transpose(bank[:, t * P:(t + 1) * P], z[:, t, :], ident[:, :])
                        mm.then_inc(done, 1)
                    if ev == "qk":
                        e.wait_ge(yT_ready, g + 1)
                        for x in range(2):
                            bank, done = bank_of(e, (ev, g, x))
                            e.matmul(bank[:, 0:T], Wqk[:, q, x * P:(x + 1) * P], yT[:, g, :],
                                     start=True, stop=True).then_inc(done, 1)
                    if ev == "v":
                        bank, done = bank_of(e, (ev, g, 0))
                        for t in range(nt):
                            mm = e.matmul(bank[:, t * P:(t + 1) * P], yT[:, g, geo.start[t]:geo.start[t] + P],
                                          Wv[:, q, :], start=True, stop=True)
                        mm.then_inc(done, 1)
                    if ev == "s":
                        h, ts = jobs[j % Jb]
                        if j % Jb == 0:
                            e.wait_ge(stacked[g], 192)
                        b, k = suse[ev, j]
                        if k > 0:
                            e.wait_ge(sfree[b], k)
                        for i, t in enumerate(ts):
                            mm = e.matmul(SB[b][:, i * T:(i + 1) * T],
                                          QS[0:96, q, g, h, geo.start[t]:geo.start[t] + P],
                                          KS[0:96, q, g, h, :], start=True, stop=True)
                        mm.then_inc(sready[b], 1)
                    if ev == "st":
                        h, ts = jobs[j % Jb]
                        b, k = suse[ev, j]
                        if k > 0:
                            e.wait_ge(sfree[b], k)
                        for i, t in enumerate(ts):
                            mm = e.matmul(SB[b][:, i * T:(i + 1) * T],
                                          KS[0:99, qb, g, h, geo.start[t]:geo.start[t] + P],
                                          QS[0:99, qb, g, h, :], start=True, stop=True)
                        mm.then_inc(sready[b], 1)
                    if ev == "m":
                        e.wait_ge(mp_ready, g + 1)
                        bank, done = bank_of(e, (ev, g, 0))
                        bb = bank[:, :].bitcast(BF16)
                        for t in range(nt):
                            mm = e.transpose(bb[0:3 * HEADS, t * P:(t + 1) * P],
                                             Mp[:, g, t, :, :].rearrange("p a h -> p (a h)"), identb[:, :])
                        mm.then_inc(done, 1)
                    if ev == "pv":
                        h, ts = jobs[j % Jb]
                        if j % Jb == 0 and g > 0:
                            e.wait_ge(os_ready, g)
                        b, k = suse["st", j]
                        e.wait_ge(sfree[b], k + 1)
                        for i, t in enumerate(ts):
                            mm = e.matmul(OB[h // 4][SLOT * (h % 4):SLOT * (h % 4 + 1), 0:T],
                                          VA[:, qb, g, t, h, :], PR[:, j % SLOTS, i * T:(i + 1) * T],
                                          start=(t == 0), stop=(t == nt - 1))
                        mm.then_inc(pv_done, 1)
                    if ev == "o":
                        e.wait_ge(os_ready, g + 1)
                        for x in range(2):
                            bank, done = bank_of(e, (ev, g, x))
                            for t in range(nt):
                                mm = e.transpose(bank[:, t * P:(t + 1) * P],
                                                 OS[:, x, geo.start[t]:geo.start[t] + P], ident[:, :])
                            mm.then_inc(done, 1)
                        e.wait_ge(done, use[ev, g, 1][1] + 1)
                        e.sem_inc(o_turned, 1)
                    if ev == "oT":
                        e.wait_ge(on_ready, g + 1)
                        bank, done = bank_of(e, (ev, g, 0))
                        for t in range(nt):
                            mm = e.transpose(bank[:, t * P:(t + 1) * P], ON[:, g, t, :], ident[:, :])
                        mm.then_inc(done, 1)
                    if ev == "proj":
                        e.wait_ge(oT_ready, g + 1)
                        bank, done = bank_of(e, (ev, g, 0))
                        for t in range(nt):
                            mm = e.matmul(bank[:, t * P:(t + 1) * P], OT[:, g, t, :], Wp[:, q, :],
                                          start=True, stop=True)
                        mm.then_inc(done, 1)
                    if ev == "fc1":
                        e.wait_ge(y2T_ready, g + 1)
                        for x in range(2):
                            bank, done = bank_of(e, (ev, g, x))
                            e.matmul(bank[:, 0:T], W1[:, q, x * P:(x + 1) * P], y2T[:, g, :],
                                     start=True, stop=True).then_inc(done, 1)
                    if ev == "fc2":
                        e.wait_ge(hid_ready, g + 1)
                        bank, done = bank_of(e, (ev, g, 0))
                        for t in range(nt):
                            for x in range(2):
                                mm = e.matmul(bank[:, t * P:(t + 1) * P],
                                              hid[:, g % 2, x, geo.start[t]:geo.start[t] + P], W2[:, q, x, :],
                                              start=(x == 0), stop=(x == 1))
                        mm.then_inc(done, 1)

            @block.scalar
            def _(e):
                def turned(g, ev, dst, cols, wcol, bcol, ready):
                    bank, free = filled(e, (ev, g, 0))
                    for t in range(nt):
                        o = geo.own[t]
                        a = e.activation(dst[:, geo.start[t] + o:geo.start[t] + P],
                                         bank[:, t * P + o:(t + 1) * P], ACT.Identity,
                                         scale=cols[:, wcol:wcol + 1], bias=cols[:, bcol:bcol + 1])
                    a.then_inc(ready, 1)
                    e.wait_ge(ready, g + 1)
                    e.sem_inc(free, 1)

                for ev, g, j in order:
                    if ev == "yT":
                        turned(g, ev, yT[:, g, :], colsA[:, q, :], 2, 3, yT_ready)
                    if ev == "y2T":
                        turned(g, ev, y2T[:, g, :], colsC[:, q, :], 4, 5, y2T_ready)
                    if ev == "qk":
                        for x in range(2):
                            bank, free = filled(e, (ev, g, x))
                            e.activation(qk32[:, g, x, :], bank[:, 0:T], ACT.Identity,
                                         bias=colsA[:, q, x:x + 1]).then_inc(free, 1)
                        e.wait_ge(gfree[use[ev, g, 1][0]], use[ev, g, 1][1] + 1)
                        e.sem_inc(qk_ready, 1)
                    if ev == "st":
                        if j >= SLOTS:
                            e.wait_ge(pv_done, j - SLOTS + 1)
                        b, k = suse[ev, j]
                        e.wait_ge(sready[b], k + 1)
                        e.activation(PR[:, j % SLOTS, :], SB[b][:, 0:JW], ACT.Exp, scale=HD ** -0.5)\
                            .then_inc(sfree[b], 1)
                    if ev == "os":
                        e.wait_ge(pv_done, (g + 1) * Jb)
                        if g > 0:
                            e.wait_ge(o_turned, g)
                        for x in range(2):
                            a = e.activation(OS[:, x, :], OB[x][:, 0:T], ACT.Identity)
                        a.then_inc(os_ready, 1)
                    if ev == "oT":
                        bank, free = filled(e, (ev, g, 0))
                        e.activation(OT[:, g, :, :].rearrange("p t c -> p (t c)"), bank[:, 0:nt * P],
                                     ACT.Identity).then_inc(oT_ready, 1)
                        e.wait_ge(oT_ready, g + 1)
                        e.sem_inc(free, 1)
                    if ev == "fc1":
                        if g > 1:
                            b, k = use["fc2", g - 2, 0]
                            e.wait_ge(gready[b], k + 1)
                        for x in range(2):
                            bank, free = filled(e, (ev, g, x))
                            e.activation(hid[:, g % 2, x, :], bank[:, 0:T], ACT.Gelu,
                                         bias=colsC[:, q, 6 + x:7 + x]).then_inc(free, 1)
                        e.wait_ge(gfree[use[ev, g, 1][0]], use[ev, g, 1][1] + 1)
                        e.sem_inc(hid_ready, 1)
                        if g == G - 1:
                            e.activation(table[:, 1:2], table[:, 0:1], ACT.Exp)

            @block.gpsimd
            def _(e):
                if "A" in stages:
                    hA = group_of(groups["A"])
                if "C" in stages:
                    hC = group_of(groups["C"])
                for ev, g, j in order:
                    if ev == "qk":
                        e.wait_ge(qk_ready, g + 1)
                        for x in range(2):
                            e.tensor_copy(parts[:, g, x, 2 * x, :], qk32[:, g, x, :]).then_inc(split1, 1)
                        for x in range(2):
                            e.wait_ge(split1, 2 * g + 1 + x)
                            e.tensor_tensor(rest[:, g, x, :], qk32[:, g, x, :], parts[:, g, x, 2 * x, :],
                                            ALU.subtract).then_inc(split2, 1)
                        e.wait_ge(split2, 2 * g + 2)
                        e.tensor_copy(parts[:, g, :, 1, :], rest[:, g, :, :]).then_inc(split3, 1)
                    if ev == "split":
                        e.tensor_tensor(hA[:, g, :, :], hA[:, g, :, :],
                                        rowp[:, q:q + 1, :].to_broadcast([P, nt, P]), ALU.add)\
                            .then_inc(h_biased, 1)
                    if ev == "y2T":
                        e.wait_ge(z2_ready, g + 1)
                        e.tensor_tensor(hC[:, g, :, :], hC[:, g, :, :],
                                        rowf[:, q:q + 1, :].to_broadcast([P, nt, P]), ALU.add)\
                            .then_inc(h2_biased, 1)
                if "A" in stages:
                    e.wait_ge(h_biased, G)

            @block.vector
            def _(e):
                linked, links = chain(e, own)
                hs = {s: group_of(groups[s]) for s in stages}

                slots = {"A": 0, "C": G * nt}

                def statistics(h, k):
                    for i in range(G * nt):
                        ins = e.bn_stats(st6[:, k + i, :], h[:, i // nt, i % nt, :])
                    linked(ins)
                    for i in range(G * nt):
                        ins = e.bn_aggr(mv[:, k + i, :], st6[:, k + i, :])
                    linked(ins)

                def normalised(h, k, g, out):
                    for t in range(nt):
                        i = k + g * nt + t
                        ins = e.tensor_scalar(out[:, t, :], h[:, g, t, :], mv[:, i, 0:1], rs[:, i:i + 1],
                                              ALU.subtract, ALU.mult)
                    return ins

                for ev, g, j in order:
                    if ev == "statsC":
                        statistics(hs["C"], slots["C"])
                    if ev == "statsA":
                        statistics(group_of(next_group), slots["A"])
                    if ev == "rsqrt":
                        k0 = 0 if "A" in upcoming else slots["C"]
                        k1 = slots["C"] + G * nt if "C" in stages else G * nt
                        linked(e.tensor_scalar(var[:, k0:k1], mv[:, k0:k1, 1], EPS, None, ALU.add))
                        rsqrt(e, linked, var[:, k0:k1], rs[:, k0:k1], tmp[:, k0:k1])
                    if ev == "z":
                        if "A" in stages:
                            e.wait_ge(yT_ready, G)
                        for i in range(G):
                            normalised(group_of(next_group), slots["A"], i, Z[:, i, :, :])
                    if ev == "z2":
                        normalised(hs["C"], slots["C"], g, Z2[:, g, :, :]).then_inc(z2_ready, 1)
                    if ev == "split":
                        e.wait_ge(split3, g + 1)
                        for x in range(2):
                            e.tensor_tensor(parts[:, g, x, 2 - 2 * x, :], rest[:, g, x, :], parts[:, g, x, 1, :],
                                            ALU.subtract).then_inc(parts_ready, 1)
                    if ev == "v":
                        bank, free = filled(e, (ev, g, 0))
                        for t in range(nt):
                            ins = e.scalar_tensor_tensor(
                                VA[:, q, g, t, :, 0:HD],
                                bank[:, t * P:(t + 1) * P].rearrange("p (h d) -> p h d", d=HD),
                                mask[:, t:t + 1], bvm[:, q, t, :].rearrange("p (h d) -> p h d", d=HD),
                                ALU.mult, ALU.add)
                        ins.then_inc(free, 1)
                    if ev == "s":
                        h, ts = jobs[j % Jb]
                        b, k = suse[ev, j]
                        e.wait_ge(sready[b], k + 1)
                        e.tensor_reduce(Mx[:, g, ts[0]:ts[-1] + 1, h],
                                        SB[b][:, 0:JW].rearrange("p (t k) -> p t k", k=T),
                                        AX.X, ALU.max).then_inc(sfree[b], 1)
                        if j % Jb == Jb - 1:
                            e.wait_ge(sfree[b], k + 1)
                            linked(e.tensor_copy(Mp[:, g, :, 0, :], Mx[:, g, :, :]))
                            linked(e.tensor_tensor(Mr[:, g, :, :], Mx[:, g, :, :], Mp[:, g, :, 0, :], ALU.subtract))
                            linked(e.tensor_copy(Mp[:, g, :, 1, :], Mr[:, g, :, :]))
                            e.tensor_tensor(Mp[:, g, :, 2, :], Mr[:, g, :, :], Mp[:, g, :, 1, :],
                                            ALU.subtract).then_inc(mp_ready, 1)
                    if ev == "m":
                        bank, free = filled(e, (ev, g, 0))
                        bb = bank[:, :].bitcast(BF16)
                        for t in range(nt):
                            o = geo.own[t]
                            ins = e.tensor_copy(MT[:, g, geo.start[t] + o:geo.start[t] + P],
                                                bb[0:3 * HEADS, t * P + o:(t + 1) * P])
                        ins.then_inc(mT_ready, 1)
                        e.wait_ge(mT_ready, g + 1)
                        e.sem_inc(free, 1)
                    if ev == "o":
                        for x in range(2):
                            bank, free = filled(e, (ev, g, x))
                            o4 = bank[:, 0:nt * P].rearrange("p (t h s) -> p t h s", t=nt, s=SLOT)
                            linked(e.reciprocal(RD[:, x, :, :], o4[:, :, :, HD]))
                            e.tensor_tensor(
                                ON[:, g, :, x * 64:(x + 1) * 64].rearrange("p t (h d) -> p t h d", d=HD),
                                o4[:, :, :, 0:HD], RD[:, x, :, :].unsqueeze(3).to_broadcast([P, nt, 4, HD]),
                                ALU.mult).then_inc(free, 1)
                        b, k = use[ev, g, 1]
                        e.wait_ge(gfree[b], k + 1)
                        e.sem_inc(on_ready, 1)
                    if ev == "proj":
                        bank, free = filled(e, (ev, g, 0))
                        e.tensor_tensor(hs["B"][:, g, :, :], bank[:, 0:nt * P].rearrange("p (t c) -> p t c", c=P),
                                        hs["B"][:, g, :, :], ALU.add).then_inc(free, 1)
                    if ev == "fc2":
                        e.wait_ge(h2_biased, g + 1)
                        bank, free = filled(e, (ev, g, 0))
                        e.tensor_tensor(hs["C"][:, g, :, :], bank[:, 0:nt * P].rearrange("p (t c) -> p t c", c=P),
                                        hs["C"][:, g, :, :], ALU.add).then_inc(free, 1)

        def in_flight(n):
            return ("A" if 0 <= n < N else "") + ("B" if 0 <= n - 1 < N else "") + ("C" if mlp and 0 <= n - 2 < N else "")

        def round_at(n, stages, q, upcoming):
            groups = {"A": (n + 2) % rounds, "B": (n + 1) % rounds, "C": n % rounds}
            next_group = (n + 3) % rounds
            layers_of = {"A": (n + 3) // rounds % layers, "B": (n + 2) // rounds % layers,
                         "C": (n + 1) // rounds % layers}
            with nc.Block(no_gpsimd_drain=True) as block:
                one_round(block, stages, q, groups, upcoming, next_group, layers_of)
            nc.all_engine_barrier(sems_to_clear=numbers)

        for n in (-1, 0, 1):
            round_at(n - 2, in_flight(n), n % 2, in_flight(n + 1))
        with nc.Fori(0, N // 2 - 1) as i:
            for p in range(2):
                stages = "ABC" if mlp else "AB"
                round_at(i * 2 + p, stages, p, stages)
        for n in (N, N + 1):
            if in_flight(n):
                round_at(n - 2, in_flight(n), n % 2, in_flight(n + 1))
        sems.finish()


def ffn_phase(nc, tag, src, dst, cfg, w, ident):
    E, chunks, act, act_ff = cfg["experts"], cfg["chunks"], cfg["act"], cfg.get("ff_chunks", 0)
    shared = cfg.get("shared", 0)
    inner, ffc = cfg["inner"], cfg.get("ff_chunks", 0)
    units = [(e * chunks, chunks) for e in range(E)] + ([(E * chunks, shared)] if shared else [])
    K = E + (1 if shared else 0)
    NCH = sum(n for _, n in units)
    tokens = src.shape[0]
    GT = 4
    full = tokens // (GT * P)
    left = tokens - full * GT * P
    assert 0 < left <= P

    with ExitStack() as ctx:
        sems = Semaphores(nc, ctx)

        def sb(name, shape, dt=F32):
            return ctx.enter_context(nc.sbuf_tensor(f"{tag}_{name}", shape, dt))

        def signal(name):
            return sems.take(f"{tag}_{name}")

        W1 = sb("W1", [P, NCH * P])
        W2 = sb("W2", [P, NCH, P])
        B1 = sb("B1", [P, NCH])
        WR = sb("WR", [P, E])
        RB = sb("RB", [P, E])
        B2 = sb("B2", [K, P])
        col = sb("col", [P, 4])
        if ffc:
            F1 = sb("F1", [P, ffc * P])
            F2 = sb("F2", [P, ffc, P])
            FB1 = sb("FB1", [P, ffc])
            FB2 = sb("FB2", [P, P])
        number = sb("number", [P, E])
        X = sb("X", [P, full * GT + 1, P])
        Y = sb("Y", [P, GT, P])
        Z = sb("Z", [P, GT, P])
        if ffc:
            Z2 = sb("Z2", [P, GT, P])
        yT = sb("yT", [P, GT * P])
        lg = sb("lg", [P, GT, E])
        pe_ = sb("expd", [P, GT, E])
        gate = sb("gate", [P, GT, E])
        comb = sb("comb", [P, GT, K])
        pick = sb("pick", [P, GT, E])
        top = sb("top", [P, GT, 8])
        topi = sb("topi", [P, GT, 8], mybir.dt.uint32)
        topf = sb("topf", [P, GT, 2])
        big = sb("big", [P, GT])
        tot = sb("tot", [P, GT])
        combT = sb("combT", [K, GT * P])
        hid = sb("hid", [P, 2, max(chunks, ffc), GT * P])
        acc = sb("acc", [P, GT, P])
        out = sb("out", [P, GT, P])
        st6 = sb("st6", [P, GT, 6])
        mv = sb("mv", [P, GT, 2])
        var = sb("var", [P, GT])
        rs = sb("rs", [P, GT])
        tmp = sb("tmp", [P, GT])
        banks = [ctx.enter_context(nc.psum_tensor(f"{tag}_ps{i}", [P, 512], F32)) for i in range(8)]
        HB, YB, GB = banks[0:4], banks[4:6], banks[6]

        first = signal("first")
        z2_ready = signal("z2_ready")
        gready = signal("gready")
        gfree = signal("gfree")
        yT_ready = signal("yT_ready")
        lg_ready = signal("lg_ready")
        e_ready = signal("e_ready")
        comb_ready = signal("comb_ready")
        cT_ready = signal("cT_ready")
        h_filled = signal("h_filled")
        h_ready = signal("h_ready")
        y_filled = signal("y_filled")
        y_added = signal("y_added")
        x_ready = signal("x_ready")
        out_ready = signal("out_ready")
        own = signal("own")
        numbers = range(first.num, own.num + 1)
        loaded = sems.take(f"{tag}_loaded")
        stored = sems.take(f"{tag}_stored")

        loads = [(X[:, 0:full * GT, :], src[0:full * GT * P, :].rearrange("(t p) c -> p t c", p=P)),
                 (X[0:left, full * GT, :], src[full * GT * P:tokens, :]),
                 (W1[:, :], w["w1"]), (W2[:, :, :], w["w2"].rearrange("(k p) c -> p k c", p=P)),
                 (B1[:, :], w["b1"]), (WR[:, :], w["router"]), (RB[:, :], w["router_b"].to_broadcast([P, E])),
                 (B2[:, :], w["b2"]), (number[:, :], w["number"].to_broadcast([P, E])),
                 (col[:, :], w["cols"])]
        if ffc:
            loads += [(F1[:, :], w["f1"]), (F2[:, :, :], w["f2"].rearrange("(k p) c -> p k c", p=P)),
                      (FB1[:, :], w["fb1"]), (FB2[:, :], w["fb2"].to_broadcast([P, P]))]

        with nc.Block() as block:
            @block.sync
            def _(e):
                for to, fr in loads:
                    e.dma_start(to, fr).then_inc(loaded, 16)
                e.wait_ge(loaded, 16 * len(loads))

            @block.vector
            def _(e):
                if shared:
                    e.memset(comb[:, :, E:K], cfg["shared_scale"])

        def rows_of(r, nt, rows):
            if isinstance(r, int):
                return X[0:rows, GT * r:GT * r + nt, :]
            return X[0:rows, bass.ds(r * GT, nt), :]

        def normalise(e, linked, x, y, nt, rows):
            for t in range(nt):
                ins = e.bn_stats(st6[0:rows, t, :], x[:, t, :])
            linked(ins)
            for t in range(nt):
                ins = e.bn_aggr(mv[0:rows, t, :], st6[0:rows, t, :])
            linked(ins)
            linked(e.tensor_scalar(var[0:rows, 0:nt], mv[0:rows, 0:nt, 1], EPS, None, ALU.add))
            rsqrt(e, linked, var[0:rows, 0:nt], rs[0:rows, 0:nt], tmp[0:rows, 0:nt])
            for t in range(nt):
                ins = e.tensor_scalar(y[0:rows, t, :], x[:, t, :], mv[0:rows, t, 0:1],
                                      rs[0:rows, t:t + 1], ALU.subtract, ALU.mult)
            return ins

        def head(e, linked, r, nt, rows):
            if inner:
                linked(normalise(e, linked, rows_of(r, nt, rows), Y, nt, rows))
                linked(normalise(e, linked, Y[0:rows, 0:nt, :], Z, nt, rows))
            else:
                linked(normalise(e, linked, rows_of(r, nt, rows), Z, nt, rows))

        def one_round(block, r, nt, rows, following):
            N = (nt - 1) * P + rows
            steps = []
            for u in range(len(units)):
                steps.append(("up", u))
                if u:
                    steps.append(("down", u - 1))
            steps.append(("down", len(units) - 1))
            hb_count = {}
            k = 0
            for u, (_, n) in enumerate(units):
                hb_count[u] = k
                k += n
            U = len(units)
            hb_count[U] = k

            def x_of():
                return rows_of(r, nt, rows)

            def chunk_list(u):
                return units[u] if u < U else (0, ffc)

            @block.tensor
            def _(e):
                use = [0]

                def general():
                    if use[0] > 0:
                        e.wait_ge(gfree, use[0])
                    use[0] += 1

                def turn(z):
                    general()
                    for t in range(nt):
                        mm = e.transpose(GB[:, t * P:t * P + rows], z[0:rows, t, :], ident[0:rows, 0:rows])
                    mm.then_inc(gready, 1)

                def up(u):
                    w1 = W1 if u < U else F1
                    at, n = chunk_list(u)
                    for c in range(n):
                        k = hb_count[u] + c
                        if k > 3:
                            e.wait_ge(h_ready, k - 3)
                        e.matmul(HB[k % 4][:, 0:N], w1[:, (at + c) * P:(at + c + 1) * P], yT[:, 0:N],
                                 start=True, stop=True).then_inc(h_filled, 1)

                def down(u):
                    w2 = W2 if u < U else F2
                    at, n = chunk_list(u)
                    e.wait_ge(h_ready, hb_count[u] + n)
                    if u > 1:
                        e.wait_ge(y_added, u)
                    for t in range(nt):
                        for c in range(n):
                            mm = e.matmul(YB[u % 2][0:rows, t * P:(t + 1) * P],
                                          hid[:, u % 2, c, t * P:t * P + rows], w2[:, at + c, :],
                                          start=(c == 0), stop=(c == n - 1))
                    mm.then_inc(y_filled, 1)

                turn(Z)
                e.wait_ge(yT_ready, 1)
                general()
                for t in range(nt):
                    mm = e.matmul(GB[0:rows, t * E:(t + 1) * E], yT[:, t * P:t * P + rows], WR[:, :],
                                  start=True, stop=True)
                mm.then_inc(gready, 1)
                for n, (what, u) in enumerate(steps):
                    if n == 3:
                        e.wait_ge(comb_ready, 1)
                        general()
                        for t in range(nt):
                            mm = e.transpose(GB[0:K, t * P:t * P + rows], comb[0:rows, t, :],
                                             ident[0:rows, 0:rows])
                        mm.then_inc(gready, 1)
                        e.wait_ge(cT_ready, 1)
                        general()
                        for t in range(nt):
                            mm = e.matmul(GB[0:rows, t * P:(t + 1) * P], combT[:, t * P:t * P + rows],
                                          B2[:, :], start=True, stop=True)
                        mm.then_inc(gready, 1)
                    (up if what == "up" else down)(u)
                if ffc:
                    e.wait_ge(z2_ready, 1)
                    turn(Z2)
                    e.wait_ge(yT_ready, 2)
                    up(U)
                    down(U)

            @block.scalar
            def _(e):
                def turned(count, use, c0):
                    e.wait_ge(gready, use)
                    if count == 2:
                        e.wait_ge(h_filled, hb_count[U])
                    if inner or count == 2:
                        ins = e.activation(yT[:, 0:N], GB[:, 0:N], ACT.Identity,
                                           scale=col[:, c0:c0 + 1], bias=col[:, c0 + 1:c0 + 2])
                    else:
                        ins = e.activation(yT[:, 0:N], GB[:, 0:N], ACT.Identity)
                    ins.then_inc(yT_ready, 1)
                    e.wait_ge(yT_ready, count)
                    e.sem_inc(gfree, 1)

                def hidden(u):
                    b1 = B1 if u < U else FB1
                    at, n = chunk_list(u)
                    if u > 1:
                        e.wait_ge(y_filled, u - 1)
                    for c in range(n):
                        k = hb_count[u] + c
                        e.wait_ge(h_filled, k + 1)
                        e.activation(hid[:, u % 2, c, 0:N], HB[k % 4][:, 0:N], act,
                                     bias=b1[:, at + c:at + c + 1]).then_inc(h_ready, 1)

                turned(1, 1, 0)
                e.wait_ge(lg_ready, 1)
                e.activation(pe_[0:rows, 0:nt, :], lg[0:rows, 0:nt, :], ACT.Exp,
                             scale=1.0 / cfg["temperature"]).then_inc(e_ready, 1)
                hidden(0)
                hidden(1)
                e.wait_ge(gready, 3)
                e.activation(combT[:, 0:N], GB[0:K, 0:N], ACT.Identity).then_inc(cT_ready, 1)
                e.wait_ge(cT_ready, 1)
                e.sem_inc(gfree, 1)
                for u in range(2, U):
                    hidden(u)
                if ffc:
                    turned(2, 5, 2)
                    hidden(U)

            @block.gpsimd
            def _(e):
                if inner:
                    e.tensor_tensor(out[0:rows, 0:nt, :], x_of(), Y[0:rows, 0:nt, :], ALU.add)\
                        .then_inc(x_ready, 1)
                    e.wait_ge(x_ready, 1)
                    e.tensor_tensor(out[0:rows, 0:nt, :], out[0:rows, 0:nt, :],
                                    FB2[0:rows, :].unsqueeze(1).to_broadcast([rows, nt, P]), ALU.add)\
                        .then_inc(x_ready, 1)

            @block.vector
            def _(e):
                linked, _n = chain(e, own)

                L, G_, C, PK = (a[0:rows, 0:nt, :] for a in (lg, gate, comb, pick))
                e.wait_ge(gready, 2)
                linked(e.tensor_tensor(L, GB[0:rows, 0:nt * E].rearrange("p (t e) -> p t e", e=E),
                                       RB[0:rows, :].unsqueeze(1).to_broadcast([rows, nt, E]), ALU.add))
                e.sem_inc(gfree, 1)
                linked(e.tensor_reduce(big[0:rows, 0:nt], L, AX.X, ALU.max))
                e.tensor_tensor(L, L, big[0:rows, 0:nt].unsqueeze(2).to_broadcast([rows, nt, E]),
                                ALU.subtract).then_inc(lg_ready, 1)
                e.wait_ge(e_ready, 1)
                linked(e.tensor_reduce(tot[0:rows, 0:nt], pe_[0:rows, 0:nt, :], AX.X, ALU.add))
                linked(e.reciprocal(tot[0:rows, 0:nt], tot[0:rows, 0:nt]))
                linked(e.tensor_tensor(G_, pe_[0:rows, 0:nt, :],
                                       tot[0:rows, 0:nt].unsqueeze(2).to_broadcast([rows, nt, E]), ALU.mult))
                for t in range(nt):
                    ins = e.max(top[0:rows, t, :], gate[0:rows, t, :])
                linked(ins)
                for t in range(nt):
                    ins = e.max_index(topi[0:rows, t, :], top[0:rows, t, :], gate[0:rows, t, :])
                linked(ins)
                linked(e.tensor_copy(topf[0:rows, 0:nt, :], topi[0:rows, 0:nt, 0:2]))
                nb = number[0:rows, :].unsqueeze(1).to_broadcast([rows, nt, E])
                for i in range(2):
                    linked(e.tensor_tensor(PK if i == 0 else L, nb,
                                           topf[0:rows, 0:nt, i:i + 1].to_broadcast([rows, nt, E]),
                                           ALU.is_equal))
                linked(e.tensor_tensor(PK, PK, L, ALU.add))
                e.tensor_tensor(comb[0:rows, 0:nt, 0:E], PK, G_, ALU.mult).then_inc(comb_ready, 1)
                e.wait_ge(gready, 4)
                e.wait_ge(comb_ready, 1)
                e.tensor_copy(acc[0:rows, 0:nt, :],
                              GB[0:rows, 0:nt * P].rearrange("p (t c) -> p t c", c=P)).then_inc(y_added, 1)
                e.wait_ge(y_added, 1)
                e.sem_inc(gfree, 1)
                for u in range(U):
                    e.wait_ge(y_filled, u + 1)
                    e.wait_ge(y_added, u + 1)
                    for t in range(nt):
                        ins = e.scalar_tensor_tensor(acc[0:rows, t, :], YB[u % 2][0:rows, t * P:(t + 1) * P],
                                                     comb[0:rows, t, u:u + 1], acc[0:rows, t, :],
                                                     ALU.mult, ALU.add)
                    ins.then_inc(y_added, 1)
                    if u == U // 2 and following:
                        e.wait_ge(yT_ready, 1)
                        if inner:
                            e.wait_ge(x_ready, 1)
                        head(e, linked, *following)
                e.wait_ge(y_added, U + 1)
                if ffc:
                    normalise(e, linked, acc[0:rows, 0:nt, :], Z2, nt, rows).then_inc(z2_ready, 1)
                    e.wait_ge(x_ready, 2)
                    linked(e.tensor_tensor(out[0:rows, 0:nt, :], out[0:rows, 0:nt, :], acc[0:rows, 0:nt, :], ALU.add))
                    e.wait_ge(y_filled, U + 1)
                    e.tensor_tensor(out[0:rows, 0:nt, :],
                                    YB[U % 2][0:rows, 0:nt * P].rearrange("p (t c) -> p t c", c=P),
                                    out[0:rows, 0:nt, :], ALU.add).then_inc(out_ready, 1)
                else:
                    e.tensor_tensor(out[0:rows, 0:nt, :], acc[0:rows, 0:nt, :], x_of(), ALU.add)\
                        .then_inc(out_ready, 1)

            @block.sync
            def _(e):
                e.wait_ge(out_ready, 1)
                if nt == 1:
                    to = dst[GT * P * r:GT * P * r + N, :]
                    e.dma_start(to, out[0:rows, 0, :]).then_inc(stored, 16)
                else:
                    to = dst[bass.ds(r * (GT * P), GT * P), :].rearrange("(t p) c -> p t c", p=P)
                    e.dma_start(to, out[:, :, :]).then_inc(stored, 16)
                e.wait_ge(stored, 16)

        clear = range(min(numbers[0], stored.num), max(numbers[-1], stored.num) + 1)
        with nc.Block() as block:
            @block.vector
            def _(e):
                linked, _n = chain(e, own)
                head(e, linked, 0, GT, P)
        nc.all_engine_barrier(sems_to_clear=clear)
        with nc.Fori(0, full - 1) as r:
            with nc.Block(no_gpsimd_drain=True) as block:
                one_round(block, r, GT, P, (r + 1, GT, P))
            nc.all_engine_barrier(sems_to_clear=clear)
        for last, nt, rows, following in ((full - 1, GT, P, (full, 1, left)), (full, 1, left, None)):
            with nc.Block(no_gpsimd_drain=True) as block:
                one_round(block, last, nt, rows, following)
            nc.all_engine_barrier(sems_to_clear=clear)
        sems.finish()


def offsets_of(tokens):
    far = (48, 64, 96, 128, 192, 256, 384, 512, 768, 1024)
    return [o for o in list(range(33)) + list(far) if o < tokens]


def dilated_phase(nc, tag, src, dst, w, ident, group=4):
    T = w["tokens"]
    geo = Geometry(T)
    nt = geo.tiles
    OFF = offsets_of(T)
    NO = len(OFF)
    STRIP = P // HEADS
    NS = -(-NO // STRIP)
    PAD = OFF[-1]
    G, rounds = group, BATCH // group
    KO = NO * HEADS
    PAIRS = -(-NO // 2)
    ADDED = NO // 2

    with ExitStack() as ctx:
        sems = Semaphores(nc, ctx)

        def sb(name, shape, dt=F32):
            return ctx.enter_context(nc.sbuf_tensor(f"{tag}_{name}", shape, dt))

        def signal(name):
            return sems.take(f"{tag}_{name}")

        Wqkvg = sb("Wqkvg", [P, 4, P])
        Wo = sb("Wo", [P, P])
        cols = sb("cols", [P, 8])
        bo = sb("bo", [P, P])
        se = sb("se", [P, NO])
        heads = sb("heads", [P, HEADS])
        sel = sb("sel", [P, NO, P])
        spread = sb("spread", [P, STRIP, P])
        pb = sb("pb", [P, NS, 3])
        eff = sb("eff", [P, NS])
        mask = sb("mask", [P, nt, NO])
        X = sb("X", [P, BATCH, nt, P])
        Z = sb("Z", [P, G, nt, P])
        yT = sb("yT", [P, G, T])
        q = sb("q", [P, G, T])
        kpad = sb("kpad", [P, G, PAD + T])
        vpad = sb("vpad", [P, G, PAD + T])
        gt = sb("gt", [P, G, T])
        PR = sb("PR", [P, 4, T])
        SC = sb("SC", [P, NS, T])
        sm = sb("sm", [P, nt, NS * P])
        big = sb("big", [P, nt, HEADS])
        tot = sb("tot", [P, nt, HEADS])
        AT = sb("AT", [P, G, NS, T])
        AV = sb("AV", [P, 3, 2, T])
        og = sb("og", [P, G, T])
        out = sb("out", [P, G, nt, P])
        st6 = sb("st6", [P, G, nt, 6])
        mv = sb("mv", [P, G, nt, 2])
        var = sb("var", [P, G * nt])
        rs = sb("rs", [P, G * nt])
        tmp = sb("tmp", [P, G * nt])
        banks = [ctx.enter_context(nc.psum_tensor(f"{tag}_ps{i}", [P, 512], F32)) for i in range(8)]
        SB, GB, BB, AB = banks[0:3], banks[3:5], banks[5:7], banks[7]

        order = [("ln", g, 0) for g in range(G)]
        order += [(ev, g, 0) for g in range(G) for ev in ("yT", "qkv")]
        for g in range(G):
            for i in range(NO):
                order.append(("sc", g, i))
                if g and i in (4, 14, 20):
                    order.append((("soft", "norm", "AT")[(4, 14, 20).index(i)], g - 1, 0))
            order.append(("strips", g, 0))
        for g in range(G):
            for i in range(NO):
                order.append(("pv", g, i))
                if g == 0 and G > 1 and i in (4, 14, 20):
                    order.append((("soft", "norm", "AT")[(4, 14, 20).index(i)], G - 1, 0))
            order.append(("gated", g, 0))
            order.append(("proj", g, 0))

        needs = {"yT": 1, "qkv": 4, "soft": nt, "AT": NS, "proj": 1}
        use, uses = {}, 0
        for ev, g, _ in order:
            for i in range(needs.get(ev, 0)):
                use[ev, g, i] = (uses % 2, uses // 2)
                uses += 1

        gready = [signal(f"gready{i}") for i in range(2)]
        gfree = [signal(f"gfree{i}") for i in range(2)]
        z_ready = signal("z_ready")
        yT_ready = signal("yT_ready")
        qkv_ready = signal("qkv_ready")
        prod_ready = signal("prod_ready")
        prod_used = signal("prod_used")
        SC_ready = signal("SC_ready")
        lg_ready = signal("lg_ready")
        e_ready = signal("e_ready")
        A_ready = signal("A_ready")
        AT_ready = signal("AT_ready")
        b_ready = signal("b_ready")
        av_ready = signal("av_ready")
        pair_ready = signal("pair_ready")
        av_used = signal("av_used")
        og_ready = signal("og_ready")
        x_ready = signal("x_ready")
        out_ready = signal("out_ready")
        own = signal("own")
        numbers = range(gready[0].num, own.num + 1)
        stored = sems.take(f"{tag}_stored")
        clear = range(numbers[0], stored.num + 1)
        loaded = sems.take(f"{tag}_loaded")
        built = sems.take(f"{tag}_built")

        srcb = src.rearrange("(b t) c -> b t c", b=BATCH)
        dstb = dst.rearrange("(b t) c -> b t c", b=BATCH)
        loads = [(X[:, :, t, :], srcb[:, geo.start[t]:geo.start[t] + P, :].rearrange("b p c -> p b c"))
                 for t in range(nt)]
        loads += [(Wqkvg[:, 0:3, :], w["qkv"].rearrange("a (x b) -> a x b", x=3)), (Wqkvg[:, 3, :], w["gate"]),
                  (Wo[:, :], w["out"]), (cols[:, 0:5], w["cols"]), (bo[:, :], w["b_out"].to_broadcast([P, P])),
                  (se[:, :], w["scale_embed"]), (heads[:, :], w["heads"]), (spread[:, :, :], w["spread"]),
                  (pb[:, :, :], w["pb"]), (mask[:, :, :], w["mask"])]
        with nc.Block() as block:
            @block.sync
            def _(e):
                for to, fr in loads:
                    e.dma_start(to, fr).then_inc(loaded, 16)
                e.wait_ge(loaded, 16 * len(loads))

            @block.vector
            def _(e):
                e.memset(kpad[:, :, 0:PAD], 0.0)
                e.memset(vpad[:, :, 0:PAD], 0.0)
                e.memset(sm[:, :, :], 0.0)
                e.memset(sel[:, :, :], 0.0).then_inc(built, 1)
                e.wait_ge(loaded, 16 * len(loads))
                e.tensor_scalar(cols[:, 5:7], cols[:, 3:5], 0.5, None, ALU.mult)
                e.tensor_scalar(se[:, :], se[:, :], 1.0, HD ** -0.5, ALU.add, ALU.mult).then_inc(built, 1)
                e.tensor_tensor(eff[:, :], pb[:, :, 1], pb[:, :, 2], ALU.mult).then_inc(built, 1)
                e.wait_ge(built, 3)
                e.tensor_tensor(eff[:, :], eff[:, :], pb[:, :, 0], ALU.add)
                for i in range(NO):
                    at = (i % STRIP) * HEADS
                    e.tensor_scalar(sel[:, i, at:at + HEADS], heads[:, :], se[:, i:i + 1], None, ALU.mult)

        def one_round(block, r):
            def xb(g):
                return X[:, bass.ds(r * G + g, 1), :, :].rearrange("p o t c -> p (o t) c")

            def cut(i):
                return 0 if i % STRIP == 0 else OFF[i]

            def filled(e, key):
                b, k = use[key]
                e.wait_ge(gready[b], k + 1)
                return GB[b], gfree[b]

            @block.tensor
            def _(e):
                def bank_of(key):
                    b, k = use[key]
                    if k > 0:
                        e.wait_ge(gfree[b], k)
                    return GB[b], gready[b]

                def add_up(g, pair):
                    if pair < ADDED:
                        e.wait_ge(pair_ready, g * ADDED + pair + 1)
                    else:
                        e.wait_ge(av_ready, (g + 1) * NO)
                    if pair == 0 and g > 0:
                        e.wait_ge(og_ready, g)
                    c = OFF[2 * pair]
                    e.matmul(AB[:, c:T], ident[:, :], AV[:, (g * PAIRS + pair) % 3, 0, c:T],
                             start=(pair == 0), stop=(pair == PAIRS - 1),
                             skip_group_check=True).then_inc(av_used, 1)

                for ev, g, i in order:
                    if ev == "yT":
                        e.wait_ge(z_ready, g + 1)
                        bank, done = bank_of((ev, g, 0))
                        for t in range(nt):
                            mm = e.transpose(bank[:, t * P:(t + 1) * P], Z[:, g, t, :], ident[:, :])
                        mm.then_inc(done, 1)
                    if ev == "qkv":
                        e.wait_ge(yT_ready, g + 1)
                        for x in range(4):
                            bank, done = bank_of((ev, g, x))
                            e.matmul(bank[:, 0:T], Wqkvg[:, x, :], yT[:, g, :], start=True, stop=True)\
                                .then_inc(done, 1)
                    if ev == "sc":
                        j = g * NO + i
                        e.wait_ge(prod_ready, j + 1)
                        if i == 0:
                            if g > 0:
                                e.wait_ge(SC_ready, g)
                        c = cut(i)
                        e.matmul(SB[i // STRIP][:, c:T], sel[:, i, :], PR[:, j % 4, c:T],
                                 start=(i % STRIP == 0), stop=(i % STRIP == STRIP - 1 or i == NO - 1),
                                 skip_group_check=True).then_inc(prod_used, 1)
                    if ev == "soft":
                        e.wait_ge(SC_ready, g + 1)
                        for t in range(nt):
                            bank, done = bank_of((ev, g, t))
                            for s in range(NS):
                                mm = e.transpose(bank[:, s * P:(s + 1) * P],
                                                 SC[:, s, geo.start[t]:geo.start[t] + P], ident[:, :])
                            mm.then_inc(done, 1)
                    if ev == "AT":
                        e.wait_ge(A_ready, g + 1)
                        for s in range(NS):
                            bank, done = bank_of((ev, g, s))
                            for t in range(nt):
                                mm = e.transpose(bank[:, t * P:(t + 1) * P], sm[:, t, s * P:(s + 1) * P],
                                                 ident[:, :])
                            mm.then_inc(done, 1)
                    if ev == "pv":
                        j = g * NO + i
                        if i == 0:
                            e.wait_ge(AT_ready, g + 1)
                        if j > 1:
                            e.wait_ge(av_ready, j - 1)
                        c = OFF[i]
                        e.matmul(BB[j % 2][:, c:T], spread[:, i % STRIP, :], AT[:, g, i // STRIP, c:T],
                                 start=True, stop=True).then_inc(b_ready, 1)
                        if i % 2 and i > 1:
                            add_up(g, i // 2 - 1)
                    if ev == "gated":
                        for pair in range(NO // 2 - 1, PAIRS):
                            add_up(g, pair)
                    if ev == "proj":
                        e.wait_ge(og_ready, g + 1)
                        bank, done = bank_of((ev, g, 0))
                        for t in range(nt):
                            mm = e.matmul(bank[:, t * P:(t + 1) * P], og[:, g, geo.start[t]:geo.start[t] + P],
                                          Wo[:, :], start=True, stop=True)
                        mm.then_inc(done, 1)

            @block.scalar
            def _(e):
                for ev, g, i in order:
                    if ev == "yT":
                        bank, free = filled(e, (ev, g, 0))
                        for t in range(nt):
                            o = geo.own[t]
                            a = e.activation(yT[:, g, geo.start[t] + o:geo.start[t] + P],
                                             bank[:, t * P + o:(t + 1) * P], ACT.Identity)
                        a.then_inc(yT_ready, 1)
                        e.wait_ge(yT_ready, g + 1)
                        e.sem_inc(free, 1)
                    if ev == "qkv":
                        for x in range(4):
                            bank, free = filled(e, (ev, g, x))
                            if x < 3:
                                to = (q[:, g, :], kpad[:, g, PAD:], vpad[:, g, PAD:])[x]
                                a = e.activation(to, bank[:, 0:T], ACT.Identity, bias=cols[:, x:x + 1])
                            else:
                                a = e.activation(gt[:, g, :], bank[:, 0:T], ACT.Tanh, scale=0.5,
                                                 bias=cols[:, 5:6])
                            a.then_inc(free, 1)
                        b, k = use[ev, g, 3]
                        e.wait_ge(gfree[b], k + 1)
                        e.sem_inc(qkv_ready, 1)
                    if ev == "strips":
                        e.wait_ge(prod_used, (g + 1) * NO)
                        if g:
                            b, k = use["soft", g - 1, nt - 1]
                            e.wait_ge(gready[b], k + 1)
                        for s in range(NS):
                            a = e.activation(SC[:, s, :], SB[s][:, 0:T], ACT.Identity, bias=eff[:, s:s + 1])
                        a.then_inc(SC_ready, 1)
                    if ev == "norm":
                        e.wait_ge(lg_ready, g + 1)
                        e.activation(sm[:, :, 0:KO], sm[:, :, 0:KO], ACT.Exp).then_inc(e_ready, 1)
                    if ev == "AT":
                        for s in range(NS):
                            bank, free = filled(e, (ev, g, s))
                            for t in range(nt):
                                o = geo.own[t]
                                a = e.activation(AT[:, g, s, geo.start[t] + o:geo.start[t] + P],
                                                 bank[:, t * P + o:(t + 1) * P], ACT.Identity)
                            a.then_inc(free, 1)
                        b, k = use[ev, g, NS - 1]
                        e.wait_ge(gfree[b], k + 1)
                        e.sem_inc(AT_ready, 1)

            @block.gpsimd
            def _(e):
                for g in range(G):
                    e.wait_ge(z_ready, g + 1)
                    e.tensor_tensor(out[:, g, :, :], xb(g), bo[:, :].unsqueeze(1).to_broadcast([P, nt, P]),
                                    ALU.add).then_inc(x_ready, 1)
                for g in range(G):
                    for pair in range(ADDED):
                        e.wait_ge(av_ready, g * NO + 2 * pair + 2)
                        c = OFF[2 * pair + 1]
                        av = AV[:, (g * PAIRS + pair) % 3, :, c:T]
                        e.tensor_tensor(av[:, 0, :], av[:, 0, :], av[:, 1, :], ALU.add).then_inc(pair_ready, 1)

            @block.vector
            def _(e):
                linked, _n = chain(e, own)
                sm4 = sm[:, :, 0:KO].rearrange("p t (o h) -> p t o h", h=HEADS)
                smh = sm[:, :, 0:KO].rearrange("p t (o h) -> p t h o", h=HEADS)
                for ev, g, i in order:
                    if ev == "ln" and g == 0:
                        for x in range(G):
                            for t in range(nt):
                                ins = e.bn_stats(st6[:, x, t, :], xb(x)[:, t, :])
                        linked(ins)
                        for x in range(G):
                            for t in range(nt):
                                ins = e.bn_aggr(mv[:, x, t, :], st6[:, x, t, :])
                        linked(ins)
                        linked(e.tensor_scalar(var[:, :], mv[:, :, :, 1].rearrange("p g t -> p (g t)"),
                                               EPS, None, ALU.add))
                        rsqrt(e, linked, var[:, :], rs[:, :], tmp[:, :])
                        for x in range(G):
                            for t in range(nt):
                                ins = e.tensor_scalar(Z[:, x, t, :], xb(x)[:, t, :], mv[:, x, t, 0:1],
                                                      rs[:, x * nt + t:x * nt + t + 1], ALU.subtract, ALU.mult)
                            ins.then_inc(z_ready, 1)
                    if ev == "sc":
                        j = g * NO + i
                        if i == 0:
                            e.wait_ge(qkv_ready, g + 1)
                        if j > 3:
                            e.wait_ge(prod_used, j - 3)
                        c = cut(i)
                        at = PAD - OFF[i]
                        e.tensor_tensor(PR[:, j % 4, c:T], q[:, g, c:T], kpad[:, g, at + c:at + T], ALU.mult)\
                            .then_inc(prod_ready, 1)
                    if ev == "soft":
                        if g > 0:
                            e.wait_ge(AT_ready, g)
                        for t in range(nt):
                            bank, free = filled(e, (ev, g, t))
                            e.tensor_tensor(sm4[:, t], bank[:, 0:KO].rearrange("p (o h) -> p o h", h=HEADS),
                                            mask[:, t, :].unsqueeze(2).to_broadcast([P, NO, HEADS]),
                                            ALU.add).then_inc(free, 1)
                        b, k = use[ev, g, nt - 1]
                        e.wait_ge(gfree[b], k + 1)
                        linked(e.tensor_reduce(big[:, :, :], smh, AX.X, ALU.max))
                        for t in range(nt):
                            ins = e.tensor_tensor(sm4[:, t], sm4[:, t],
                                                  big[:, t, :].unsqueeze(1).to_broadcast([P, NO, HEADS]),
                                                  ALU.subtract)
                        ins.then_inc(lg_ready, 1)
                    if ev == "norm":
                        e.wait_ge(e_ready, g + 1)
                        linked(e.tensor_reduce(tot[:, :, :], smh, AX.X, ALU.add))
                        linked(e.reciprocal(tot[:, :, :], tot[:, :, :]))
                        for t in range(nt):
                            ins = e.tensor_tensor(sm4[:, t], sm4[:, t],
                                                  tot[:, t, :].unsqueeze(1).to_broadcast([P, NO, HEADS]), ALU.mult)
                        ins.then_inc(A_ready, 1)
                    if ev == "pv":
                        j = g * NO + i
                        e.wait_ge(b_ready, j + 1)
                        pair = g * PAIRS + i // 2
                        if pair > 2:
                            e.wait_ge(av_used, pair - 2)
                        c = OFF[i]
                        at = PAD - c
                        e.tensor_tensor(AV[:, pair % 3, i % 2, c:T], BB[j % 2][:, c:T], vpad[:, g, at + c:at + T],
                                        ALU.mult).then_inc(av_ready, 1)
                    if ev == "gated":
                        linked(e.tensor_scalar(gt[:, g, :], gt[:, g, :], cols[:, 6:7], cols[:, 6:7],
                                               ALU.mult, ALU.add))
                        e.wait_ge(av_used, (g + 1) * PAIRS)
                        e.tensor_tensor(og[:, g, :], AB[:, 0:T], gt[:, g, :], ALU.mult)\
                            .then_inc(og_ready, 1)
                    if ev == "proj":
                        e.wait_ge(x_ready, g + 1)
                        bank, free = filled(e, (ev, g, 0))
                        e.tensor_tensor(out[:, g, :, :], bank[:, 0:nt * P].rearrange("p (t c) -> p t c", c=P),
                                        out[:, g, :, :], ALU.add).then_inc(out_ready, 1)
                        e.wait_ge(out_ready, g + 1)
                        e.sem_inc(free, 1)

            @block.sync
            def _(e):
                for g in range(G):
                    e.wait_ge(out_ready, g + 1)
                    to = dstb[bass.ds(r * G + g, 1)].rearrange("o t c -> (o t) c")
                    e.dma_start(to[0:(nt - 1) * P, :].rearrange("(t p) c -> p t c", p=P),
                                out[:, g, 0:nt - 1, :]).then_inc(stored, 16)
                    e.dma_start(to[(nt - 1) * P:T, :], out[geo.own[-1]:P, g, nt - 1, :]).then_inc(stored, 16)
                e.wait_ge(stored, 32 * G)

        with nc.Fori(0, rounds) as r:
            with nc.Block(no_gpsimd_drain=True) as block:
                one_round(block, r)
            nc.all_engine_barrier(sems_to_clear=clear)
        sems.finish()


def embed_phase(nc, H, hA, w, ident, group=4):
    GRID, PX, CH = 14, 16, 3
    geo = Geometry(GRID * GRID + 1)
    nt, T = geo.tiles, geo.tokens
    K = CH * PX
    S, SEM = 77, 512
    NC = SEM // P
    G, rounds = group, BATCH // group

    with ExitStack() as ctx:
        sems = Semaphores(nc, ctx)

        def sb(name, shape, dt=F32):
            return ctx.enter_context(nc.sbuf_tensor(f"emb_{name}", shape, dt))

        def signal(name):
            return sems.take(f"emb_{name}")

        CW = sb("CW", [K, PX, P])
        cols = sb("cols", [P, 2])
        pos = sb("pos", [P, nt, P])
        WT = sb("WT", [P, NC, P])
        idx = sb("idx", [S, BATCH], I32)
        low = sb("low", [S, BATCH], I32)
        idg = sb("idg", [S, G], I32)
        XI = sb("XI", [K, G, GRID, GRID * PX])
        ET = sb("ET", [P, G, T])
        TX = sb("TX", [S, G, SEM])
        TXT = sb("TXT", [P, G, NC, S])
        sums = sb("sums", [S, G])
        TO = sb("TO", [S, G, P])
        banks = [ctx.enter_context(nc.psum_tensor(f"emb_ps{i}", [P, 512], F32)) for i in range(8)]
        EB, TB, XB, YB = banks[0:2], banks[2:4], banks[4:6], banks[6:8]

        arrived = [signal(f"arrived{g}") for g in range(G)]
        gathered = [signal(f"gathered{g}") for g in range(G)]
        emb_filled = signal("emb_filled")
        ET_ready = signal("ET_ready")
        tb_filled = signal("tb_filled")
        h_ready = signal("h_ready")
        id_ready = signal("id_ready")
        sum_ready = signal("sum_ready")
        xb_filled = signal("xb_filled")
        TXT_ready = signal("TXT_ready")
        yb_filled = signal("yb_filled")
        TO_ready = signal("TO_ready")
        own = signal("own")
        stored = sems.take("emb_stored")
        clear = range(arrived[0].num, stored.num + 1)
        loaded = sems.take("emb_loaded")
        set_up = sems.take("emb_set_up")

        rowsA = hA.rearrange("(b t) c -> b t c", b=BATCH)
        loads = [(CW[:, :, :], w["conv"].rearrange("(k x) d -> k x d", x=PX)), (cols[:, :], w["cols"]),
                 (WT[:, :, :], w["W"].rearrange("(k p) d -> p k d", p=P)), (idx[:, :], w["idx"])]
        loads += [(pos[:, t, :], w["pos"][geo.start[t]:geo.start[t] + P, :]) for t in range(nt)]
        with nc.Block() as block:
            @block.sync
            def _(e):
                for to, fr in loads:
                    e.dma_start(to, fr).then_inc(loaded, 16)
                e.wait_ge(loaded, 16 * len(loads))

            @block.vector
            def _(e):
                e.wait_ge(loaded, 16 * len(loads))
                e.tensor_scalar(low[:, :], idx[:, :], 0.0, float(w["vocab"]), ALU.is_lt, ALU.mult)\
                    .then_inc(set_up, 1)
                e.wait_ge(set_up, 1)
                e.tensor_tensor(idx[:, :], idx[:, :], low[:, :], ALU.add).then_inc(set_up, 1)
                e.wait_ge(set_up, 2)
                e.tensor_scalar(idx[:, :], idx[:, :], 0.0, float(w["vocab"] - 1), ALU.max, ALU.min)

        def one_round(block, r):
            order = []
            for i in range(G + 2):
                if i < G:
                    order.append(("emb", i))
                    order.append(("txt", i))
                if 1 <= i <= G:
                    order.append(("turn", i - 1))
                    order.append(("prod", i - 1))

            @block.sync
            def _(e):
                for g in range(G):
                    for c in range(CH):
                        src = w["x"][bass.ds(r * G + g, 1), c].rearrange("o (a p) x -> p (o a) x", p=PX)
                        e.dma_start(XI[c * PX:(c + 1) * PX, g, :, :], src).then_inc(arrived[g], 16)
                for g in range(G):
                    e.wait_ge(TO_ready, g + 1)
                    e.dma_start(rowsA[bass.ds(r * G + g, 1), T:T + S, :].rearrange("o t c -> (o t) c"),
                                TO[:, g, :]).then_inc(stored, 16)
                e.wait_ge(stored, 16 * G)

            @block.gpsimd
            def _(e):
                e.wait_ge(id_ready, 1)
                for g in range(G):
                    e.indirect_dma_start(TX[:, g, :], None, w["table"],
                                         bass.IndirectOffsetOnAxis(ap=idg[:, g:g + 1], axis=0))\
                        .then_inc(gathered[g], 16)
                for g in range(G):
                    e.wait_ge(gathered[g], 16)
                e.dma_reset(range(gathered[0].num, gathered[-1].num + 1))

            @block.tensor
            def _(e):
                for ev, g in order:
                    if ev == "emb":
                        e.wait_ge(arrived[g], 16 * CH)
                        if g > 1:
                            e.wait_ge(ET_ready, g - 1)
                        for x in range(PX):
                            mm = e.matmul(EB[g % 2][:, 0:T - 1], CW[:, x, :],
                                          XI[:, g, :, :].rearrange("k a (b x) -> k a b x", x=PX)[:, :, :, x],
                                          start=(x == 0), stop=(x == PX - 1))
                        mm.then_inc(emb_filled, 1)
                    if ev == "txt":
                        e.wait_ge(gathered[g], 16)
                        if g > 1:
                            e.wait_ge(TXT_ready, g - 1)
                        for c in range(NC):
                            mm = e.transpose(XB[g % 2][:, c * S:(c + 1) * S], TX[:, g, c * P:(c + 1) * P],
                                             ident[0:S, 0:S])
                        mm.then_inc(xb_filled, 1)
                    if ev == "turn":
                        e.wait_ge(ET_ready, g + 1)
                        if g > 1:
                            e.wait_ge(h_ready, g - 1)
                        for t in range(nt):
                            mm = e.transpose(TB[g % 2][:, t * P:(t + 1) * P],
                                             ET[:, g, geo.start[t]:geo.start[t] + P], ident[:, :])
                        mm.then_inc(tb_filled, 1)
                    if ev == "prod":
                        e.wait_ge(TXT_ready, g + 1)
                        if g > 1:
                            e.wait_ge(TO_ready, g - 1)
                        for c in range(NC):
                            mm = e.matmul(YB[g % 2][0:S, 0:P], TXT[:, g, c, :], WT[:, c, :],
                                          start=(c == 0), stop=(c == NC - 1))
                        mm.then_inc(yb_filled, 1)

            @block.scalar
            def _(e):
                for ev, g in order:
                    if ev == "emb":
                        e.wait_ge(emb_filled, g + 1)
                        e.activation(ET[:, g, 0:1], cols[:, 1:2], ACT.Identity)
                        e.activation(ET[:, g, 1:T], EB[g % 2][:, 0:T - 1], ACT.Identity, bias=cols[:, 0:1])\
                            .then_inc(ET_ready, 1)
                    if ev == "txt":
                        e.wait_ge(xb_filled, g + 1)
                        e.activation(TXT[:, g, :, :].rearrange("p c s -> p (c s)"), XB[g % 2][:, 0:NC * S],
                                     ACT.Identity).then_inc(TXT_ready, 1)
                    if ev == "prod":
                        e.wait_ge(yb_filled, g + 1)
                        e.wait_ge(sum_ready, g + 1)
                        e.activation(TO[:, g, :], YB[g % 2][0:S, 0:P], ACT.Identity, scale=sums[:, g:g + 1])\
                            .then_inc(TO_ready, 1)

            @block.vector
            def _(e):
                linked, _n = chain(e, own)
                e.tensor_copy(idg[:, :], idx[:, bass.ds(r * G, G)]).then_inc(id_ready, 1)
                for ev, g in order:
                    if ev == "txt":
                        e.wait_ge(gathered[g], 16)
                        linked(e.tensor_reduce(sums[:, g:g + 1], TX[:, g, :], AX.X, ALU.add))
                        linked(e.tensor_scalar(sums[:, g:g + 1], sums[:, g:g + 1], 1e-6, P ** -0.5,
                                               ALU.add, ALU.mult))
                        e.reciprocal(sums[:, g:g + 1], sums[:, g:g + 1]).then_inc(sum_ready, 1)
                    if ev == "turn":
                        e.wait_ge(tb_filled, g + 1)
                        h = H[:, bass.ds(r * G + g, 1), :, :].rearrange("p o t c -> p (o t) c")
                        e.tensor_tensor(h, TB[g % 2][:, 0:nt * P].rearrange("p (t c) -> p t c", c=P),
                                        pos[:, :, :], ALU.add).then_inc(h_ready, 1)

        with nc.Fori(0, rounds) as r:
            with nc.Block() as block:
                one_round(block, r)
            nc.all_engine_barrier(sems_to_clear=clear)
        sems.finish()


def final_norm_phase(nc, H, hA, wb, group=4):
    geo = Geometry(197)
    nt, T, G, rounds = geo.tiles, geo.tokens, group, BATCH // group
    with ExitStack() as ctx:
        sems = Semaphores(nc, ctx)

        def sb(name, shape):
            return ctx.enter_context(nc.sbuf_tensor(f"fin_{name}", shape, F32))

        W = sb("W", [P, 2, P])
        N = sb("N", [P, G, nt, P])
        st6 = sb("st6", [P, G, nt, 6])
        mv = sb("mv", [P, G, nt, 2])
        var, rs, tmp = (sb(x, [P, G * nt]) for x in ("var", "rs", "tmp"))
        n_ready = sems.take("fin_n_ready")
        out_ready = sems.take("fin_out_ready")
        own = sems.take("fin_own")
        stored = sems.take("fin_stored")
        loaded = sems.take("fin_loaded")
        rowsA = hA.rearrange("(b t) c -> b t c", b=BATCH)
        with nc.Block() as block:
            @block.sync
            def _(e):
                e.dma_start(W[:, :, :], wb.rearrange("(o a) b -> o (a b)", o=1).to_broadcast([P, 2 * P]))\
                    .then_inc(loaded, 16)
                e.wait_ge(loaded, 16)
        with nc.Fori(0, rounds) as r:
            with nc.Block(no_gpsimd_drain=True) as block:
                @block.vector
                def _(e):
                    linked, _n = chain(e, own)

                    def h(g):
                        return H[:, bass.ds(r * G + g, 1), :, :].rearrange("p o t c -> p (o t) c")

                    for g in range(G):
                        for t in range(nt):
                            ins = e.bn_stats(st6[:, g, t, :], h(g)[:, t, :])
                    linked(ins)
                    for g in range(G):
                        for t in range(nt):
                            ins = e.bn_aggr(mv[:, g, t, :], st6[:, g, t, :])
                    linked(ins)
                    linked(e.tensor_scalar(var[:, :], mv[:, :, :, 1].rearrange("p g t -> p (g t)"), EPS, None,
                                           ALU.add))
                    rsqrt(e, linked, var[:, :], rs[:, :], tmp[:, :])
                    for g in range(G):
                        for t in range(nt):
                            ins = e.tensor_scalar(N[:, g, t, :], h(g)[:, t, :], mv[:, g, t, 0:1],
                                                  rs[:, g * nt + t:g * nt + t + 1], ALU.subtract, ALU.mult)
                        linked(ins)
                        e.tensor_tensor(N[:, g, :, :], N[:, g, :, :],
                                        W[:, 0:1, :].to_broadcast([P, nt, P]), ALU.mult).then_inc(n_ready, 1)

                @block.gpsimd
                def _(e):
                    for g in range(G):
                        e.wait_ge(n_ready, g + 1)
                        e.tensor_tensor(N[:, g, :, :], N[:, g, :, :], W[:, 1:2, :].to_broadcast([P, nt, P]),
                                        ALU.add).then_inc(out_ready, 1)

                @block.sync
                def _(e):
                    for g in range(G):
                        e.wait_ge(out_ready, g + 1)
                        to = rowsA[bass.ds(r * G + g, 1)].rearrange("o t c -> (o t) c")
                        e.dma_start(to[0:P, :], N[:, g, 0, :]).then_inc(stored, 16)
                        e.dma_start(to[P:T, :], N[geo.own[1]:P, g, 1, :]).then_inc(stored, 16)
                    e.wait_ge(stored, 32 * G)
            nc.all_engine_barrier(sems_to_clear=range(n_ready.num, stored.num + 1))
        sems.finish()


def move_phase(nc, tag, H, geo, rows, store):
    with ExitStack() as ctx:
        sems = Semaphores(nc, ctx)
        moved = sems.take(f"{tag}_moved")
        r = rows.rearrange("(b t) c -> b t c", b=BATCH)
        with nc.Block() as block:
            @block.sync
            def _(e):
                for t in range(geo.tiles):
                    s, o = geo.start[t], geo.own[t] if store else 0
                    out = r[:, s + o:s + P, :].rearrange("b p c -> p b c")
                    sb = H[o:P, :, t, :]
                    e.dma_start(*((out, sb) if store else (sb, out))).then_inc(moved, 16)
                e.wait_ge(moved, 16 * geo.tiles)
        sems.finish()


IMAGE, TEXT = 197, 77
TOKENS = IMAGE + TEXT


def build(nc, d, out):
    hA, hB, hC, hD = (nc.dram_tensor(f"h{x}", (BATCH * TOKENS, P), F32).ap() for x in "ABCD")
    flat = out.rearrange("b t c -> (b t) c")
    with ExitStack() as ctx:
        ident = ctx.enter_context(nc.sbuf_tensor("ident", [P, P], F32))
        identb = ctx.enter_context(nc.sbuf_tensor("identb", [P, P], BF16))
        ident_in = ctx.enter_context(nc.semaphore("ident_in"))
        with nc.Block() as block:
            @block.sync
            def _(e):
                e.dma_start(ident[:, :], d["ident"]).then_inc(ident_in, 16)

            @block.vector
            def _(e):
                e.wait_ge(ident_in, 16)
                e.tensor_copy(identb[:, :], ident[:, :])

        with nc.sbuf_tensor("H", [P, BATCH, 2, P], F32) as H:
            embed_phase(nc, H, hA, dict(conv=d["conv_w"], cols=d["emb_cols"], pos=d["pos"], W=d["txt_W"],
                                        idx=d["idx"], table=d["table"], vocab=d["table"].shape[0],
                                        x=d["x"]), ident)
            attention_phase(nc, "vit", H, IMAGE, 4, 4,
                            dict(qkv=d["vit_qkv"], proj=d["vit_proj"], cols=d["vit_cols"], rows=d["vit_rows"],
                                 bvm=d["vit_bvm"], fc1=d["vit_fc1"], fc2=d["vit_fc2"]), ident, identb, d["mask_image"])
            final_norm_phase(nc, H, hA, d["norm_wb"])
        with nc.sbuf_tensor("H3", [P, BATCH, 3, P], F32) as H:
            move_phase(nc, "in0", H, Geometry(TOKENS), hA, False)
            attention_phase(nc, "att", H, TOKENS, 2, 1,
                            dict(qkv=d["att_qkv"], proj=d["att_proj"], cols=d["att_cols"], rows=d["att_rows"],
                                 bvm=d["att_bvm"]),
                            ident, identb, d["mask_all"])
            move_phase(nc, "out0", H, Geometry(TOKENS), hB, True)
        ffn_phase(nc, "moe0", hB, hC, dict(experts=16, chunks=4, act=ACT.Silu, inner=True, shared=2,
                                           shared_scale=0.25, ff_chunks=4, temperature=0.7),
                  {k[5:]: v for k, v in d.items() if k.startswith("moe0_")}, ident)
        dilated_phase(nc, "dil", hC, hD, {**{k[4:]: v for k, v in d.items() if k.startswith("dil_")},
                                          "tokens": TOKENS}, ident)
        ffn_phase(nc, "moe1", hD, flat, dict(experts=8, chunks=2, act=ACT.Gelu_apprx_tanh, inner=False,
                                             temperature=1.0),
                  {k[5:]: v for k, v in d.items() if k.startswith("moe1_")}, ident)


def kernel(**inputs):
    import numpy as np
    import concourse.bacc as bacc
    from concourse.bass_utils import run_bass_kernel_spmd

    a = {k: np.asarray(v) for k, v in inputs.items()}
    t0, t1, m0, m1 = "L0_tok_", "L1_attn_", "L0_ffn_", "L1_ffn_"
    zero, one = np.zeros(P, np.float32), np.ones(P, np.float32)

    def columns(v):
        return v.reshape(-1, P).T

    def keys_mask(tokens):
        geo = Geometry(tokens)
        m = np.ones((P, geo.tiles), np.float32)
        m[:geo.own[-1], -1] = 0.0
        return m

    def value_bias(bias, tokens):
        geo = Geometry(tokens)
        rows = np.zeros((P, geo.tiles, P), np.float32)
        rows[:, :-1] = bias
        rows[geo.own[-1]:, -1] = bias
        return rows

    OFF = offsets_of(TOKENS)
    NO, STRIP = len(OFF), P // HEADS
    NS = -(-NO // STRIP)
    geo = Geometry(TOKENS)
    log_max = math.log(1.0 + 4096.0)
    omega = [x * math.pi / log_max for x in (0, 0, 1, 1, 4, 4, 6, 6)]
    cosine = np.array([[math.cos(om * math.log(1.0 + o)) if om > 0 else 0.0 for om in omega] for o in OFF],
                      np.float32)
    pb = np.zeros((3, NS * STRIP, HEADS), np.float32)
    pb[0, :NO] = a[t1 + "pos_bias"][:NO]
    pb[1, :NO] = cosine
    pb[2, :NO] = np.broadcast_to(a[t1 + "disp_amp"], (NO, HEADS))
    token = np.array([[geo.start[t] + p for t in range(geo.tiles)] for p in range(P)])
    far = np.where(token[:, :, None] >= np.array(OFF), 0.0, -1e30).astype(np.float32)
    spread = np.zeros((P, STRIP, P), np.float32)
    for i in range(STRIP):
        for h in range(HEADS):
            spread[i * HEADS + h, i, h * HD:(h + 1) * HD] = 1.0

    layers = range(4)
    d = {
        "ident": np.eye(P, dtype=np.float32),
        "x": a["x"], "idx": a["x_txt"].T, "table": a["L0_txt_word2sememe"], "txt_W": a["L0_txt_W"],
        "conv_w": a[t0 + "conv_w"], "emb_cols": np.stack([a[t0 + "conv_b"], a[t0 + "cls_token"][0, 0]], -1),
        "pos": a[t0 + "pos_embed"][0],
        "vit_qkv": a[t0 + "qkv_w"], "vit_proj": a[t0 + "proj_w"], "vit_fc1": a[t0 + "fc1_w"],
        "vit_fc2": a[t0 + "fc2_w"],
        "vit_cols": np.stack([np.stack([a[t0 + "qkv_b"][l, :P], a[t0 + "qkv_b"][l, P:2 * P], a[t0 + "ln1_w"][l],
                                        a[t0 + "ln1_b"][l], a[t0 + "ln2_w"][l], a[t0 + "ln2_b"][l],
                                        a[t0 + "fc1_b"][l, :P], a[t0 + "fc1_b"][l, P:]], -1) for l in layers]),
        "vit_rows": np.stack([np.stack([a[t0 + "proj_b"][l], a[t0 + "fc2_b"][l]]) for l in layers]),
        "vit_bvm": np.stack([value_bias(a[t0 + "qkv_b"][l, 2 * P:], IMAGE) for l in layers]),
        "mask_image": keys_mask(IMAGE), "mask_all": keys_mask(TOKENS),
        "norm_wb": np.stack([a[t0 + "norm_w"], a[t0 + "norm_b"]]),
        "att_qkv": a["L0_attn_w_qkv"].T[None], "att_proj": a["L0_attn_w_agg"].T[None],
        "att_cols": np.stack([zero, zero, one, zero, one, zero, zero, zero], -1)[None],
        "att_rows": np.stack([a["L0_attn_b_agg"], zero])[None],
        "att_bvm": value_bias(zero, TOKENS)[None],
        "moe0_w1": np.concatenate([*a[m0 + "ew1"], a[m0 + "sw1"]], 1),
        "moe0_w2": np.concatenate([*a[m0 + "ew2"], a[m0 + "sw2"]], 0),
        "moe0_b1": columns(np.concatenate([a[m0 + "eb1"].reshape(-1), a[m0 + "sb1"]])),
        "moe0_b2": np.concatenate([a[m0 + "eb2"], a[m0 + "sb2"][None]]),
        "moe0_router": a[m0 + "router_w"], "moe0_router_b": a[m0 + "router_b"][None],
        "moe0_number": np.arange(16, dtype=np.float32)[None],
        "moe0_cols": np.stack([a[m0 + "ln_in_g"], a[m0 + "ln_in_b"], a[m0 + "ff_ln_g"], a[m0 + "ff_ln_b"]], -1),
        "moe0_f1": a[m0 + "ff_w1"], "moe0_f2": a[m0 + "ff_w2"], "moe0_fb1": columns(a[m0 + "ff_b1"]),
        "moe0_fb2": a[m0 + "ff_b2"][None],
        "dil_qkv": a[t1 + "W_qkv"], "dil_gate": a[t1 + "W_gate"], "dil_out": a[t1 + "W_out"],
        "dil_cols": np.stack([*a[t1 + "b_qkv"].reshape(3, P), a[t1 + "b_gate"], np.repeat(a[t1 + "if_gain"], HD)], -1),
        "dil_b_out": a[t1 + "b_out"][None],
        "dil_scale_embed": np.tile(a[t1 + "scale_embed"][:NO].T, (HEADS, 1)),
        "dil_heads": np.repeat(np.eye(HEADS, dtype=np.float32), HD, axis=0), "dil_spread": spread,
        "dil_pb": pb.reshape(3, NS, P).transpose(2, 1, 0), "dil_mask": far,
        "moe1_w1": np.concatenate([*a[m1 + "W1"]], 1), "moe1_w2": np.concatenate([*a[m1 + "W2"]], 0),
        "moe1_b1": columns(a[m1 + "b1"].reshape(-1)), "moe1_b2": a[m1 + "b2"],
        "moe1_router": a[m1 + "Wg"], "moe1_router_b": np.zeros((1, 8), np.float32),
        "moe1_number": np.arange(8, dtype=np.float32)[None],
        "moe1_cols": np.stack([one, zero, one, zero], -1),
    }
    nc = bacc.Bacc("TRN2", target_bir_lowering=False, num_devices=1)
    arrays, aps = {}, {}
    for name, v in d.items():
        v = np.ascontiguousarray(v)
        arrays[f"in_{name}"] = v
        aps[name] = nc.dram_tensor(f"in_{name}", v.shape, mybir.dt.from_np(v.dtype), kind="ExternalInput").ap()
    out = nc.dram_tensor("out_dram", (BATCH, TOKENS, P), F32, kind="ExternalOutput").ap()
    build(nc, aps, out)
    r = run_bass_kernel_spmd(nc, [arrays], core_ids=[0])
    return r.results[0]["out_dram"]
```
